# Optimizing a Trainium2 kernel written in Bass

```python
import numpy as np
import jax
import jax.numpy as jnp

def _softmax(x, axis=-1):
    return jax.nn.softmax(x, axis=axis)
def _gelu(x):
    return jax.nn.gelu(x, approximate=True)
def _silu(x):
    return jax.nn.silu(x)
def _sigmoid(x):
    return jax.nn.sigmoid(x)
def _layernorm(x, axis=-1, eps=1e-5):
    m = jnp.mean(x, axis=axis, keepdims=True)
    v = jnp.var(x, axis=axis, keepdims=True)
    return (x - m) / jnp.sqrt(v + eps)
def _scatter_add(tgt, idx, src, axis=0):
    return tgt.at[idx].add(src)
def _segment_sum(src, seg, n):
    return jax.ops.segment_sum(src, seg, n)

kernel_name = 'mk_conv_attn_hybrid_d4_conv_nhwc128_ffa068'

def setup_inputs(seed: int = 0):
    np.random.seed(seed)
    _w = jnp.asarray
    def _rec_inputs():
        import jax
        import jax.numpy as jnp
        _gk = jax.random.key(seed)
        x = -0.0009896 + 1 * jax.random.normal(jax.random.fold_in(_gk, 1), (4, 56, 56, 128), jnp.float32)
        return x
    x = _rec_inputs()
    def _L0_conv_setup():
        import jax, jax.numpy as jnp
        import numpy as np
        DIM = 128
        NUM_HEADS = 4
        HEAD_DIM = DIM // NUM_HEADS
        KSIZE = 7
        DILATION = 1
        SCALE = HEAD_DIM ** (-0.5)

        def _rpb_bias(rpb):
            coords = np.stack(np.meshgrid(np.arange(KSIZE), np.arange(KSIZE), indexing='ij'))
            coords = coords.reshape(2, -1).T
            rel = coords - KSIZE // 2 + (KSIZE - 1)
            return rpb[:, rel[:, 0], rel[:, 1]]
        key = jax.random.key(seed)
        ks = jax.random.split(key, 6)
        B, H, W = (4, 56, 56)
        x = jax.random.normal(ks[0], (B, H, W, DIM), dtype=jnp.float32)
        qkv_w = jax.random.normal(ks[1], (3 * DIM, DIM), dtype=jnp.float32) * 0.02
        qkv_b = jnp.zeros((3 * DIM,), dtype=jnp.float32)
        rpb = jax.random.normal(ks[2], (NUM_HEADS, 2 * KSIZE - 1, 2 * KSIZE - 1), dtype=jnp.float32) * 0.02
        proj_w = jax.random.normal(ks[3], (DIM, DIM), dtype=jnp.float32) * 0.02
        proj_b = jnp.zeros((DIM,), dtype=jnp.float32)
        return {'x': x, 'qkv_w': qkv_w, 'qkv_b': qkv_b, 'rpb': rpb, 'proj_w': proj_w, 'proj_b': proj_b}
    _L0_conv_all = _L0_conv_setup()
    _L0_conv_in = {k: v for k, v in _L0_conv_all.items() if k in ('qkv_w', 'qkv_b', 'rpb', 'proj_w', 'proj_b', )}
    del _L0_conv_all

    def _L1_conv_setup():
        import jax, jax.numpy as jnp
        import numpy as np
        B, H, W, C, K = (4, 64, 64, 128, 8)
        CK = C // K
        key = jax.random.key(seed)
        k1, k2, k3, k4, k5 = jax.random.split(key, 5)
        x = jax.random.normal(k1, (B, H, W, C), dtype=jnp.float32)
        kernel_f = jax.random.normal(k2, (1, 1, C, CK), dtype=jnp.float32) * (1.0 / np.sqrt(C))
        kernel_g = jax.random.normal(k3, (1, 1, C, CK), dtype=jnp.float32) * (1.0 / np.sqrt(C))
        kernel_h = jax.random.normal(k4, (1, 1, C, C), dtype=jnp.float32) * (1.0 / np.sqrt(C))
        gamma = jax.random.uniform(k5, (1,), dtype=jnp.float32)
        return {'x': x, 'kernel_f': kernel_f, 'kernel_g': kernel_g, 'kernel_h': kernel_h, 'gamma': gamma}
    _L1_conv_all = _L1_conv_setup()
    _L1_conv_in = {k: v for k, v in _L1_conv_all.items() if k in ('kernel_f', 'kernel_g', 'kernel_h', 'gamma', )}
    del _L1_conv_all

    def _L2_attn_setup():
        import jax, jax.numpy as jnp
        import numpy as np
        from jax import lax
        TAU_MEM = 10.0
        THRESHOLD = 1.0
        WINDOW = 128
        STRIDE = 64
        NUM_GLOBAL = 4

        def _spike_indicators(x, Ws, bs):
            B, S, D = x.shape
            decay = jnp.exp(jnp.float32(-1.0 / TAU_MEM))
            cur = x @ Ws + bs
            cur_t = jnp.swapaxes(cur, 0, 1)

            def step(mem, c):
                mem = decay * mem + c
                spk = mem >= THRESHOLD
                mem = jnp.where(spk, 0.0, mem)
                return (mem, spk.astype(jnp.float32))
            _, spikes = lax.scan(step, jnp.zeros((B, 1), jnp.float32), cur_t)
            spike_ind = spikes.mean(axis=1)[:, 0]
            return spike_ind != 0.0

        def _sparse_mask(S, spike_bool):
            i = jnp.arange(S)[:, None]
            j = jnp.arange(S)[None, :]
            local = (j <= i) & (j >= i - WINDOW)
            glob = j % STRIDE == 0
            first = j < NUM_GLOBAL
            return (local | glob | first) & spike_bool[None, :]
        key = jax.random.key(seed)
        ks = jax.random.split(key, 8)
        B, S, D = (2, 8192, 128)
        s = 1.0 / np.sqrt(D)
        x = jax.random.normal(ks[0], (B, S, D), jnp.float32)
        Wq = jax.random.normal(ks[1], (D, D), jnp.float32) * s
        Wk = jax.random.normal(ks[2], (D, D), jnp.float32) * s
        Wv = jax.random.normal(ks[3], (D, D), jnp.float32) * s
        Wo = jax.random.normal(ks[4], (D, D), jnp.float32) * s
        Ws = jax.random.normal(ks[5], (D, 1), jnp.float32) * s
        return {'x': x, 'Wq': Wq, 'bq': jnp.zeros((D,), jnp.float32), 'Wk': Wk, 'bk': jnp.zeros((D,), jnp.float32), 'Wv': Wv, 'bv': jnp.zeros((D,), jnp.float32), 'Wo': Wo, 'bo': jnp.zeros((D,), jnp.float32), 'Ws': Ws, 'bs': jnp.zeros((1,), jnp.float32)}
    _L2_attn_all = _L2_attn_setup()
    _L2_attn_in = {k: v for k, v in _L2_attn_all.items() if k in ('Wq', 'bq', 'Wk', 'bk', 'Wv', 'bv', 'Wo', 'bo', 'Ws', 'bs', )}
    del _L2_attn_all

    def _L2_ffn_setup():
        import jax, jax.numpy as jnp
        import numpy as np
        B, S, D, E, H, O, K = (512, 2048, 128, 64, 512, 128, 8)
        key = jax.random.key(seed)
        k0, k1, k2, k3 = jax.random.split(key, 4)
        x = jax.random.normal(k0, (B, S, D), dtype=jnp.float32)
        gate_w = jax.random.normal(k1, (E, D), dtype=jnp.float32) * (1.0 / np.sqrt(D))
        gate_b = jnp.zeros((E,), dtype=jnp.float32)
        weight1 = jax.random.uniform(k2, (E, D + 1, H), dtype=jnp.float32, minval=-1.0, maxval=1.0) * (1.0 / np.sqrt(D + 1))
        weight2 = jax.random.uniform(k3, (E, H + 1, O), dtype=jnp.float32, minval=-1.0, maxval=1.0) * (1.0 / np.sqrt(H + 1))
        return {'x': x, 'gate_w': gate_w, 'gate_b': gate_b, 'weight1': weight1, 'weight2': weight2}
    _L2_ffn_all = _L2_ffn_setup()
    _L2_ffn_in = {k: v for k, v in _L2_ffn_all.items() if k in ('gate_w', 'gate_b', 'weight1', 'weight2', )}
    del _L2_ffn_all

    def _L3_attn_setup():
        import jax, jax.numpy as jnp
        import numpy as np
        key = jax.random.key(seed)
        x = jax.random.normal(key, (4, 4096, 128), dtype=jnp.float32)
        return {'x': x}
    _L3_attn_all = _L3_attn_setup()
    _L3_attn_in = {k: v for k, v in _L3_attn_all.items() if k in ()}
    del _L3_attn_all

    def _L3_ffn_setup():
        import jax, jax.numpy as jnp
        import numpy as np
        BN_EPS = 1e-05
        key = jax.random.key(seed)
        k1, k2, k3 = jax.random.split(key, 3)
        B, T, I, H = (64, 2048, 128, 128)
        x = jax.random.normal(k1, (B, T, I), dtype=jnp.float32)
        W = jax.random.normal(k2, (H, I), dtype=jnp.float32) * (1.0 / np.sqrt(I))
        V = jnp.linalg.qr(jax.random.normal(k3, (H, H), dtype=jnp.float32))[0]
        gamma = jnp.ones((H,), dtype=jnp.float32)
        beta = jnp.zeros((H,), dtype=jnp.float32)
        return {'x': x, 'W': W, 'V': V, 'gamma': gamma, 'beta': beta}
    _L3_ffn_all = _L3_ffn_setup()
    _L3_ffn_in = {k: v for k, v in _L3_ffn_all.items() if k in ('W', 'V', 'gamma', 'beta', )}
    del _L3_ffn_all

    return {
        "x": x,
        "L0_conv_qkv_w": _L0_conv_in["qkv_w"],
        "L0_conv_qkv_b": _L0_conv_in["qkv_b"],
        "L0_conv_rpb": _L0_conv_in["rpb"],
        "L0_conv_proj_w": _L0_conv_in["proj_w"],
        "L0_conv_proj_b": _L0_conv_in["proj_b"],
        "L1_conv_kernel_f": _L1_conv_in["kernel_f"],
        "L1_conv_kernel_g": _L1_conv_in["kernel_g"],
        "L1_conv_kernel_h": _L1_conv_in["kernel_h"],
        "L1_conv_gamma": _L1_conv_in["gamma"],
        "L2_attn_Wq": _L2_attn_in["Wq"],
        "L2_attn_bq": _L2_attn_in["bq"],
        "L2_attn_Wk": _L2_attn_in["Wk"],
        "L2_attn_bk": _L2_attn_in["bk"],
        "L2_attn_Wv": _L2_attn_in["Wv"],
        "L2_attn_bv": _L2_attn_in["bv"],
        "L2_attn_Wo": _L2_attn_in["Wo"],
        "L2_attn_bo": _L2_attn_in["bo"],
        "L2_attn_Ws": _L2_attn_in["Ws"],
        "L2_attn_bs": _L2_attn_in["bs"],
        "L2_ffn_gate_w": _L2_ffn_in["gate_w"],
        "L2_ffn_gate_b": _L2_ffn_in["gate_b"],
        "L2_ffn_weight1": _L2_ffn_in["weight1"],
        "L2_ffn_weight2": _L2_ffn_in["weight2"],
        "L3_ffn_W": _L3_ffn_in["W"],
        "L3_ffn_V": _L3_ffn_in["V"],
        "L3_ffn_gamma": _L3_ffn_in["gamma"],
        "L3_ffn_beta": _L3_ffn_in["beta"],
    }

def reference(x, L0_conv_qkv_w, L0_conv_qkv_b, L0_conv_rpb, L0_conv_proj_w, L0_conv_proj_b, L1_conv_kernel_f, L1_conv_kernel_g, L1_conv_kernel_h, L1_conv_gamma, L2_attn_Wq, L2_attn_bq, L2_attn_Wk, L2_attn_bk, L2_attn_Wv, L2_attn_bv, L2_attn_Wo, L2_attn_bo, L2_attn_Ws, L2_attn_bs, L2_ffn_gate_w, L2_ffn_gate_b, L2_ffn_weight1, L2_ffn_weight2, L3_ffn_W, L3_ffn_V, L3_ffn_gamma, L3_ffn_beta):
    import jax
    import jax.numpy as jnp
    def _L0_conv_ref(x, qkv_w, qkv_b, rpb, proj_w, proj_b):
        import jax, jax.numpy as jnp
        import numpy as np
        DIM = 128
        NUM_HEADS = 4
        HEAD_DIM = DIM // NUM_HEADS
        KSIZE = 7
        DILATION = 1
        SCALE = HEAD_DIM ** (-0.5)

        def _rpb_bias(rpb):
            coords = np.stack(np.meshgrid(np.arange(KSIZE), np.arange(KSIZE), indexing='ij'))
            coords = coords.reshape(2, -1).T
            rel = coords - KSIZE // 2 + (KSIZE - 1)
            return rpb[:, rel[:, 0], rel[:, 1]]
        B, H, W, C = x.shape
        qkv = x @ qkv_w.T + qkv_b
        qkv = qkv.reshape(B, H, W, 3, NUM_HEADS, HEAD_DIM).transpose(3, 0, 4, 1, 2, 5)
        q, k, v = (qkv[0], qkv[1], qkv[2])
        pad = KSIZE // 2 * DILATION
        kp = jnp.pad(k, ((0, 0), (0, 0), (pad, pad), (pad, pad), (0, 0)))
        vp = jnp.pad(v, ((0, 0), (0, 0), (pad, pad), (pad, pad), (0, 0)))
        off = jnp.arange(0, KSIZE * DILATION, DILATION)
        idx_i = jnp.arange(H)[:, None] + off[None, :]
        idx_j = jnp.arange(W)[:, None] + off[None, :]
        Ai = idx_i[:, None, :, None]
        Aj = idx_j[None, :, None, :]
        k_win = kp[:, :, Ai, Aj, :].reshape(B, NUM_HEADS, H, W, KSIZE * KSIZE, HEAD_DIM)
        v_win = vp[:, :, Ai, Aj, :].reshape(B, NUM_HEADS, H, W, KSIZE * KSIZE, HEAD_DIM)
        bias = _rpb_bias(rpb)
        attn = jnp.einsum('bnhwd,bnhwkd->bnhwk', q, k_win) * SCALE
        attn = attn + bias[None, :, None, None, :]
        attn = jax.nn.softmax(attn, axis=-1)
        out = jnp.einsum('bnhwk,bnhwkd->bnhwd', attn, v_win)
        out = out.transpose(0, 2, 3, 1, 4).reshape(B, H, W, C)
        return out @ proj_w.T + proj_b

    def _L1_conv_ref(x, kernel_f, kernel_g, kernel_h, gamma):
        import jax, jax.numpy as jnp
        import numpy as np
        B, H, W, C, K = (4, 64, 64, 128, 8)
        CK = C // K
        b, h, w, c = x.shape
        n = h * w
        xf = x.reshape(b, n, c)
        f = jnp.einsum('bnc,cd->bnd', xf, kernel_f[0, 0])
        g = jnp.einsum('bnc,cd->bnd', xf, kernel_g[0, 0])
        hh = jnp.einsum('bnc,cd->bnd', xf, kernel_h[0, 0])
        s = jnp.einsum('bnd,bmd->bnm', g, f)
        beta = jax.nn.softmax(s, axis=1)
        v = jnp.einsum('bnm,bmc->bnc', beta, hh)
        v = v.reshape(b, h, w, c)
        return gamma * v + x

    def _L2_attn_ref(x, Wq, bq, Wk, bk, Wv, bv, Wo, bo, Ws, bs):
        import jax, jax.numpy as jnp
        import numpy as np
        from jax import lax
        TAU_MEM = 10.0
        THRESHOLD = 1.0
        WINDOW = 128
        STRIDE = 64
        NUM_GLOBAL = 4

        def _spike_indicators(x, Ws, bs):
            B, S, D = x.shape
            decay = jnp.exp(jnp.float32(-1.0 / TAU_MEM))
            cur = x @ Ws + bs
            cur_t = jnp.swapaxes(cur, 0, 1)

            def step(mem, c):
                mem = decay * mem + c
                spk = mem >= THRESHOLD
                mem = jnp.where(spk, 0.0, mem)
                return (mem, spk.astype(jnp.float32))
            _, spikes = lax.scan(step, jnp.zeros((B, 1), jnp.float32), cur_t)
            spike_ind = spikes.mean(axis=1)[:, 0]
            return spike_ind != 0.0

        def _sparse_mask(S, spike_bool):
            i = jnp.arange(S)[:, None]
            j = jnp.arange(S)[None, :]
            local = (j <= i) & (j >= i - WINDOW)
            glob = j % STRIDE == 0
            first = j < NUM_GLOBAL
            return (local | glob | first) & spike_bool[None, :]
        B, S, D = x.shape
        spike_bool = _spike_indicators(x, Ws, bs)
        mask = _sparse_mask(S, spike_bool)
        Q = x @ Wq + bq
        K = x @ Wk + bk
        V = x @ Wv + bv
        scale = jnp.float32(1.0 / np.sqrt(D))
        scores = jnp.einsum('bid,bjd->bij', Q, K) * scale
        scores = jnp.where(mask[None, :, :], scores, -jnp.inf)
        w = jax.nn.softmax(scores, axis=-1)
        w = jnp.nan_to_num(w, nan=0.0)
        out = jnp.einsum('bij,bjd->bid', w, V)
        return out @ Wo + bo

    def _L2_ffn_ref(x, gate_w, gate_b, weight1, weight2):
        import jax, jax.numpy as jnp
        import numpy as np
        B, S, D, E, H, O, K = (512, 2048, 128, 64, 512, 128, 8)
        Bn, Sn, Dn = x.shape
        logits = jnp.einsum('bsd,ed->bse', x, gate_w) + gate_b
        probs = jax.nn.softmax(logits, axis=1)
        vals, idx = jax.lax.top_k(probs.transpose(0, 2, 1), K)
        topv = vals.transpose(0, 2, 1)
        topi = idx.transpose(0, 2, 1)
        flat_idx = topi.reshape(Bn, K * E)
        gathered = jnp.take_along_axis(x, flat_idx[:, :, None], axis=1)
        gathered = gathered.reshape(Bn, K, E, Dn)
        pooled = jnp.einsum('bked,bke->bed', gathered, topv)
        ones = jnp.ones((E, Bn, 1), dtype=x.dtype)
        h = jnp.concatenate([pooled.transpose(1, 0, 2), ones], axis=-1)
        h = jax.nn.gelu(jnp.einsum('ebd,edh->ebh', h, weight1), approximate=False)
        h = jnp.concatenate([h, ones], axis=-1)
        out = jnp.einsum('ebh,eho->ebo', h, weight2)
        out = out.transpose(1, 0, 2)
        weighted = jnp.einsum('beo,bke->bkeo', out, topv).reshape(Bn, K * E, O)
        outputs = jnp.zeros((Bn, Sn, O), dtype=x.dtype)
        outputs = outputs.at[jnp.arange(Bn)[:, None], flat_idx].add(weighted)
        return outputs

    def _L3_attn_ref(x):
        import jax, jax.numpy as jnp
        import numpy as np
        scores = jnp.einsum('bsd,btd->bst', x, x)
        attn_weights = jax.nn.softmax(scores, axis=-1)
        return jnp.einsum('bst,btd->bsd', attn_weights, x)

    def _L3_ffn_ref(x, W, V, gamma, beta):
        import jax, jax.numpy as jnp
        import numpy as np
        BN_EPS = 1e-05
        B, T, H = (x.shape[0], x.shape[1], W.shape[0])
        Wx = jnp.einsum('bti,hi->bth', x, W)
        flat = Wx.reshape(B * T, H)
        mean = jnp.mean(flat, axis=0)
        var = jnp.var(flat, axis=0)
        Wx = ((flat - mean) * jax.lax.rsqrt(var + BN_EPS) * gamma + beta).reshape(B, T, H)
        Vt = V.T

        def step(yt, wx_t):
            yt = jax.nn.sigmoid(wx_t + yt @ Vt)
            return (yt, yt)
        y0 = jnp.zeros((B, H), dtype=Wx.dtype)
        _, ys = jax.lax.scan(step, y0, jnp.swapaxes(Wx, 0, 1))
        return jnp.swapaxes(ys, 0, 1)

    def _gn(v, G=32, eps=1e-5):
        B_, H_, W_, C_ = v.shape
        g = v.reshape(B_, H_, W_, G, C_ // G)
        m = jnp.mean(g, axis=(1, 2, 4), keepdims=True)
        s = jnp.var(g, axis=(1, 2, 4), keepdims=True)
        return ((g - m) / jnp.sqrt(s + eps)).reshape(v.shape)

    def _ln_c(v, eps=1e-6):
        m = jnp.mean(v, axis=-1, keepdims=True)
        s = jnp.var(v, axis=-1, keepdims=True)
        return (v - m) / jnp.sqrt(s + eps)

    def _ln_t(v, eps=1e-5):
        m = jnp.mean(v, axis=-1, keepdims=True)
        s = jnp.var(v, axis=-1, keepdims=True)
        return (v - m) / jnp.sqrt(s + eps)

    def _to_tokens(v):
        B_, H_, W_, C_ = v.shape
        return v.reshape(B_, H_ * W_, C_)
    def _from_tokens(t, like):
        return t.reshape(like.shape)

    x = x + _L0_conv_ref(_gn(x), L0_conv_qkv_w, L0_conv_qkv_b, L0_conv_rpb, L0_conv_proj_w, L0_conv_proj_b)
    x = _L1_conv_ref(x, L1_conv_kernel_f, L1_conv_kernel_g, L1_conv_kernel_h, L1_conv_gamma)
    t = _to_tokens(x)
    t = t + _L2_attn_ref(_ln_t(t), L2_attn_Wq, L2_attn_bq, L2_attn_Wk, L2_attn_bk, L2_attn_Wv, L2_attn_bv, L2_attn_Wo, L2_attn_bo, L2_attn_Ws, L2_attn_bs)
    t = t + _L2_ffn_ref(_ln_t(t), L2_ffn_gate_w, L2_ffn_gate_b, L2_ffn_weight1, L2_ffn_weight2)
    t = t + _L3_attn_ref(_ln_t(t))
    t = t + _L3_ffn_ref(_ln_t(t), L3_ffn_W, L3_ffn_V, L3_ffn_gamma, L3_ffn_beta)
    x = _from_tokens(t, x)
    return x


_drawn_inputs = setup_inputs


def setup_inputs(seed=0):
    import zlib

    import numpy as np

    out = dict(_drawn_inputs(seed))
    spreads = {'L0_conv_qkv_b': (0.0, 0.1),
     'L0_conv_proj_b': (0.0, 0.1),
     'L2_attn_bq': (0.0, 0.356),
     'L2_attn_bk': (0.0, 2.0),
     'L2_attn_bv': (0.0, 0.1),
     'L2_attn_bo': (0.0, 0.1),
     'L2_ffn_gate_b': (0.0, 2.0),
     'L3_ffn_gamma': (1.0, 0.6),
     'L3_ffn_beta': (0.0, 0.8)}
    factors = {'L0_conv_rpb': 49.044,
     'L2_ffn_gate_w': 8.0,
     'L2_ffn_weight1': 6.723,
     'L2_ffn_weight2': 6.262}
    for name, (base, spread) in spreads.items():
        noise = np.random.default_rng([zlib.crc32(name.encode()), seed]).standard_normal(out[name].shape)
        drawn = base * np.exp(spread * noise) if base else spread * noise
        out[name] = jnp.asarray(drawn.astype(out[name].dtype))
    for name, factor in factors.items():
        out[name] = (out[name] * factor).astype(out[name].dtype)
    return out
```

```python
import concourse.bass as bass
import concourse.mybir as mybir
import numpy as np
from contextlib import ExitStack

FP32 = mybir.dt.float32
FP32R = mybir.dt.float32r
BF16 = mybir.dt.bfloat16
ALU = mybir.AluOpType
ACT = mybir.ActivationFunctionType
AX = mybir.AxisListType.X

B, H, W, C = 4, 56, 56, 128
N = H * W
TOKENS = B * N
TILE = 112
CHUNK = 4 * TILE
TILES = TOKENS // TILE
CHUNKS = TOKENS // CHUNK
CPI = N // CHUNK
TPI = N // TILE
BANK = 512
NEG = -1e30


def at_least(eng, sem, value):
    if not isinstance(value, int) or value > 0:
        eng.wait_ge(sem, value)


def paced(eng, count, step):
    step(0, 0, True, False)
    step(1, 1, False, False)
    with eng.Fori(1, count // 2 - 1) as j:
        step(2 * j, 0, False, False)
        step(2 * j + 1, 1, False, False)
    step(count - 2, 0, False, False)
    step(count - 1, 1, False, True)


def pipelined(eng, count, ops):
    deepest = max(lag for lag, _ in ops)
    head = deepest + deepest % 2 + 2

    def step(s, parity, lo, hi):
        for lag, op in ops:
            if lo is None or lo <= s - lag < hi:
                op(s - lag, (parity - lag) % 2)
    for s in range(head):
        step(s, s % 2, 0, count)
    with eng.Fori(head // 2, count // 2) as j:
        step(2 * j, 0, None, None)
        step(2 * j + 1, 1, None, None)
    for s in range(count, count + deepest):
        step(s, s % 2, 0, count)


def allocators(nc, ctx, stage):
    def sb(name, shape, dtype=FP32):
        return ctx.enter_context(nc.sbuf_tensor(f"{stage}_{name}", shape, dtype))

    def ps(name, shape, dtype=FP32):
        return ctx.enter_context(nc.psum_tensor(f"{stage}_{name}", shape, dtype))

    taken = []

    def sem(name):
        taken.append(nc.alloc_semaphore(f"{stage}_{name}"))
        return taken[-1]

    def give_back():
        nc.clear_and_free_semaphores(taken)
        nc.all_engine_barrier()
    ctx.callback(give_back)
    return sb, ps, sem


class Norm:

    def __init__(self, nc, ctx, stage, resid, mean_w, eps):
        sb, ps, sem = allocators(nc, ctx, stage + "_ln")
        self.nc, self.resid, self.mean_w, self.eps = nc, resid, mean_w, eps
        self.centred = sb("centred", [C, 2, CHUNK])
        self.squared = sb("squared", [C, 2, CHUNK])
        self.inverse = sb("inverse", [C, 2, CHUNK])
        self.normed = sb("normed", [C, 2, CHUNK])
        self.mean_ps = ps("mean_ps", [C, BANK])
        self.var_ps = ps("var_ps", [C, BANK])
        self.mean_done = sem("mean_done")
        self.centred_done = sem("centred_done")
        self.squared_done = sem("squared_done")
        self.var_done = sem("var_done")
        self.log_done = sem("log_done")
        self.inverse_done = sem("inverse_done")
        self.normed_done = sem("normed_done")

    def pe_mean(self, pe, i, u):
        at_least(pe, self.centred_done, i)
        self.nc.tensor.matmul(self.mean_ps[:, 0:CHUNK], self.mean_w[:, :],
                              self.resid[:, bass.ds(i * CHUNK, CHUNK)],
                              start=True, stop=True).then_inc(self.mean_done, 1)

    def pe_var(self, pe, i, u):
        pe.wait_ge(self.squared_done, i + 1)
        at_least(pe, self.log_done, i)
        self.nc.tensor.matmul(self.var_ps[:, 0:CHUNK], self.mean_w[:, :], self.squared[:, u, :],
                              start=True, stop=True).then_inc(self.var_done, 1)

    def dve_centre(self, dve, i, u):
        dve.wait_ge(self.mean_done, i + 1)
        at_least(dve, self.normed_done, i - 1)
        at_least(dve, self.squared_done, i - 1)
        self.nc.vector.tensor_tensor(self.centred[:, u, :], self.resid[:, bass.ds(i * CHUNK, CHUNK)],
                                     self.mean_ps[:, 0:CHUNK], ALU.subtract).then_inc(self.centred_done, 1)

    def act_square(self, act, i, u):
        act.wait_ge(self.centred_done, i + 1)
        at_least(act, self.var_done, i - 1)
        self.nc.scalar.activation(self.squared[:, u, :], self.centred[:, u, :],
                                  ACT.Square).then_inc(self.squared_done, 1)

    def act_inverse(self, act, i, u):
        act.wait_ge(self.var_done, i + 1)
        at_least(act, self.normed_done, i - 1)
        self.nc.scalar.activation(self.inverse[:, u, :], self.var_ps[:, 0:CHUNK], ACT.Ln,
                                  bias=self.eps[:, 0:1]).then_inc(self.log_done, 1)
        act.wait_ge(self.log_done, i + 1)
        self.nc.scalar.activation(self.inverse[:, u, :], self.inverse[:, u, :], ACT.Exp,
                                  scale=-0.5).then_inc(self.inverse_done, 1)

    def dve_normalise(self, dve, i, u, used):
        dve.wait_ge(self.inverse_done, i + 1)
        for sem, per_chunk in used:
            at_least(dve, sem, (i - 1) * per_chunk)
        self.nc.vector.tensor_tensor(self.normed[:, u, :], self.centred[:, u, :], self.inverse[:, u, :],
                                     ALU.mult).then_inc(self.normed_done, 1)

    def tensor_steps(self, pe, project):
        def step(i, u, first, last):
            if first:
                self.pe_mean(pe, i, u)
            if not last:
                self.pe_mean(pe, i + 1, 1 - u)
            self.pe_var(pe, i, u)
            if not first:
                project(i - 1, 1 - u)
            if last:
                project(i, u)
        paced(pe, CHUNKS, step)

    def vector_steps(self, dve, used, copy_out):
        def step(i, u, first, last):
            if first:
                self.dve_centre(dve, i, u)
            if not last:
                self.dve_centre(dve, i + 1, 1 - u)
            self.dve_normalise(dve, i, u, used)
            if not first:
                copy_out(i - 1, 1 - u)
            if last:
                copy_out(i, u)
        paced(dve, CHUNKS, step)

    def scalar_steps(self, act, copy_out):
        def step(i, u, first, last):
            if first:
                self.act_square(act, i, u)
            if not last:
                self.act_square(act, i + 1, 1 - u)
            self.act_inverse(act, i, u)
            if not first:
                copy_out(i - 1, 1 - u)
            if last:
                copy_out(i, u)
        paced(act, CHUNKS, step)


def shape_constants():
    span = np.arange(TILES)
    query, key = np.arange(TILE)[:, None], np.arange(C + TILE)[None, :]
    return {
        "not_first": (span % TPI != 0).astype(np.float32)[:, None],
        "group_mean": np.kron(np.eye(C // 4), np.full((4, 4), 0.25)).astype(np.float32),
        "head_rows": np.kron(np.eye(4), np.ones((C // 4, 1))).astype(np.float32),
        "image_sum": (span[:, None] % TPI == np.arange(TPI)[None, :]).astype(np.float32),
        "band": np.where((key >= query) & (key <= query + C), 0.0, NEG).astype(np.float32),
    }


def windowed_attention(nc, ctx, resid, io, ident, mean_w, eps):
    HEADS, D, KSIZE = 4, C // 4, 7
    PAD = KSIZE // 2
    SCALE = float(D) ** -0.5
    TW = 14
    TH = TILE // TW
    ACROSS = W // TW
    KW, KH = TW + 2 * PAD, TH + 2 * PAD
    KEYS = KW * KH
    LOTS, LOT = 3, 5 * KW
    PW = W + 2 * PAD
    PIXELS = (H + 2 * PAD) * PW
    RUNON = PW
    sb, ps, sem = allocators(nc, ctx, "window")
    k_t = sb("k_t", [C, B * PIXELS + RUNON])
    q_dram = nc.dram_tensor("window_q", [TILES, C, TILE], FP32).ap()
    v_dram = nc.dram_tensor("window_v", [B * PIXELS + RUNON, C], FP32).ap()
    BIAS_ROW = TW * KEYS + KW
    BIAS_HEAD = TH * BIAS_ROW
    bias_dram = nc.dram_tensor("window_bias_table", [HEADS * BIAS_HEAD], FP32).ap()
    proj_w = sb("proj_w", [C, C])
    proj_b = sb("proj_b", [C, 1])
    factor = sb("factor", [C, B])
    offset = sb("offset", [C, B])
    proj_in = sem("proj_in")

    def padded_pixel(chunk):
        return chunk // CPI * PIXELS + chunk % CPI * (CHUNK // W * PW) + PAD * PW + PAD

    with ExitStack() as own:
        sb1, ps1, sem1 = allocators(nc, own, "window_norm")
        group_mean = sb1("group_mean", [C, C])
        stats = sb1("stats", [C, CHUNKS, 6])
        moments = sb1("moments", [C, B, 2])
        apart = sb1("apart", [C, B])
        spread = sb1("spread", [C, B])
        negs = sb1("negs", [C, HEADS * BIAS_HEAD // C])
        mean_ps = ps1("mean_ps", [C, BANK])
        var_ps = ps1("var_ps", [C, BANK])
        weights = sem1("weights")
        negs_done = sem1("negs_done")
        bias_cleared = sem1("bias_cleared")
        bias_stored = sem1("bias_stored")
        borders = sem1("borders")
        zeroed = sem1("zeroed")
        stats_done = sem1("stats_done")
        moments_done = sem1("moments_done")
        means_done = sem1("means_done")
        chain = sem1("chain")
        var_done = sem1("var_done")
        log_done = sem1("log_done")
        zeros = sb1("zeros", [61, 2 * PAD * C])
        block = own.enter_context(nc.Block())

        @block.gpsimd
        def _(pool):
            nc.gpsimd.memset(negs[:, :], NEG).then_inc(negs_done, 1)
            nc.gpsimd.memset(zeros[:, :], 0.0).then_inc(zeroed, 1)
            nc.gpsimd.memset(k_t[:, :], 0.0)

        @block.sync
        def _(sp):
            sp.dma_start(group_mean[:, :], io["group_mean"]).then_inc(weights, 16)
            sp.wait_ge(negs_done, 1)
            sp.dma_start(bias_dram.rearrange("(p n) -> p n", p=C), negs[:, :]).then_inc(bias_cleared, 16)
            sp.wait_ge(zeroed, 1)
            edge = PAD * PW - PAD
            for b in range(B):
                top, side, low = b * PIXELS, b * PIXELS + edge, (b + 1) * PIXELS - edge
                for start in (top, low):
                    sp.dma_start(v_dram[start:start + edge, :].rearrange("(p a) c -> p (a c)", a=PAD),
                                 zeros[0:edge // PAD, 0:PAD * C]).then_inc(borders, 16)
                rows = v_dram[side:side + (H + 1) * PW, :].rearrange("(r w) c -> r w c", w=PW)
                sp.dma_start(rows[:, 0:2 * PAD, :].rearrange("r w c -> r (w c)"), zeros[0:H + 1, :])\
                  .then_inc(borders, 16)
            sp.dma_start(proj_w[:, :], io["proj_w"]).then_inc(proj_in, 16)
            sp.dma_start(proj_b[:, :], io["proj_b"]).then_inc(proj_in, 16)
            sp.wait_ge(bias_cleared, 16)
            for h in range(HEADS):
                own_bias = io["rpb"][h, PAD:PAD + KSIZE, PAD:PAD + KSIZE].unsqueeze(0)
                for r in range(TH):
                    start = h * BIAS_HEAD + r * BIAS_ROW
                    to = bias_dram[start:start + TW * (KEYS + 1)].rearrange("(q s) -> q s", s=KEYS + 1)
                    to = to[:, 0:KSIZE * KW].rearrange("q (a b) -> q a b", b=KW)[:, :, 0:KSIZE]
                    sp.dma_start(to, own_bias.to_broadcast([TW, KSIZE, KSIZE])).then_inc(bias_stored, 16)
            sp.wait_ge(borders, 3 * B * 16)
            sp.wait_ge(bias_stored, HEADS * TH * 16)

        @block.vector
        def _(dve):
            with dve.Fori(0, CHUNKS) as i:
                nc.vector.bn_stats(stats[:, bass.ds(i, 1), :].rearrange("p a s -> p (a s)"),
                                   resid[:, bass.ds(i * CHUNK, CHUNK)]).then_inc(stats_done, 1)
            dve.wait_ge(stats_done, CHUNKS)
            for b in range(B):
                nc.vector.bn_aggr(moments[:, b, :], stats[:, b * CPI:(b + 1) * CPI, :].rearrange("p a s -> p (a s)"))\
                    .then_inc(moments_done, 1)
            dve.wait_ge(moments_done, B)
            dve.wait_ge(means_done, 1)
            nc.vector.tensor_tensor(apart[:, :], moments[:, :, 0], mean_ps[:, 0:B], ALU.subtract).then_inc(chain, 1)
            dve.wait_ge(chain, 1)
            nc.vector.tensor_tensor(spread[:, :], apart[:, :], apart[:, :], ALU.mult).then_inc(chain, 1)
            dve.wait_ge(chain, 2)
            nc.vector.tensor_tensor(spread[:, :], spread[:, :], moments[:, :, 1], ALU.add).then_inc(chain, 1)
            dve.wait_ge(log_done, 2)
            nc.vector.tensor_tensor(offset[:, :], factor[:, :], mean_ps[:, 0:B], ALU.mult).then_inc(chain, 1)
            dve.wait_ge(chain, 4)
            nc.vector.tensor_scalar(offset[:, :], offset[:, :], -1.0, None, ALU.mult)

        @block.tensor
        def _(pe):
            pe.wait_ge(weights, 16)
            pe.wait_ge(moments_done, B)
            nc.tensor.matmul(mean_ps[:, 0:B], group_mean[:, :], moments[:, :, 0], start=True, stop=True)\
                .then_inc(means_done, 1)
            pe.wait_ge(chain, 3)
            nc.tensor.matmul(var_ps[:, 0:B], group_mean[:, :], spread[:, :], start=True, stop=True)\
                .then_inc(var_done, 1)

        @block.scalar
        def _(act):
            nc.scalar.preload_act_table_set("natural_log_exp_and_others")
            act.wait_ge(var_done, 1)
            nc.scalar.activation(factor[:, :], var_ps[:, 0:B], ACT.Ln, bias=eps[:, 0:1]).then_inc(log_done, 1)
            act.wait_ge(log_done, 1)
            nc.scalar.activation(factor[:, :], factor[:, :], ACT.Exp, scale=-0.5).then_inc(log_done, 1)

    with ExitStack() as own:
        sb1, ps1, sem1 = allocators(nc, own, "window_in")
        qkv_w = sb1("qkv_w", [C, 3 * C])
        qkv_b = sb1("qkv_b", [C, 3])
        v_bias = sb1("v_bias", [TILE, C])
        q_bias = sb1("q_bias", [C, 1])
        normed = sb1("normed", [C, 2, CHUNK])
        query = sb1("query", [C, 2, ACROSS, TILE])
        value = sb1("value", [TILE, 2, 4, C])
        qk_ps = ps1("qk_ps", [C, 2, 2, BANK])
        value_ps = ps1("value_ps", [TILE, 2, 4, C])
        weights = sem1("weights")
        q_bias_done = sem1("q_bias_done")
        normed_done = sem1("normed_done")
        q_done, k_done, value_done = sem1("q_done"), sem1("k_done"), sem1("value_done")
        q_out, k_out, value_out = sem1("q_out"), sem1("k_out"), sem1("value_out")
        q_stored = [sem1(f"q_stored{u}") for u in range(2)]
        v_stored = [sem1(f"v_stored{u}") for u in range(2)]
        block = own.enter_context(nc.Block())

        @block.sync
        def _(sp):
            sp.dma_start(qkv_w[:, :], io["qkv_w"]).then_inc(weights, 16)
            sp.dma_start(qkv_b[:, :], io["qkv_b"]).then_inc(weights, 16)
            sp.dma_start(v_bias[:, :], io["qkv_b_row"][:, 2 * C:3 * C].to_broadcast([TILE, C])).then_inc(weights, 16)

            def step(i, u, first, last):
                sp.wait_ge(q_out, i + 1)
                sp.dma_start(q_dram[bass.ds(i * 4, 4), :, :].rearrange("t c q -> c t q"), query[:, u, :, :])\
                  .then_inc(q_stored[u], 16)
                sp.wait_ge(value_out, i + 1)
                for r in range(2):
                    rows = v_dram[bass.ds(padded_pixel(i) + r * PW, 4 * 2 * PW), :]
                    sp.dma_start(rows.rearrange("(t w) c -> w t c", w=2 * PW)[0:W, :, :],
                                 value[r * W:(r + 1) * W, u, :, :]).then_inc(v_stored[u], 16)
            paced(sp, CHUNKS, step)
            for u in range(2):
                sp.wait_ge(q_stored[u], 16 * (CHUNKS // 2))
                sp.wait_ge(v_stored[u], 32 * (CHUNKS // 2))

        @block.tensor
        def _(pe):
            pe.wait_ge(weights, 48)

            def step(i, u, first, last):
                pe.wait_ge(normed_done, i + 1)
                for x, (done, out) in enumerate(((q_done, q_out), (k_done, k_out))):
                    at_least(pe, out, i - 1)
                    nc.tensor.matmul(qk_ps[:, u, x, 0:CHUNK], qkv_w[:, x * C:(x + 1) * C], normed[:, u, :],
                                     start=True, stop=True).then_inc(done, 1)
                at_least(pe, value_out, i - 1)
                for t in range(4):
                    mm = nc.tensor.matmul(value_ps[:, u, t, :], normed[:, u, t * TILE:(t + 1) * TILE],
                                          qkv_w[:, 2 * C:3 * C], start=True, stop=True)
                mm.then_inc(value_done, 1)
            paced(pe, CHUNKS, step)

        @block.scalar
        def _(act):
            act.wait_ge(weights, 48)
            nc.scalar.activation(q_bias[:, :], qkv_b[:, 0:1], ACT.Copy, scale=SCALE).then_inc(q_bias_done, 1)
            act.wait_ge(q_bias_done, 1)

            def step(i, u, first, last):
                act.wait_ge(q_done, i + 1)
                if not (isinstance(i, int) and i < 2):
                    act.wait_ge(q_stored[u], 8 * (i - u))
                by_tile = qk_ps[:, u, 0, 0:CHUNK].rearrange("p (r x c) -> p x r c", x=ACROSS, c=TW)
                nc.scalar.activation(query[:, u, :, :].rearrange("p x (r c) -> p x r c", c=TW), by_tile,
                                     ACT.Identity, bias=q_bias[:, 0:1], scale=SCALE).then_inc(q_out, 1)
                act.wait_ge(k_done, i + 1)
                rows = k_t[:, bass.ds(padded_pixel(i), CHUNK // W * PW)].rearrange("p (r w) -> p r w", w=PW)
                nc.scalar.activation(rows[:, :, 0:W], qk_ps[:, u, 1, 0:CHUNK].rearrange("p (r w) -> p r w", w=W),
                                     ACT.Identity, bias=qkv_b[:, 1:2]).then_inc(k_out, 1)
            paced(act, CHUNKS, step)

        @block.vector
        def _(dve):
            def normalise(i, u):
                at_least(dve, value_done, i - 1)
                nc.vector.tensor_scalar(normed[:, u, :], resid[:, bass.ds(i * CHUNK, CHUNK)],
                                        factor[:, bass.ds(i // CPI, 1)], offset[:, bass.ds(i // CPI, 1)],
                                        ALU.mult, ALU.add).then_inc(normed_done, 1)

            def copy_out(i, u):
                dve.wait_ge(value_done, i + 1)
                if not (isinstance(i, int) and i < 2):
                    dve.wait_ge(v_stored[u], 16 * (i - u))
                nc.vector.tensor_tensor(value[:, u, :, :], value_ps[:, u, :, :],
                                        v_bias[:, :].unsqueeze(1).to_broadcast([TILE, 4, C]), ALU.add)\
                    .then_inc(value_out, 1)

            def step(i, u, first, last):
                if first:
                    normalise(i, u)
                if not last:
                    normalise(i + 1, 1 - u)
                copy_out(i, u)
            dve.wait_ge(weights, 48)
            paced(dve, CHUNKS, step)

    bias = sb("bias", [TILE, HEADS, KEYS])
    query = sb("query", [C, 2, HEADS, TILE])
    values = sb("values", [LOT, 2, LOTS, C])
    probs = sb("probs", [TILE, 2, HEADS, LOTS * LOT])
    weights_t = sb("weights_t", [LOT, 2, LOTS, TILE])
    row_max = sb("row_max", [TILE, 2, HEADS])
    neg_max = sb("neg_max", [TILE, 2, HEADS])
    row_sum = sb("row_sum", [TILE, 2, HEADS])
    row_inv = sb("row_inv", [TILE, 2, HEADS])
    mixed = sb("mixed", [C, 2, TILE])
    gate = sb("gate", [1, HEADS])
    score_ps = ps("score_ps", [TILE, HEADS, BANK])
    turned_ps = ps("turned_ps", [LOT, 2, BANK])
    mixed_ps = ps("mixed_ps", [C, BANK])
    out_ps = ps("out_ps", [C, BANK])
    constants = sem("constants")
    bias_in = sem("bias_in")
    query_in = [sem(f"query_in{u}") for u in range(2)]
    values_in = [sem(f"values_in{u}") for u in range(2)]
    scores_done = sem("scores_done")
    biased = sem("biased")
    neg_done = sem("neg_done")
    exp_done = sem("exp_done")
    inv_done = sem("inv_done")
    probs_done = sem("probs_done")
    turned = sem("turned")
    even_out = sem("even_out")
    odd_out = sem("odd_out")
    mixed_done = sem("mixed_done")
    mixed_out = sem("mixed_out")
    out_done = sem("out_done")
    added = sem("added")
    block = ctx.enter_context(nc.Block())

    def first_key(n):
        return n // TPI * PIXELS + n % TPI // ACROSS * (TH * PW) + n % ACROSS * TW

    @block.sync
    def _(sp):
        sp.dma_start(bias[:, :, :],
                     bias_dram.rearrange("(h n) -> h n", h=HEADS)[:, 0:TILE * KEYS]
                     .rearrange("h (q k) -> q h k", k=KEYS)).then_inc(bias_in, 16)
        sp.wait_ge(constants, 3)

        def load_query(n, u):
            at_least(sp, scores_done, (n - 1) * HEADS)
            for h in range(HEADS):
                rows = slice(h * D, (h + 1) * D)
                sp.dma_start(query[rows, u, h, :], q_dram[bass.ds(n, 1), rows, :].rearrange("t c q -> (t c) q"))\
                  .then_inc(query_in[u], 16)

        def load_values(n, u):
            at_least(sp, mixed_done, n - 1)
            for x in range(LOTS):
                height = min(LOT // KW, KH - x * (LOT // KW))
                rows = v_dram[bass.ds(first_key(n) + x * (LOT // KW) * PW, height * PW), :]
                sp.dma_start(values[0:height * KW, u, x, :],
                             rows.rearrange("(r w) c -> r w c", w=PW)[:, 0:KW, :]).then_inc(values_in[u], 16)
        pipelined(sp, TILES, [(0, load_query), (2, load_values)])

    @block.gpsimd
    def _(pool):
        nc.gpsimd.memset(query[:, :, :, :], 0.0).then_inc(constants, 1)
        nc.gpsimd.memset(values[:, :, :, :], 0.0).then_inc(constants, 1)
        nc.gpsimd.memset(probs[:, :, :, :], 0.0).then_inc(constants, 1)

        def normalise(n, u):
            pool.wait_ge(inv_done, n + 1)
            nc.gpsimd.tensor_tensor(probs[:, u, :, 0:KEYS], probs[:, u, :, 0:KEYS],
                                    row_inv[:, u, :].unsqueeze(2).to_broadcast([TILE, HEADS, KEYS]), ALU.mult)\
                .then_inc(probs_done, 1)
        pipelined(pool, TILES, [(1, normalise)])

    @block.tensor
    def _(pe):
        def scores(h):
            def op(n, u):
                if h == 0:
                    pe.wait_ge(query_in[u], 16 * HEADS // 2 * (n - u) + 16 * HEADS)
                at_least(pe, biased, (n - 1) * HEADS + h + 1)
                keys = k_t[:, bass.ds(first_key(n), KH * PW)].rearrange("p (r w) -> p r w", w=PW)[:, :, 0:KW]
                nc.tensor.matmul(score_ps[:, h, 0:KEYS], query[:, u, h, :], keys, start=True, stop=True)\
                    .then_inc(scores_done, 1)
            return op

        def turn(h):
            def op(n, u):
                if h == 0:
                    pe.wait_ge(probs_done, n + 1)
                copied = odd_out if h % 2 else even_out
                at_least(pe, copied, n * 2 + h // 2)
                for x in range(LOTS):
                    mm = nc.tensor.transpose(turned_ps[:, h % 2, x * TILE:(x + 1) * TILE],
                                             probs[:, u, h, x * LOT:(x + 1) * LOT], ident[0:TILE, 0:TILE])
                mm.then_inc(turned, 1)
            return op

        def product(h):
            def op(n, u):
                if h == 0:
                    pe.wait_ge(values_in[u], 16 * LOTS // 2 * (n - u) + 16 * LOTS)
                    at_least(pe, mixed_out, n)
                copied = odd_out if h % 2 else even_out
                pe.wait_ge(copied, n * 2 + h // 2 + 1)
                for x in range(LOTS):
                    mm = nc.tensor.matmul(mixed_ps[h * D:(h + 1) * D, 0:TILE], values[:, u, x, h * D:(h + 1) * D],
                                          weights_t[:, h % 2, x, :], start=(x == 0), stop=(x == LOTS - 1))
                if h == HEADS - 1:
                    mm.then_inc(mixed_done, 1)
            return op

        def project(n, u):
            pe.wait_ge(mixed_out, n + 1)
            at_least(pe, added, n)
            nc.tensor.matmul(out_ps[:, 0:TILE], proj_w[:, :], mixed[:, u, :], start=True, stop=True)\
                .then_inc(out_done, 1)

        pe.wait_ge(proj_in, 32)
        pe.wait_ge(constants, 3)
        pipelined(pe, TILES, [
            (0, scores(0)), (2, turn(0)), (3, product(3)),
            (0, scores(1)), (2, turn(1)), (2, product(0)),
            (0, scores(2)), (2, turn(2)), (2, product(1)), (3, project),
            (0, scores(3)), (2, turn(3)), (2, product(2))])

    def turned_copy(eng, copy, h, done):
        def op(n, u):
            eng.wait_ge(turned, n * HEADS + h + 1)
            copy(weights_t[:, h % 2, :, :], turned_ps[:, h % 2, 0:LOTS * TILE].rearrange("p (x q) -> p x q", x=LOTS))\
                .then_inc(done, 1)
        return op

    @block.vector
    def _(dve):
        def add_bias(h):
            def op(n, u):
                dve.wait_ge(scores_done, n * HEADS + h + 1)
                at_least(dve, turned, (n - 2) * HEADS + h + 1)
                nc.vector.memset(gate[:, h:h + 1], 0.0)
                nc.vector.tensor_tensor_reduce(probs[:, u, h, 0:KEYS], score_ps[:, h, 0:KEYS], bias[:, h, :],
                                               1.0, -3e38, ALU.add, ALU.max, row_max[:, u, h:h + 1])\
                    .then_inc(biased, 1)
            return op

        def negative(n, u):
            dve.wait_ge(biased, (n + 1) * HEADS)
            nc.vector.tensor_scalar(neg_max[:, u, :], row_max[:, u, :], -1.0, None, ALU.mult).then_inc(neg_done, 1)

        def inverse(n, u):
            dve.wait_ge(exp_done, n + 1)
            at_least(dve, probs_done, n - 1)
            nc.vector.reciprocal(row_inv[:, u, :], row_sum[:, u, :]).then_inc(inv_done, 1)

        def add_up(n, u):
            dve.wait_ge(out_done, n + 1)
            at = resid[:, bass.ds(n // ACROSS * CHUNK, CHUNK)].rearrange("p (r w) -> p r w", w=W)
            at = at[:, :, bass.ds(n % ACROSS * TW, TW)]
            nc.vector.scalar_tensor_tensor(at, out_ps[:, 0:TILE].rearrange("p (r w) -> p r w", w=TW),
                                           proj_b[:, 0:1], at, ALU.add, ALU.add).then_inc(added, 1)

        def turned_copy_of(h):
            return turned_copy(dve, nc.vector.tensor_copy, h, even_out)
        dve.wait_ge(bias_in, 16)
        dve.wait_ge(proj_in, 32)
        dve.wait_ge(constants, 3)
        pipelined(dve, TILES, [
            (0, add_bias(0)), (2, turned_copy_of(0)), (0, add_bias(1)), (1, inverse),
            (0, add_bias(2)), (2, turned_copy_of(2)), (3, add_up), (0, add_bias(3)), (0, negative)])

    @block.scalar
    def _(act):
        def exponentials(h):
            def op(n, u):
                if h == 0:
                    act.wait_ge(neg_done, n + 1)
                    at_least(act, inv_done, n - 1)
                e = nc.scalar.activation(probs[:, u, h, 0:KEYS], probs[:, u, h, 0:KEYS], ACT.Exp,
                                         bias=neg_max[:, u, h:h + 1], accum_out=row_sum[:, u, h:h + 1])
                if h == HEADS - 1:
                    e.then_inc(exp_done, 1)
            return op

        def turned_copy_of(h):
            return turned_copy(act, lambda to, at: nc.scalar.activation(to, at, ACT.Copy), h, odd_out)

        def mixed_copy(n, u):
            act.wait_ge(mixed_done, n + 1)
            at_least(act, out_done, n - 1)
            nc.scalar.activation(mixed[:, u, :], mixed_ps[:, 0:TILE], ACT.Copy).then_inc(mixed_out, 1)

        pipelined(act, TILES, [
            (1, exponentials(0)), (1, exponentials(1)), (3, mixed_copy), (2, turned_copy_of(1)),
            (1, exponentials(2)), (1, exponentials(3)), (2, turned_copy_of(3))])


def channel_attention(nc, ctx, resid, io):
    D = 16
    STACK = 96
    GROUP = 4
    GROUPS = TILES // GROUP
    GPI = TPI // GROUP
    LAG = 4
    SBANKS = 4
    sb, ps, sem = allocators(nc, ctx, "chan")
    g_dram = nc.dram_tensor("g_scratch", [STACK, TOKENS], FP32).ap()
    f_dram = nc.dram_tensor("f_scratch", [STACK, TOKENS], FP32).ap()
    hh_dram = nc.dram_tensor("hh_scratch", [TILE, TILES, C], FP32).ap()

    with ExitStack() as own:
        sb1, ps1, sem1 = allocators(nc, own, "chan_in")
        gf_w = sb1("gf_w", [C, 2, STACK])
        hh_w = sb1("hh_w", [C, C])
        chunk = sb1("chunk", [C, 2, CHUNK])
        gf = sb1("gf", [STACK, 2, 2, CHUNK], FP32R)
        hh = sb1("hh", [TILE, 2, 4, C])
        gf_ps = ps1("gf_ps", [STACK, 2, 2, BANK])
        hh_ps = ps1("hh_ps", [TILE, 2, 4, C])
        weights = sem1("weights")
        zeroed = sem1("zeroed")
        staged = sem1("staged")
        gf_done = sem1("gf_done")
        hh_done = sem1("hh_done")
        hi_out = sem1("hi_out")
        gf_out = sem1("gf_out")
        hh_out = sem1("hh_out")
        stored = [sem1(f"stored{u}") for u in range(2)]
        block = own.enter_context(nc.Block())

        def stores_before(i, u):
            return 24 * (i - u)

        @block.gpsimd
        def _(pool):
            nc.gpsimd.memset(gf_w[:, :, :], 0.0).then_inc(zeroed, 1)

            def step(i, u, first, last):
                at_least(pool, hh_done, i - 1)
                nc.gpsimd.tensor_copy(chunk[:, u, :], resid[:, bass.ds(i * CHUNK, CHUNK)]).then_inc(staged, 1)
            paced(pool, CHUNKS, step)

        @block.sync
        def _(sp):
            sp.wait_ge(zeroed, 1)
            for p in range(0, STACK, 32):
                sp.dma_start(gf_w[:, 0, p:p + D], io["kernel_g"]).then_inc(weights, 16)
                sp.dma_start(gf_w[:, 1, p:p + D], io["kernel_f"]).then_inc(weights, 16)
            sp.dma_start(hh_w[:, :], io["kernel_h"]).then_inc(weights, 16)

            def step(i, u, first, last):
                sp.wait_ge(gf_out, i + 1)
                sp.wait_ge(hh_out, i + 1)
                sp.dma_start(g_dram[:, bass.ds(i * CHUNK, CHUNK)], gf[:, u, 0, :].bitcast(FP32)).then_inc(stored[u], 16)
                sp.dma_start(f_dram[:, bass.ds(i * CHUNK, CHUNK)], gf[:, u, 1, :].bitcast(FP32)).then_inc(stored[u], 16)
                sp.dma_start(hh_dram[:, bass.ds(i * 4, 4), :], hh[:, u, :, :]).then_inc(stored[u], 16)
            paced(sp, CHUNKS, step)
            for u in range(2):
                sp.wait_ge(stored[u], 48 * (CHUNKS // 2))

        @block.tensor
        def _(pe):
            pe.wait_ge(weights, 7 * 16)

            def step(i, u, first, last):
                pe.wait_ge(staged, i + 1)
                at_least(pe, gf_out, i - 1)
                for x in range(2):
                    mm = nc.tensor.matmul(gf_ps[:, u, x, 0:CHUNK], gf_w[:, x, :], chunk[:, u, :],
                                          start=True, stop=True)
                mm.then_inc(gf_done, 1)
                at_least(pe, hh_out, i - 1)
                for t in range(4):
                    mm = nc.tensor.matmul(hh_ps[:, u, t, :], chunk[:, u, t * TILE:(t + 1) * TILE], hh_w[:, :],
                                          start=True, stop=True)
                mm.then_inc(hh_done, 1)
            paced(pe, CHUNKS, step)

        @block.scalar
        def _(act):
            def step(i, u, first, last):
                act.wait_ge(gf_done, i + 1)
                if not first and not (isinstance(i, int) and i < 2):
                    act.wait_ge(stored[u], stores_before(i, u))
                nc.scalar.activation(gf[:, u, :, :], gf_ps[:, u, :, 0:CHUNK], ACT.Copy).then_inc(hi_out, 1)
            paced(act, CHUNKS, step)

        @block.vector
        def _(dve):
            def step(i, u, first, last):
                dve.wait_ge(hh_done, i + 1)
                if not (isinstance(i, int) and i < 2):
                    dve.wait_ge(stored[u], stores_before(i, u))
                nc.vector.tensor_copy(hh[:, u, :, :], hh_ps[:, u, :, :]).then_inc(hh_out, 1)
                dve.wait_ge(hi_out, i + 1)
                for x, p in ((0, 32), (1, 64)):
                    part = gf[p:p + 32, u, x, :]
                    lo = nc.vector.tensor_tensor(part, gf_ps[p:p + 32, u, x, 0:CHUNK], part.bitcast(FP32),
                                                 ALU.subtract)
                lo.then_inc(gf_out, 1)
            paced(dve, CHUNKS, step)

    g_row = sb("g_row", [STACK, 2, N], FP32R)
    f_cols = sb("f_cols", [STACK, 2, GROUP * TILE], FP32R)
    values = sb("values", [TILE, 2, GROUP, C])
    scaled = sb("scaled", [TILE, 2, GROUP, C])
    probs = sb("probs", [TILE, 2, GROUP, N])
    chunk_max = sb("chunk_max", [TILE, 2, GROUP, CPI])
    row_max = sb("row_max", [TILE, 2, GROUP])
    neg_max = sb("neg_max", [TILE, 2, GROUP])
    row_sum = sb("row_sum", [TILE, 2, GROUP])
    row_inv = sb("row_inv", [TILE, 2, GROUP])
    gamma = sb("gamma", [C, 1])
    score_ps = ps("score_ps", [TILE, SBANKS, BANK])
    out_ps = ps("out_ps", [C, 2, BANK])
    gamma_in = sem("gamma_in")
    loaded = [sem(f"loaded{u}") for u in range(2)]
    scores_done = sem("scores_done")
    copied = sem("copied")
    max_done = sem("max_done")
    neg_done = sem("neg_done")
    exp_done = sem("exp_done")
    inv_done = sem("inv_done")
    scaled_done = sem("scaled_done")
    product_done = sem("product_done")
    added = sem("added")
    block = ctx.enter_context(nc.Block())

    @block.sync
    def _(sp):
        sp.dma_start(gamma[:, :], io["gamma"]).then_inc(gamma_in, 16)

        def step(i, u, first, last):
            at_least(sp, scores_done, (i - 1) * GROUP * CPI)
            sp.dma_start(g_row[:, u, :].bitcast(FP32), g_dram[:, bass.ds((i // GPI) * N, N)]).then_inc(loaded[u], 16)
            sp.dma_start(f_cols[:, u, :].bitcast(FP32), f_dram[:, bass.ds(i * CHUNK, CHUNK)]).then_inc(loaded[u], 16)
            at_least(sp, scaled_done, (i - 1) * GROUP)
            sp.dma_start(values[:, u, :, :], hh_dram[:, bass.ds(i * GROUP, GROUP), :]).then_inc(loaded[u], 16)
        paced(sp, GROUPS, step)

    @block.tensor
    def _(pe):
        def scores(i, u, k):
            at_least(pe, copied, i * GROUP * CPI + k - (SBANKS - 1))
            m, c = k // CPI, k % CPI
            nc.tensor.matmul(score_ps[:, k % SBANKS, 0:CHUNK], f_cols[:, u, m * TILE:(m + 1) * TILE],
                             g_row[:, u, c * CHUNK:(c + 1) * CHUNK], start=True, stop=True)\
                .then_inc(scores_done, 1)

        def product(i, u, k):
            c, m = k // GROUP, k % GROUP
            if m == 0:
                if c == 0:
                    pe.wait_ge(scaled_done, (i + 1) * GROUP)
                at_least(pe, added, i * CPI + c - 1)
            mm = nc.tensor.matmul(out_ps[:, (u + c) % 2, 0:CHUNK], scaled[:, u, m, :],
                                  probs[:, u, m, c * CHUNK:(c + 1) * CHUNK],
                                  start=(m == 0), stop=(m == GROUP - 1))
            if m == GROUP - 1:
                mm.then_inc(product_done, 1)

        def step(i, u, first, last):
            pe.wait_ge(loaded[u], 24 * (i - u) + 48)
            for k in range(GROUP * CPI):
                scores(i, u, k)
                if not first and k >= LAG:
                    product(i - 1, 1 - u, k - LAG)
            if not first:
                for k in range(GROUP * CPI - LAG, GROUP * CPI):
                    product(i - 1, 1 - u, k)
            if last:
                for k in range(GROUP * CPI):
                    product(i, u, k)
        paced(pe, GROUPS, step)

    @block.vector
    def _(dve):
        def copy_out(i, u, k):
            m, c = k // CPI, k % CPI
            dve.wait_ge(scores_done, i * GROUP * CPI + k + 1)
            if k == 0:
                at_least(dve, product_done, (i - 1) * CPI)
            nc.vector.tensor_scalar(probs[:, u, m, c * CHUNK:(c + 1) * CHUNK], score_ps[:, k % SBANKS, 0:CHUNK],
                                    1.0, None, ALU.mult, ALU.max,
                                    accum_out=chunk_max[:, u, m, c:c + 1]).then_inc(copied, 1)

        def negative_max(i, u, m):
            dve.wait_ge(copied, (i * GROUP + m + 1) * CPI)
            nc.vector.tensor_reduce(row_max[:, u, m:m + 1], chunk_max[:, u, m, :], AX, ALU.max).then_inc(max_done, 1)
            dve.wait_ge(max_done, i * GROUP + m + 1)
            nc.vector.tensor_scalar(neg_max[:, u, m:m + 1], row_max[:, u, m:m + 1], -1.0, None, ALU.mult)\
                .then_inc(neg_done, 1)

        def scale_values(i, u, m):
            dve.wait_ge(exp_done, i * GROUP + m + 1)
            nc.vector.reciprocal(row_inv[:, u, m:m + 1], row_sum[:, u, m:m + 1]).then_inc(inv_done, 1)
            dve.wait_ge(inv_done, i * GROUP + m + 1)
            if m == 0:
                dve.wait_ge(loaded[u], 24 * (i - u) + 48)
            nc.vector.tensor_scalar(scaled[:, u, m, :], values[:, u, m, :], row_inv[:, u, m:m + 1], None, ALU.mult)\
                .then_inc(scaled_done, 1)

        def add_up(i, u, c):
            dve.wait_ge(product_done, i * CPI + c + 1)
            at = resid[:, bass.ds((i // GPI) * N + c * CHUNK, CHUNK)]
            nc.vector.scalar_tensor_tensor(at, out_ps[:, (u + c) % 2, 0:CHUNK], gamma[:, 0:1], at,
                                           ALU.mult, ALU.add).then_inc(added, 1)

        def step(i, u, first, last):
            for k in range(GROUP * CPI):
                copy_out(i, u, k)
                if k % CPI == CPI - 1:
                    negative_max(i, u, k // CPI)
                if k % CPI == LAG - 1:
                    if k >= CPI:
                        scale_values(i, u, k // CPI - 1)
                    elif not first:
                        scale_values(i - 1, 1 - u, GROUP - 1)
                if not first and k >= LAG + GROUP and (k - LAG) % GROUP == 0:
                    add_up(i - 1, 1 - u, (k - LAG) // GROUP - 1)
            if not first:
                for c in range((GROUP * CPI - 1 - LAG) // GROUP, CPI):
                    add_up(i - 1, 1 - u, c)
            if last:
                scale_values(i, u, GROUP - 1)
                for c in range(CPI):
                    add_up(i, u, c)
        dve.wait_ge(gamma_in, 16)
        paced(dve, GROUPS, step)

    @block.scalar
    def _(act):
        def step(i, u, first, last):
            for m in range(GROUP):
                act.wait_ge(neg_done, i * GROUP + m + 1)
                nc.scalar.activation(probs[:, u, m, :], probs[:, u, m, :], ACT.Exp, bias=neg_max[:, u, m:m + 1],
                                     accum_out=row_sum[:, u, m:m + 1]).then_inc(exp_done, 1)
        paced(act, GROUPS, step)


def sparse_attention(nc, ctx, resid, io, ident, mean_w, eps):
    WINDOW, STRIDE, FIRST = 128, 64, 4
    EVERY = N // STRIDE
    GLOBALS = EVERY + FIRST - 1
    LOCAL = WINDOW + TILE
    SCALE = float(np.float32(1.0 / np.sqrt(C)))
    DECAY = float(np.exp(np.float32(-1.0 / 10.0)))
    PADDED = WINDOW + N
    COLS = LOCAL + GLOBALS
    KEYS = 3 * C
    SPLIT = C - TILE
    sb, ps, sem = allocators(nc, ctx, "sparse")
    k_t = sb("k_t", [C, B * PADDED])
    q_t = sb("q_t", [C, TOKENS])
    k_every = sb("k_every", [C, B, GLOBALS])
    v_dram = nc.dram_tensor("sparse_v", [B * PADDED, C], FP32).ap()
    local_mask = sb("local_mask", [1, PADDED], BF16)
    every_mask = sb("every_mask", [1, GLOBALS], BF16)
    current = sb("current", [TILES, TILE])
    wo = sb("wo", [C, C])
    bo = sb("bo", [C, 1])
    loaded = sem("loaded")

    with ExitStack() as own:
        norm = Norm(nc, own, "sparse", resid, mean_w, eps)
        sb1, ps1, sem1 = allocators(nc, own, "sparse_in")
        wq, wk = sb1("wq", [C, C]), sb1("wk", [C, C])
        wvs = sb1("wvs", [C, C + 1])
        bq = sb1("bq", [C, 1])
        bk = sb1("bk", [C, 1])
        bv = sb1("bv", [TILE, C])
        bs = sb1("bs", [TILE, 1])
        value = sb1("value", [TILE, 2, 4, C])
        by_token = sb1("by_token", [TILE, TILES])
        zeros = sb1("zeros", [C, C])
        qk_ps = ps1("qk_ps", [C, 2, BANK])
        value_ps = ps1("value_ps", [TILE, 2, BANK])
        turn_ps = ps1("turn_ps", [C, BANK])
        zeroed = sem1("zeroed")
        weights = sem1("weights")
        q_done, k_done = sem1("q_done"), sem1("k_done")
        value_done = sem1("value_done")
        q_out, k_out = sem1("q_out"), sem1("k_out")
        value_out = sem1("value_out")
        stored = [sem1(f"stored{u}") for u in range(2)]
        padded = sem1("padded")
        turned = sem1("turned")
        block = own.enter_context(nc.Block())

        @block.gpsimd
        def _(pool):
            nc.gpsimd.memset(zeros[:, :], 0.0).then_inc(zeroed, 1)
            nc.gpsimd.memset(k_t[:, :].rearrange("p (b n) -> p b n", b=B)[:, :, 0:WINDOW], 0.0).then_inc(zeroed, 1)

        @block.sync
        def _(sp):
            for to, name in ((wq[:, :], "Wq"), (wk[:, :], "Wk"), (wvs[:, 0:C], "Wv"), (wvs[:, C:C + 1], "Ws"),
                             (bq[:, :], "bq"), (bk[:, :], "bk")):
                sp.dma_start(to, io[name]).then_inc(weights, 16)
            sp.dma_start(bv[:, :], io["bv"].to_broadcast([TILE, C])).then_inc(weights, 16)
            sp.dma_start(bs[:, :], io["bs"].to_broadcast([TILE, 1])).then_inc(weights, 16)
            sp.dma_start(wo[:, :], io["Wo"]).then_inc(loaded, 16)
            sp.dma_start(bo[:, :], io["bo"]).then_inc(loaded, 16)
            sp.wait_ge(zeroed, 2)
            for b in range(B):
                sp.dma_start(v_dram[b * PADDED:b * PADDED + WINDOW, :], zeros[:, :]).then_inc(padded, 16)

            def step(i, u, first, last):
                sp.wait_ge(value_out, i + 1)
                row = i * CHUNK + (i // CPI + 1) * WINDOW
                sp.dma_start(v_dram[bass.ds(row, CHUNK), :].rearrange("(t p) c -> p t c", p=TILE),
                             value[:, u, :, :]).then_inc(stored[u], 16)
            paced(sp, CHUNKS, step)
            sp.wait_ge(padded, 16 * B)
            for u in range(2):
                sp.wait_ge(stored[u], 16 * (CHUNKS // 2))

        @block.tensor
        def _(pe):
            pe.wait_ge(weights, 8 * 16)

            def project(i, u):
                pe.wait_ge(norm.normed_done, i + 1)
                x = norm.normed[:, u, :]
                at_least(pe, q_out, i)
                nc.tensor.matmul(qk_ps[:, 0, 0:CHUNK], wq[:, :], x, start=True, stop=True).then_inc(q_done, 1)
                at_least(pe, k_out, i)
                nc.tensor.matmul(qk_ps[:, 1, 0:CHUNK], wk[:, :], x, start=True, stop=True).then_inc(k_done, 1)
                at_least(pe, value_out, i)
                for t in range(4):
                    mm = nc.tensor.matmul(value_ps[:, t // 2, t % 2 * 256:t % 2 * 256 + C + 1],
                                          norm.normed[:, u, t * TILE:(t + 1) * TILE], wvs[:, :],
                                          start=True, stop=True)
                mm.then_inc(value_done, 1)
            norm.tensor_steps(pe, project)
            pe.wait_ge(value_out, CHUNKS)
            nc.tensor.transpose(turn_ps[0:TILES, 0:TILE], by_token[:, :], ident[0:TILE, 0:TILE]).then_inc(turned, 1)

        @block.scalar
        def _(act):
            nc.scalar.preload_act_table_set("natural_log_exp_and_others")
            act.wait_ge(weights, 8 * 16)

            def copy_out(i, u):
                act.wait_ge(q_done, i + 1)
                nc.scalar.activation(q_t[:, bass.ds(i * CHUNK, CHUNK)], qk_ps[:, 0, 0:CHUNK], ACT.Identity,
                                     bias=bq[:, 0:1]).then_inc(q_out, 1)
                act.wait_ge(k_done, i + 1)
                nc.scalar.activation(k_t[:, bass.ds(i * CHUNK + (i // CPI + 1) * WINDOW, CHUNK)],
                                     qk_ps[:, 1, 0:CHUNK], ACT.Identity, bias=bk[:, 0:1]).then_inc(k_out, 1)
            norm.scalar_steps(act, copy_out)

        @block.vector
        def _(dve):
            dve.wait_ge(weights, 8 * 16)

            def copy_out(i, u):
                dve.wait_ge(value_done, i + 1)
                if not (isinstance(i, int) and i < 2):
                    dve.wait_ge(stored[u], 8 * (i - u))
                tiles = value_ps[:, :, :].rearrange("p a (b n) -> p (a b) n", b=2)
                nc.vector.tensor_scalar(by_token[:, bass.ds(i * 4, 4)], tiles[:, :, C], bs[:, 0:1], None, ALU.add)
                nc.vector.tensor_tensor(value[:, u, :, :], tiles[:, :, 0:C],
                                        bv[:, :].unsqueeze(1).to_broadcast([TILE, 4, C]), ALU.add)\
                    .then_inc(value_out, 1)
            norm.vector_steps(dve, ((value_done, 1),), copy_out)
            dve.wait_ge(turned, 1)
            nc.vector.tensor_copy(current[:, :], turn_ps[0:TILES, 0:TILE])
            dve.wait_ge(k_out, CHUNKS)
            images = k_t[:, :].rearrange("p (b n) -> p b n", b=B)
            nc.vector.tensor_copy(k_every[:, :, 0:EVERY], images[:, :, WINDOW:PADDED:STRIDE])
            nc.vector.tensor_copy(k_every[:, :, EVERY:GLOBALS], images[:, :, WINDOW + 1:WINDOW + FIRST])

    with ExitStack() as own:
        sb1, ps1, sem1 = allocators(nc, own, "sparse_fire")
        mask_dram = nc.dram_tensor("sparse_mask", [TPI, TILE], BF16).ap()
        LOT = 16
        STEPS = TILE // LOT * (2 * LOT + 2)
        RUNS = 3
        charge = sb1("charge", [TILES, TILE])
        lot_in = sb1("lot_in", [TILES, LOT])
        lot_charge = sb1("lot_charge", [TILES, LOT])
        start = sb1("start", [TILES, 1])
        state = sb1("state", [TILES, 2])
        end = sb1("end", [TILES, 1])
        fired = sb1("fired", [TILES, TILE])
        apart = sb1("apart", [TILES, 1])
        ones = sb1("ones", [TILES, 1])
        not_first = sb1("not_first", [TILES, 1])
        image_sum = sb1("image_sum", [TILES, TPI])
        mask_rows = sb1("mask_rows", [TPI, TILE], BF16)
        count = sb1("count", [1, 1], mybir.dt.int32)
        sum_ps = ps1("sum_ps", [C, BANK])
        count_ps = ps1("count_ps", [C, BANK])
        constants = sem1("constants")
        consts_in = sem1("consts_in")
        chain = sem1("chain")
        again_chain = sem1("again_chain")
        moved = sem1("moved")
        moved_again = sem1("moved_again")
        end_out = sem1("end_out")
        end_again = sem1("end_again")
        count_ready = sem1("count_ready")
        count_done = sem1("count_done")
        count_out = sem1("count_out")
        fired_done = sem1("fired_done")
        sum_done = sem1("sum_done")
        rows_out = sem1("rows_out")
        flat = sem1("flat")
        block = own.enter_context(nc.Block())

        def shift_down(sp, to):
            return sp.dma_start(start[1:TILES, :], end[0:TILES - 1, :]).then_inc(to, 16)

        @block.gpsimd
        def _(pool):
            nc.gpsimd.memset(ones[:, :], 1.0).then_inc(constants, 1)
            nc.gpsimd.memset(local_mask[0:1, 0:WINDOW], NEG).then_inc(constants, 1)

        @block.sync
        def _(sp):
            sp.dma_start(not_first[:, :], io["not_first"]).then_inc(consts_in, 16)
            sp.dma_start(image_sum[:, :], io["image_sum"]).then_inc(consts_in, 16)
            for r in range(1, RUNS):
                sp.wait_ge(end_out, r)
                shift_down(sp, moved)
            sp.wait_ge(count_out, 1)
            wrong = sp.value_load(count[0:1, 0:1])
            with sp.If(wrong):
                with sp.Fori(0, TPI) as r:
                    sp.wait_ge(end_again, r)
                    shift_down(sp, moved_again)
            sp.wait_ge(rows_out, 1)
            sp.dma_start(mask_dram[:, :], mask_rows[:, :]).then_inc(flat, 16)
            sp.wait_ge(flat, 16)
            sp.dma_start(local_mask[0:1, WINDOW:PADDED], mask_dram.rearrange("(a s) n -> a (s n)", a=1))\
              .then_inc(flat, 16)

        def run(dve, links, base):
            per_lot = 2 * LOT + 2
            with dve.Fori(0, TILE // LOT) as g:
                at = base + g * per_lot
                dve.wait_ge(links, at)
                nc.vector.tensor_copy(lot_in[:, :], current[:, bass.ds(g * LOT, LOT)]).then_inc(links, 1)
                for k in range(LOT):
                    u = k % 2
                    dve.wait_ge(links, at + 1 + 2 * k)
                    nc.vector.scalar_tensor_tensor(lot_charge[:, k:k + 1], state[:, 1 - u:2 - u], DECAY,
                                                   lot_in[:, k:k + 1], ALU.mult, ALU.add).then_inc(links, 1)
                    dve.wait_ge(links, at + 2 + 2 * k)
                    nc.vector.scalar_tensor_tensor(state[:, u:u + 1], lot_charge[:, k:k + 1], 1.0,
                                                   lot_charge[:, k:k + 1], ALU.is_lt, ALU.mult).then_inc(links, 1)
                nc.vector.tensor_copy(charge[:, bass.ds(g * LOT, LOT)], lot_charge[:, :]).then_inc(links, 1)
            dve.wait_ge(links, base + STEPS)
            return nc.vector.tensor_copy(end[:, :], state[:, 1:2])

        @block.vector
        def _(dve):
            dve.wait_ge(constants, 2)
            dve.wait_ge(consts_in, 32)
            nc.vector.memset(start[:, :], 0.0).then_inc(chain, 1)
            nc.vector.memset(state[:, :], 0.0).then_inc(chain, 1)
            run(dve, chain, 2).then_inc(end_out, 1)
            done = 2 + STEPS
            for r in range(1, RUNS):
                dve.wait_ge(moved, 16 * r)
                nc.vector.tensor_tensor(state[:, 1:2], start[:, :], not_first[:, :], ALU.mult).then_inc(chain, 1)
                done += 1
                if r == RUNS - 1:
                    nc.vector.tensor_copy(apart[:, :], end[:, :]).then_inc(chain, 1)
                    done += 1
                run(dve, chain, done).then_inc(end_out, 1)
                done += STEPS
            dve.wait_ge(end_out, RUNS)
            nc.vector.tensor_tensor(apart[:, :], apart[:, :], end[:, :], ALU.not_equal).then_inc(count_ready, 1)
            dve.wait_ge(count_done, 1)
            nc.vector.tensor_copy(count[:, :], count_ps[0:1, 0:1]).then_inc(count_out, 1)
            dve.wait_ge(count_out, 1)
            wrong = dve.value_load(count[0:1, 0:1])
            with dve.If(wrong):
                with dve.Fori(0, TPI) as r:
                    dve.wait_ge(moved_again, 16 * (r + 1))
                    nc.vector.tensor_tensor(state[:, 1:2], start[:, :], not_first[:, :], ALU.mult)\
                        .then_inc(again_chain, 1)
                    run(dve, again_chain, r * (STEPS + 1) + 1).then_inc(end_again, 1)
                dve.wait_ge(end_again, TPI)
            nc.vector.tensor_scalar(fired[:, :], charge[:, :], 1.0, None, ALU.is_ge).then_inc(fired_done, 1)
            dve.wait_ge(sum_done, 1)
            nc.vector.tensor_scalar(mask_rows[:, :], sum_ps[0:TPI, 0:TILE], 0.5, NEG, ALU.is_lt, ALU.mult)\
                .then_inc(rows_out, 1)
            dve.wait_ge(flat, 32)
            nc.vector.tensor_copy(every_mask[0:1, 0:EVERY], local_mask[0:1, WINDOW:PADDED:STRIDE]).then_inc(rows_out, 1)
            nc.vector.tensor_copy(every_mask[0:1, EVERY:GLOBALS],
                                  local_mask[0:1, WINDOW + 1:WINDOW + FIRST]).then_inc(rows_out, 1)
            dve.wait_ge(rows_out, 3)
            nc.vector.memset(local_mask[0:1, WINDOW:PADDED:STRIDE], NEG).then_inc(rows_out, 1)
            nc.vector.memset(local_mask[0:1, WINDOW + 1:WINDOW + FIRST], NEG)

        @block.tensor
        def _(pe):
            pe.wait_ge(constants, 2)
            pe.wait_ge(count_ready, 1)
            nc.tensor.matmul(count_ps[0:1, 0:1], apart[:, :], ones[:, :], start=True, stop=True).then_inc(count_done, 1)
            pe.wait_ge(consts_in, 32)
            pe.wait_ge(fired_done, 1)
            nc.tensor.matmul(sum_ps[0:TPI, 0:TILE], image_sum[:, :], fired[:, :], start=True, stop=True)\
                .then_inc(sum_done, 1)

    band = sb("band", [TILE, LOCAL], BF16)
    band_full = sb("band_full", [TILE, LOCAL])
    ident_half = sb("ident_half", [TILE, TILE], BF16)
    ones_row = sb("ones_row", [1, TILE], BF16)
    query = sb("query", [C, 2, TILE])
    values = sb("values", [C, 2, 3, C])
    probs = sb("probs", [TILE, 2, KEYS])
    weights_t = sb("weights_t", [C, 2, 3, TILE])
    row_max = sb("row_max", [TILE, 2])
    neg_max = sb("neg_max", [TILE, 2])
    row_sum = sb("row_sum", [TILE, 2])
    row_inv = sb("row_inv", [TILE, 2])
    mixed = sb("mixed", [C, 2, TILE])
    score_ps = ps("score_ps", [TILE, 2, BANK])
    turned_ps = ps("turned_ps", [C, 2, BANK])
    mixed_ps = ps("mixed_ps", [C, 2, BANK])
    out_ps = ps("out_ps", [C, 2, BANK])
    constants = sem("constants")
    band_in = sem("band_in")
    band_out = sem("band_out")
    query_in = sem("query_in")
    values_in = [sem(f"values_in{u}") for u in range(2)]
    scores_done = sem("scores_done")
    max_done = sem("max_done")
    neg_done = sem("neg_done")
    exp_done = sem("exp_done")
    sum_safe = sem("sum_safe")
    inv_done = sem("inv_done")
    probs_done = sem("probs_done")
    turned = sem("turned")
    turned_out = sem("turned_out")
    mixed_done = sem("mixed_done")
    mixed_out = sem("mixed_out")
    out_done = sem("out_done")
    added = sem("added")
    block = ctx.enter_context(nc.Block())

    @block.gpsimd
    def _(pool):
        nc.gpsimd.memset(ones_row[:, :], 1.0).then_inc(constants, 1)
        nc.gpsimd.memset(probs[:, :, :], 0.0).then_inc(constants, 1)
        nc.gpsimd.memset(values[:, :, :, :], 0.0).then_inc(constants, 1)

    @block.sync
    def _(sp):
        sp.dma_start(band_full[:, :], io["band"]).then_inc(band_in, 16)
        sp.wait_ge(constants, 3)
        with sp.Fori(0, B) as b:
            def step(t, u, first, last):
                n = b * TPI + t
                if isinstance(t, int) and t < 2:
                    sp.wait_ge(mixed_done, b * TPI)
                else:
                    sp.wait_ge(mixed_done, n - 1)
                row = b * PADDED + t * TILE
                sp.dma_start(values[:, u, 0, :], v_dram[bass.ds(row, WINDOW), :]).then_inc(values_in[u], 16)
                sp.dma_start(values[0:TILE, u, 1, :], v_dram[bass.ds(row + WINDOW, TILE), :])\
                  .then_inc(values_in[u], 16)
                if isinstance(t, int) and t < 2:
                    every = v_dram[bass.ds(b * PADDED + WINDOW, N), :].rearrange("(g s) c -> g s c", s=STRIDE)
                    sp.dma_start(values[TILE:C, u, 1, :], every[0:SPLIT, 0, :]).then_inc(values_in[u], 16)
                    sp.dma_start(values[0:EVERY - SPLIT, u, 2, :], every[SPLIT:EVERY, 0, :])\
                      .then_inc(values_in[u], 16)
                    sp.dma_start(values[EVERY - SPLIT:GLOBALS - SPLIT, u, 2, :],
                                 v_dram[bass.ds(b * PADDED + WINDOW + 1, FIRST - 1), :]).then_inc(values_in[u], 16)
            paced(sp, TPI, step)

    def values_loaded(n, u):
        return (n - u) * 16 + n // TPI * 48 + 80

    @block.tensor
    def _(pe):
        def scores(n, u):
            pe.wait_ge(query_in, n + 1)
            at_least(pe, exp_done, n - 1)
            s = score_ps[:, u, :]
            nc.tensor.matmul(s[:, 0:LOCAL], query[:, u, :], k_t[:, bass.ds(n * TILE + n // TPI * WINDOW, LOCAL)],
                             start=True, stop=False)
            nc.tensor.matmul(s[:, 0:LOCAL], ident_half[:, :], band[:, :], start=False, stop=False)
            nc.tensor.matmul(s[:, 0:LOCAL], ones_row[:, :],
                             local_mask[0:1, bass.ds(n % TPI * TILE, LOCAL)], start=False, stop=True)
            nc.tensor.matmul(s[:, LOCAL:COLS], query[:, u, :], every_t[:, bass.ds(n // TPI * GLOBALS, GLOBALS)],
                             start=True, stop=False)
            nc.tensor.matmul(s[:, LOCAL:COLS], ones_row[:, :], every_mask[:, :], start=False, stop=True)\
                .then_inc(scores_done, 1)

        def turn(n, u):
            pe.wait_ge(probs_done, n + 1)
            at_least(pe, turned_out, n - 1)
            for x in range(3):
                mm = nc.tensor.transpose(turned_ps[:, u, x * TILE:(x + 1) * TILE],
                                         probs[:, u, x * C:(x + 1) * C], ident[0:TILE, 0:TILE])
            mm.then_inc(turned, 1)

        def product(n, u):
            pe.wait_ge(values_in[u], values_loaded(n, u))
            pe.wait_ge(turned_out, n + 1)
            at_least(pe, mixed_out, n - 1)
            for x in range(3):
                mm = nc.tensor.matmul(mixed_ps[:, u, 0:TILE], values[:, u, x, :], weights_t[:, u, x, :],
                                      start=(x == 0), stop=(x == 2))
            mm.then_inc(mixed_done, 1)

        def project(n, u):
            pe.wait_ge(mixed_out, n + 1)
            at_least(pe, added, n - 1)
            nc.tensor.matmul(out_ps[:, u, 0:TILE], wo[:, :], mixed[:, u, :], start=True, stop=True)\
                .then_inc(out_done, 1)

        every_t = k_every[:, :, :].rearrange("p b g -> p (b g)")
        pe.wait_ge(constants, 3)
        pe.wait_ge(band_out, 2)
        pe.wait_ge(loaded, 32)
        pipelined(pe, TILES, [(0, scores), (2, turn), (3, product), (4, project)])

    @block.scalar
    def _(act):
        def take_query(n, u):
            at_least(act, scores_done, n - 1)
            nc.scalar.activation(query[:, u, :], q_t[:, bass.ds(n * TILE, TILE)], ACT.Copy).then_inc(query_in, 1)

        def exponential(n, u):
            act.wait_ge(neg_done, n + 1)
            at_least(act, turned, n - 1)
            at_least(act, inv_done, n - 1)
            nc.scalar.activation(probs[:, u, 0:COLS], score_ps[:, u, 0:COLS], ACT.Exp, bias=neg_max[:, u:u + 1],
                                 scale=SCALE, accum_out=row_sum[:, u:u + 1]).then_inc(exp_done, 1)

        def copy_mixed(n, u):
            act.wait_ge(mixed_done, n + 1)
            at_least(act, out_done, n - 1)
            nc.scalar.activation(mixed[:, u, :], mixed_ps[:, u, 0:TILE], ACT.Copy).then_inc(mixed_out, 1)

        act.wait_ge(constants, 3)
        pipelined(act, TILES, [(0, take_query), (2, exponential), (4, copy_mixed)])

    @block.vector
    def _(dve):
        def largest(n, u):
            dve.wait_ge(scores_done, n + 1)
            nc.vector.tensor_reduce(row_max[:, u:u + 1], score_ps[:, u, 0:COLS], AX, ALU.max).then_inc(max_done, 1)
            dve.wait_ge(max_done, n + 1)
            at_least(dve, exp_done, n - 1)
            nc.vector.tensor_scalar(neg_max[:, u:u + 1], row_max[:, u:u + 1], NEG / 10, -SCALE, ALU.max, ALU.mult)\
                .then_inc(neg_done, 1)

        def normalise(n, u):
            dve.wait_ge(exp_done, n + 1)
            nc.vector.tensor_scalar(row_inv[:, u:u + 1], row_sum[:, u:u + 1], 1e-30, None, ALU.max)\
                .then_inc(sum_safe, 1)
            dve.wait_ge(sum_safe, n + 1)
            nc.vector.reciprocal(row_inv[:, u:u + 1], row_inv[:, u:u + 1]).then_inc(inv_done, 1)
            dve.wait_ge(inv_done, n + 1)
            nc.vector.tensor_scalar(probs[:, u, 0:COLS], probs[:, u, 0:COLS], row_inv[:, u:u + 1], None,
                                    ALU.mult).then_inc(probs_done, 1)

        def copy_turned(n, u):
            dve.wait_ge(turned, n + 1)
            at_least(dve, mixed_done, n - 1)
            nc.vector.tensor_copy(weights_t[:, u, :, :].rearrange("p x n -> p (x n)"),
                                  turned_ps[:, u, 0:3 * TILE]).then_inc(turned_out, 1)

        def add(n, u):
            dve.wait_ge(out_done, n + 1)
            at = resid[:, bass.ds(n * TILE, TILE)]
            nc.vector.scalar_tensor_tensor(at, out_ps[:, u, 0:TILE], bo[:, 0:1], at, ALU.add, ALU.add)\
                .then_inc(added, 1)

        nc.vector.tensor_copy(ident_half[:, :], ident[0:TILE, 0:TILE]).then_inc(band_out, 1)
        dve.wait_ge(band_in, 16)
        nc.vector.tensor_copy(band[:, :], band_full[:, :]).then_inc(band_out, 1)
        dve.wait_ge(loaded, 32)
        pipelined(dve, TILES, [(1, normalise), (0, largest), (2, copy_turned), (4, add)])


def expert_choice(nc, ctx, resid, io, ident, mean_w, eps):
    E = 64
    HID = io["weight1"].shape[2]
    KCH = HID // C
    GROUP = 4
    PAIRS = B // 2
    sb, ps, sem = allocators(nc, ctx, "expert")
    z = sb("z", [TILE, TILES, C])
    weights = sb("weights", [C, PAIRS, N])
    exp_sum = sb("exp_sum", [C, PAIRS])
    bias1 = sb("bias1", [C, E, KCH])
    bias2 = sb("bias2", [C, E])
    biases = sem("biases")
    pooled_t = sb("pooled_t", [C, B, E])

    with ExitStack() as first_half:
        logits = allocators(nc, first_half, "expert_gate")[0]("logits", [C, B, N])
        with ExitStack() as own:
            norm = Norm(nc, own, "expert", resid, mean_w, eps)
            sb1, ps1, sem1 = allocators(nc, own, "expert_in")
            gate = sb1("gate", [C, 2, E])
            gate_b = sb1("gate_b", [C, 1])
            turned_ps = ps1("turned_ps", [TILE, 2, 4, C])
            logit_ps = ps1("logit_ps", [C, 2, BANK])
            gate_in = sem1("gate_in")
            turned = sem1("turned")
            z_out = sem1("z_out")
            logit_done = sem1("logit_done")
            logit_out = sem1("logit_out")
            block = own.enter_context(nc.Block())

            @block.sync
            def _(sp):
                for h in range(2):
                    sp.dma_start(gate[:, h, :], io["gate_w"]).then_inc(gate_in, 16)
                    sp.dma_start(gate_b[h * E:(h + 1) * E, :], io["gate_b"]).then_inc(gate_in, 16)
                sp.dma_start(bias1[:, :, :], io["bias1"]).then_inc(biases, 16)
                sp.dma_start(bias2[:, :], io["bias2"]).then_inc(biases, 16)

            @block.tensor
            def _(pe):
                pe.wait_ge(gate_in, 64)

                def project(i, u):
                    pe.wait_ge(norm.normed_done, i + 1)
                    at_least(pe, logit_out, i - 1)
                    nc.tensor.matmul(logit_ps[:, u, 0:CHUNK], gate[:, :, :].rearrange("p h e -> p (h e)"),
                                     norm.normed[:, u, :], start=True, stop=True).then_inc(logit_done, 1)
                    at_least(pe, z_out, i - 1)
                    for t in range(4):
                        mm = nc.tensor.transpose(turned_ps[:, u, t, :], norm.normed[:, u, t * TILE:(t + 1) * TILE],
                                                 ident[:, :])
                    mm.then_inc(turned, 1)
                norm.tensor_steps(pe, project)

            @block.vector
            def _(dve):
                def copy_out(i, u):
                    dve.wait_ge(turned, i + 1)
                    nc.vector.tensor_copy(z[:, bass.ds(i * 4, 4), :], turned_ps[:, u, :, :]).then_inc(z_out, 1)
                norm.vector_steps(dve, ((turned, 1),), copy_out)

            @block.scalar
            def _(act):
                nc.scalar.preload_act_table_set("natural_log_exp_and_others")
                act.wait_ge(gate_in, 64)
                flat = logits[:, :, :].rearrange("p b n -> p (b n)")

                def copy_out(i, u):
                    act.wait_ge(logit_done, i + 1)
                    nc.scalar.activation(flat[:, bass.ds(i * CHUNK, CHUNK)], logit_ps[:, u, 0:CHUNK], ACT.Identity,
                                         bias=gate_b[:, 0:1]).then_inc(logit_out, 1)
                norm.scalar_steps(act, copy_out)

        with ExitStack() as own:
            sb1, _, sem1 = allocators(nc, own, "expert_soft")
            largest = sb1("largest", [C, B])
            max_done = sem1("max_done")
            neg_done = sem1("neg_done")
            block = own.enter_context(nc.Block())

            @block.vector
            def _(dve):
                for b in range(B):
                    nc.vector.tensor_reduce(largest[:, b:b + 1], logits[:, b, :], AX, ALU.max).then_inc(max_done, 1)
                    dve.wait_ge(max_done, b + 1)
                    nc.vector.tensor_scalar(largest[:, b:b + 1], largest[:, b:b + 1], -1.0, None, ALU.mult)\
                        .then_inc(neg_done, 1)

            @block.scalar
            def _(act):
                for b in range(B):
                    rows = slice(b % 2 * E, b % 2 * E + E)
                    act.wait_ge(neg_done, b + 1)
                    nc.scalar.activation(weights[rows, b // 2, :], logits[rows, b, :], ACT.Exp,
                                         bias=largest[rows, b:b + 1], accum_out=exp_sum[rows, b // 2:b // 2 + 1])

    with ExitStack() as own:
        sb1, ps1, sem1 = allocators(nc, own, "expert_top")
        rest = sb1("rest", [C, N])
        top = sb1("top", [C, 8])
        exp_inv = sb1("exp_inv", [C, PAIRS])
        chunk = sb1("chunk", [C, 2, CHUNK])
        by_token = sb1("by_token", [TILE, 2, 4, C])
        pooled = sb1("pooled", [C, PAIRS, 2 * C])
        own_half = sb1("own_half", [C, PAIRS, C])
        turned_ps = ps1("turned_ps", [TILE, 2, 4, C])
        pooled_ps = ps1("pooled_ps", [C, 2, BANK])
        pooled_t_ps = ps1("pooled_t_ps", [C, BANK])
        zeroed = sem1("zeroed")
        chain = sem1("chain")
        weights_done = sem1("weights_done")
        staged = sem1("staged")
        turned = sem1("turned")
        by_token_out = sem1("by_token_out")
        pooled_done = sem1("pooled_done")
        pooled_out = sem1("pooled_out")
        half_out = sem1("half_out")
        pooled_turned = sem1("pooled_turned")
        STEPS = PAIRS * CPI
        block = own.enter_context(nc.Block())

        @block.gpsimd
        def _(pool):
            nc.gpsimd.memset(pooled[:, :, :], 0.0).then_inc(zeroed, 1)

        @block.vector
        def _(dve):
            links = 0
            for m in range(PAIRS):
                w = weights[:, m, :]
                for op in (
                    lambda: nc.vector.max(top[:, :], w),
                    lambda: nc.vector.match_replace(rest[:, :], top[:, :], w, 0.0),
                    lambda: nc.vector.scalar_tensor_tensor(w, rest[:, :], -1.0, w, ALU.mult, ALU.add),
                    lambda: nc.vector.reciprocal(exp_inv[:, m:m + 1], exp_sum[:, m:m + 1]),
                ):
                    op().then_inc(chain, 1)
                    links += 1
                    dve.wait_ge(chain, links)
                nc.vector.tensor_scalar(w, w, exp_inv[:, m:m + 1], None, ALU.mult).then_inc(weights_done, 1)

            def copy_turned(i, u):
                dve.wait_ge(turned, i + 1)
                at_least(dve, pooled_done, i - 1)
                nc.vector.tensor_copy(by_token[:, u, :, :], turned_ps[:, u, :, :]).then_inc(by_token_out, 1)

            def add(i, u):
                dve.wait_ge(pooled_done, i + 1)
                at_least(dve, pooled_out, i)
                at = pooled[:, bass.ds(i // CPI, 1), :].rearrange("p a c -> p (a c)")
                nc.vector.tensor_tensor(at, at, pooled_ps[:, u, 0:2 * C], ALU.add).then_inc(pooled_out, 1)
            dve.wait_ge(zeroed, 1)
            pipelined(dve, STEPS, [(1, copy_turned), (2, add)])
            dve.wait_ge(pooled_out, STEPS)
            for h in range(2):
                rows = slice(h * E, h * E + E)
                nc.vector.tensor_copy(own_half[rows, :, :], pooled[rows, :, h * C:(h + 1) * C]).then_inc(half_out, 1)
            dve.wait_ge(pooled_turned, 1)
            nc.vector.tensor_copy(pooled_t[:, :, :].rearrange("p b e -> p (b e)"), pooled_t_ps[:, 0:B * E])

        @block.scalar
        def _(act):
            flat = weights[:, :, :].rearrange("p m n -> p (m n)")
            act.wait_ge(weights_done, PAIRS)

            def stage(i, u):
                at_least(act, turned, i - 1)
                nc.scalar.activation(chunk[:, u, :], flat[:, bass.ds(i * CHUNK, CHUNK)], ACT.Copy).then_inc(staged, 1)
            pipelined(act, STEPS, [(0, stage)])

        @block.tensor
        def _(pe):
            def turn(i, u):
                pe.wait_ge(staged, i + 1)
                at_least(pe, by_token_out, i - 1)
                for t in range(4):
                    mm = nc.tensor.transpose(turned_ps[:, u, t, :], chunk[:, u, t * TILE:(t + 1) * TILE], ident[:, :])
                mm.then_inc(turned, 1)

            def pool_tokens(i, u):
                pe.wait_ge(by_token_out, i + 1)
                at_least(pe, pooled_out, i - 1)
                for t in range(4):
                    tokens = z[:, bass.DynSlice(i * 4 + i // CPI * TPI + t, 2, step=TPI), :]
                    mm = nc.tensor.matmul(pooled_ps[:, u, 0:2 * C].rearrange("p (h c) -> p h c", h=2),
                                          by_token[:, u, t, :], tokens, start=(t == 0), stop=(t == 3))
                mm.then_inc(pooled_done, 1)
            pipelined(pe, STEPS, [(1, turn), (2, pool_tokens)])
            pe.wait_ge(half_out, 2)
            for m in range(PAIRS):
                mm = nc.tensor.transpose(pooled_t_ps[:, m * C:(m + 1) * C], own_half[:, m, :], ident[:, :])
            mm.then_inc(pooled_turned, 1)

    outputs_t = sb("outputs_t", [C, B, E])
    with ExitStack() as own:
        sb1, ps1, sem1 = allocators(nc, own, "expert_mlp")
        SLOTS = 2
        w1 = sb1("w1", [C, SLOTS, GROUP, HID])
        w2 = sb1("w2", [C, SLOTS, GROUP, KCH, C])
        tokens = sb1("tokens", [C, 2, GROUP, B])
        biased = sb1("biased", [C, 2, GROUP, KCH, B])
        hidden = sb1("hidden", [C, 2, GROUP, KCH, B])
        hidden_ps = ps1("hidden_ps", [C, 2, BANK])
        out_ps = ps1("out_ps", [C, 2, BANK])
        loaded = [sem1(f"loaded{u}") for u in range(2)]
        tokens_in = sem1("tokens_in")
        hidden_done = sem1("hidden_done")
        biased_done = sem1("biased_done")
        gelu_done = sem1("gelu_done")
        out_done = sem1("out_done")
        out_out = sem1("out_out")
        STEPS = E // GROUP
        block = own.enter_context(nc.Block())

        @block.sync
        def _(sp):
            def load(i, u):
                at_least(sp, hidden_done, i - 1)
                sp.dma_start(w1[:, u, :, :], io["weight1"][bass.ds(i * GROUP, GROUP), 0:C, :]
                             .rearrange("e d h -> d e h")).then_inc(loaded[u], 16)
                at_least(sp, out_done, i - 1)
                sp.dma_start(w2[:, u, :, :, :].rearrange("p e k o -> p e (k o)"),
                             io["weight2"][bass.ds(i * GROUP, GROUP), 0:HID, :]
                             .rearrange("e (p k) o -> p e (k o)", k=KCH)).then_inc(loaded[u], 16)
            pipelined(sp, STEPS, [(0, load)])

        @block.tensor
        def _(pe):
            def up(i, u):
                pe.wait_ge(loaded[u], 16 * (i - u) + 32)
                pe.wait_ge(tokens_in, i + 1)
                at_least(pe, biased_done, i - 1)
                out = hidden_ps[:, u, 0:GROUP * KCH * B].rearrange("p (e k b) -> p e k b", e=GROUP, k=KCH)
                for e in range(GROUP):
                    for k in range(KCH):
                        mm = nc.tensor.matmul(out[:, e, k, :], w1[:, u, e, k:HID:KCH], tokens[:, u, e, :],
                                              start=True, stop=True)
                mm.then_inc(hidden_done, 1)

            def down(i, u):
                pe.wait_ge(gelu_done, i + 1)
                at_least(pe, out_out, i - 1)
                out = out_ps[:, u, 0:GROUP * B].rearrange("p (e b) -> p e b", e=GROUP)
                for e in range(GROUP):
                    for k in range(KCH):
                        mm = nc.tensor.matmul(out[:, e, :], w2[:, u, e, k, :], hidden[:, u, e, k, :],
                                              start=(k == 0), stop=(k == KCH - 1))
                mm.then_inc(out_done, 1)
            pipelined(pe, STEPS, [(0, up), (1, down)])

        @block.scalar
        def _(act):
            by_expert = pooled_t[:, :, :].rearrange("p b e -> p e b")

            def take_tokens(i, u):
                at_least(act, hidden_done, i - 1)
                nc.scalar.activation(tokens[:, u, :, :], by_expert[:, bass.ds(i * GROUP, GROUP), :], ACT.Copy)\
                    .then_inc(tokens_in, 1)

            def gelu(i, u):
                act.wait_ge(biased_done, i + 1)
                at_least(act, out_done, i - 1)
                nc.scalar.activation(hidden[:, u, :, :, :].rearrange("p e k b -> p (e k b)"),
                                     biased[:, u, :, :, :].rearrange("p e k b -> p (e k b)"), ACT.Gelu)\
                    .then_inc(gelu_done, 1)
            pipelined(act, STEPS, [(0, take_tokens), (1, gelu)])

        @block.vector
        def _(dve):
            dve.wait_ge(biases, 32)

            def add_bias(i, u):
                dve.wait_ge(hidden_done, i + 1)
                at_least(dve, gelu_done, i - 1)
                nc.vector.tensor_tensor(biased[:, u, :, :, :].rearrange("p e k b -> p (e k) b"),
                                        hidden_ps[:, u, 0:GROUP * KCH * B].rearrange("p (n b) -> p n b", b=B),
                                        bias1[:, bass.ds(i * GROUP, GROUP), :].rearrange("p e k -> p (e k)")
                                        .unsqueeze(2).to_broadcast([C, GROUP * KCH, B]), ALU.add)\
                    .then_inc(biased_done, 1)

            def take_output(i, u):
                dve.wait_ge(out_done, i + 1)
                nc.vector.tensor_tensor(outputs_t[:, :, bass.ds(i * GROUP, GROUP)].rearrange("p b e -> p e b"),
                                        out_ps[:, u, 0:GROUP * B].rearrange("p (e b) -> p e b", e=GROUP),
                                        bias2[:, bass.ds(i * GROUP, GROUP)].unsqueeze(2)
                                        .to_broadcast([C, GROUP, B]), ALU.add).then_inc(out_out, 1)
            pipelined(dve, STEPS, [(0, add_bias), (1, take_output)])

    with ExitStack() as own:
        sb1, ps1, sem1 = allocators(nc, own, "expert_out")
        outputs = sb1("outputs", [C, PAIRS, 2, C])
        turned_ps = ps1("turned_ps", [C, BANK])
        back_ps = ps1("back_ps", [C, 2, BANK])
        zeroed = sem1("zeroed")
        turned = sem1("turned")
        outputs_out = sem1("outputs_out")
        back_done = sem1("back_done")
        added = sem1("added")
        block = own.enter_context(nc.Block())

        @block.gpsimd
        def _(pool):
            nc.gpsimd.memset(outputs[:, :, :, :], 0.0).then_inc(zeroed, 1)

        @block.tensor
        def _(pe):
            for m in range(PAIRS):
                mm = nc.tensor.transpose(turned_ps[:, m * C:(m + 1) * C],
                                         outputs_t[:, 2 * m:2 * m + 2, :].rearrange("p h e -> p (h e)"), ident[:, :])
            mm.then_inc(turned, 1)
            pe.wait_ge(outputs_out, 2)
            for m in range(PAIRS):
                def step(c, first):
                    for h in range(2):
                        n = (m * CPI + c) * 2 + h
                        if not first:
                            pe.wait_ge(added, n - 1)
                        nc.tensor.matmul(back_ps[:, h, 0:CHUNK], outputs[:, m, h, :],
                                         weights[:, m, bass.ds(c * CHUNK, CHUNK)], start=True, stop=True)\
                            .then_inc(back_done, 1)
                step(0, m == 0)
                with pe.Fori(1, CPI) as c:
                    step(c, False)

        @block.vector
        def _(dve):
            dve.wait_ge(zeroed, 1)
            dve.wait_ge(turned, 1)
            for h in range(2):
                rows = slice(h * E, h * E + E)
                nc.vector.tensor_copy(outputs[rows, :, h, :],
                                      turned_ps[rows, 0:PAIRS * C].rearrange("p (m c) -> p m c", m=PAIRS))\
                    .then_inc(outputs_out, 1)
            for m in range(PAIRS):
                with dve.Fori(0, CPI) as c:
                    for h in range(2):
                        dve.wait_ge(back_done, (m * CPI + c) * 2 + h + 1)
                        at = resid[:, bass.ds((2 * m + h) * N + c * CHUNK, CHUNK)]
                        nc.vector.tensor_tensor(at, at, back_ps[:, h, 0:CHUNK], ALU.add).then_inc(added, 1)


def self_attention(nc, ctx, resid, io, ident, mean_w, eps):
    SHIFT = -52.0
    sb, ps, sem = allocators(nc, ctx, "self")
    z_t = sb("z_t", [C, TOKENS])
    z = sb("z", [TILE, TILES, C])

    with ExitStack() as own:
        norm = Norm(nc, own, "self", resid, mean_w, eps)
        _, ps1, sem1 = allocators(nc, own, "self_in")
        turned_ps = ps1("turned_ps", [TILE, 2, 4, C])
        turned = sem1("turned")
        z_out = sem1("z_out")
        zt_out = sem1("zt_out")
        block = own.enter_context(nc.Block())

        @block.tensor
        def _(pe):
            def turn(i, u):
                pe.wait_ge(norm.normed_done, i + 1)
                at_least(pe, z_out, i - 1)
                for t in range(4):
                    mm = nc.tensor.transpose(turned_ps[:, u, t, :], norm.normed[:, u, t * TILE:(t + 1) * TILE],
                                             ident[:, :])
                mm.then_inc(turned, 1)
            norm.tensor_steps(pe, turn)

        @block.vector
        def _(dve):
            norm.vector_steps(dve, ((turned, 1), (zt_out, 1)), lambda i, u: None)

        @block.scalar
        def _(act):
            nc.scalar.preload_act_table_set("natural_log_exp_and_others")

            def copy_out(i, u):
                act.wait_ge(turned, i + 1)
                nc.scalar.activation(z[:, bass.ds(i * 4, 4), :], turned_ps[:, u, :, :], ACT.Copy).then_inc(z_out, 1)
            norm.scalar_steps(act, copy_out)

        @block.gpsimd
        def _(pool):
            def step(i, u, first, last):
                pool.wait_ge(norm.normed_done, i + 1)
                nc.gpsimd.tensor_copy(z_t[:, bass.ds(i * CHUNK, CHUNK)], norm.normed[:, u, :]).then_inc(zt_out, 1)
            paced(pool, CHUNKS, step)

    LOTS = ((0, 4), (4, 3))
    key_t = sb("key_t", [C, 2, TILE])
    key = sb("key", [TILE, 2, C])
    probs = sb("probs", [TILE, 2, 4, CHUNK])
    sums = sb("sums", [TILE, 2, 4])
    lot_sum = sb("lot_sum", [TILE, 2, TPI])
    total = sb("total", [TILE, TPI])
    inverse = sb("inverse", [TILE, TPI])
    diag = sb("diag", [TILE, 4, TILE])
    raw = sb("raw", [C, N])
    shift = sb("shift", [C, 1])
    ones = sb("ones", [TILE, C])
    zeros = sb("zeros", [TILE, CHUNK], BF16)
    score_ps = ps("score_ps", [C, 4, BANK])
    out_ps = ps("out_ps", [C, 4, BANK])
    constants = sem("constants")
    key_t_in = [sem(f"key_t_in{u}") for u in range(2)]
    key_in = [sem(f"key_in{u}") for u in range(2)]
    scores_done = sem("scores_done")
    exp_done = sem("exp_done")
    product_done = sem("product_done")
    lot_done = sem("lot_done")
    summed = sem("summed")
    raw_out = sem("raw_out")
    total_done = sem("total_done")
    inverse_done = sem("inverse_done")
    diag_done = sem("diag_done")
    spread_done = sem("spread_done")
    scaled = sem("scaled")
    added = sem("added")
    block = ctx.enter_context(nc.Block())

    def before(b, lot):
        return b * TPI * CPI + lot * TPI * LOTS[0][1]

    def tiles_in(b, lot, j, u):
        return (b * 2 + lot) * TPI * 8 + (j - u) * 8 + 16

    @block.gpsimd
    def _(pool):
        nc.gpsimd.memset(shift[:, :], SHIFT).then_inc(constants, 1)
        nc.gpsimd.memset(ones[:, :], 1.0).then_inc(constants, 1)
        nc.gpsimd.memset(zeros[:, :], 0.0).then_inc(constants, 1)

    @block.sync
    def _(sp):
        with sp.Fori(0, B) as b:
            for lot, (c0, n) in enumerate(LOTS):
                def step(j, u, first, last):
                    some = not (isinstance(j, int) and j < 2)
                    sp.wait_ge(scores_done, before(b, lot) + ((j - 1) * n if some else 0))
                    sp.dma_start(key_t[:, u, :], z_t[:, bass.ds(b * N + j * TILE, TILE)])\
                      .then_inc(key_t_in[u], 16)
                    sp.wait_ge(product_done, before(b, lot) + ((j - 1) * n if some else 0))
                    sp.dma_start(key[:, u, :], z[:, bass.ds(b * TPI + j, 1), :].rearrange("p a c -> p (a c)"))\
                      .then_inc(key_in[u], 16)
                paced(sp, TPI, step)

    @block.tensor
    def _(pe):
        pe.wait_ge(constants, 3)
        with pe.Fori(0, B) as b:
            for lot, (c0, n) in enumerate(LOTS):
                def scores(j, u, c):
                    pe.wait_ge(key_t_in[u], tiles_in(b, lot, j, u))
                    if isinstance(j, int) and j == 0:
                        pe.wait_ge(exp_done, before(b, lot))
                    else:
                        pe.wait_ge(exp_done, before(b, lot) + (j - 1) * n + c + 1)
                    nc.tensor.matmul(score_ps[0:TILE, c, 0:CHUNK], key_t[:, u, :],
                                     z_t[:, bass.ds(b * N + (c0 + c) * CHUNK, CHUNK)],
                                     start=True, stop=True).then_inc(scores_done, 1)

                def product(j, u, c):
                    pe.wait_ge(key_in[u], tiles_in(b, lot, j, u))
                    pe.wait_ge(exp_done, before(b, lot) + j * n + c + 1)
                    nc.tensor.matmul(out_ps[:, c, 0:CHUNK], key[:, u, :], probs[:, u, c, :],
                                     start=False, stop=False).then_inc(product_done, 1)

                def step(j, u, first, last):
                    if first:
                        if lot == 0:
                            pe.wait_ge(scaled, b * CPI)
                        for c in range(n):
                            scores(j, u, c)
                        pe.wait_ge(raw_out, b * 2 + lot)
                        for c in range(n):
                            nc.tensor.matmul(out_ps[:, c, 0:CHUNK], zeros[:, 0:C], zeros[:, :], start=True, stop=False)
                    for c in range(n):
                        if not last:
                            scores(j + 1, 1 - u, c)
                        product(j, u, c)
                    if last:
                        for c in range(n):
                            mm = nc.tensor.matmul(out_ps[:, c, 0:CHUNK], zeros[:, 0:C], zeros[:, :],
                                                  start=False, stop=True)
                        mm.then_inc(lot_done, 1)
                paced(pe, TPI, step)
            pe.wait_ge(exp_done, before(b, 0) + TPI * CPI)
            for c in range(CPI):
                pe.wait_ge(diag_done, b * CPI + c + 1)
                pe.wait_ge(scaled, b * CPI + max(c - 3, 0))
                nc.tensor.matmul(score_ps[:, c % 4, 0:CHUNK], ones[:, :], diag[:, :, :]
                                 .rearrange("p t n -> p (t n)"), start=True, stop=True).then_inc(spread_done, 1)

    @block.scalar
    def _(act):
        act.wait_ge(constants, 3)
        with act.Fori(0, B) as b:
            for lot, (c0, n) in enumerate(LOTS):
                def step(j, u, first, last):
                    for c in range(n):
                        act.wait_ge(scores_done, before(b, lot) + j * n + c + 1)
                        if isinstance(j, int) and j < 2:
                            if c == 0:
                                act.wait_ge(product_done, before(b, lot))
                                act.wait_ge(summed, (b * 2 + lot) * TPI)
                        else:
                            act.wait_ge(product_done, before(b, lot) + (j - 2) * n + c + 1)
                            if c == 0:
                                act.wait_ge(summed, (b * 2 + lot) * TPI + j - 1)
                        nc.scalar.activation(probs[:, u, c, :], score_ps[0:TILE, c, 0:CHUNK], ACT.Exp,
                                             bias=shift[0:TILE, 0:1],
                                             accum_out=sums[:, u, c:c + 1]).then_inc(exp_done, 1)
                paced(act, TPI, step)

    @block.vector
    def _(dve):
        with dve.Fori(0, B) as b:
            for lot, (c0, n) in enumerate(LOTS):
                def step(j, u, first, last):
                    dve.wait_ge(exp_done, before(b, lot) + (j + 1) * n)
                    if first:
                        dve.wait_ge(total_done, b)
                    nc.vector.tensor_reduce(lot_sum[:, lot, bass.ds(j, 1)], sums[:, u, 0:n], AX, ALU.add)\
                        .then_inc(summed, 1)
                paced(dve, TPI, step)
                dve.wait_ge(lot_done, b * 2 + lot + 1)
                if lot == 0:
                    dve.wait_ge(added, b * CPI)
                nc.vector.tensor_copy(raw[:, c0 * CHUNK:(c0 + n) * CHUNK].rearrange("p (c n) -> p c n", c=n),
                                      out_ps[:, 0:n, 0:CHUNK]).then_inc(raw_out, 1)
            dve.wait_ge(summed, (b + 1) * 2 * TPI)
            nc.vector.tensor_tensor(total[:, :], lot_sum[:, 0, :], lot_sum[:, 1, :], ALU.add).then_inc(total_done, 1)
            dve.wait_ge(total_done, b + 1)
            dve.wait_ge(diag_done, b * CPI)
            nc.vector.reciprocal(inverse[:, :], total[:, :]).then_inc(inverse_done, 1)
            dve.wait_ge(inverse_done, b + 1)

            def finish(c):
                dve.wait_ge(spread_done, b * CPI + c + 1)
                part = raw[:, c * CHUNK:(c + 1) * CHUNK]
                at = resid[:, bass.ds(b * N + c * CHUNK, CHUNK)]
                nc.vector.tensor_tensor(part, part, score_ps[:, c % 4, 0:CHUNK], ALU.mult).then_inc(scaled, 1)
                dve.wait_ge(scaled, b * CPI + c + 1)
                nc.vector.tensor_tensor(at, at, part, ALU.add).then_inc(added, 1)

            dve.wait_ge(raw_out, (b + 1) * 2)
            for c in range(CPI):
                dve.wait_ge(spread_done, b * CPI + c)
                nc.vector.tensor_tensor(diag[:, :, :],
                                        ident[0:TILE, 0:TILE].unsqueeze(1).to_broadcast([TILE, 4, TILE]),
                                        inverse[:, 4 * c:4 * c + 4].unsqueeze(2).to_broadcast([TILE, 4, TILE]),
                                        ALU.mult).then_inc(diag_done, 1)
                if c:
                    finish(c - 1)
            finish(CPI - 1)


def recurrence(nc, ctx, resid, io, ident, mean_w, eps):
    SPAN = 64
    SPANS = N // SPAN
    COLS = TOKENS // SPAN
    WARM = 16
    SLACK = 2.0 ** -22
    sb, ps, sem = allocators(nc, ctx, "rnn")
    pre = sb("pre", [C, WARM + TOKENS])
    w = sb("w", [C, C])
    v = sb("v", [C, C])
    gamma = sb("gamma", [C, 1])
    beta = sb("beta", [C, 1])
    stats = sb("stats", [C, CHUNKS, 6])
    moments = sb("moments", [C, 2])
    factor = sb("factor", [C, 1])
    offset = sb("offset", [C, 1])
    loaded = sem("loaded")

    with ExitStack() as own:
        norm = Norm(nc, own, "rnn", resid, mean_w, eps)
        _, ps1, sem1 = allocators(nc, own, "rnn_in")
        wx_ps = ps1("wx_ps", [C, 2, BANK])
        wx_done = sem1("wx_done")
        pre_out = sem1("pre_out")
        stats_done = sem1("stats_done")
        chain = sem1("chain")
        log_done = sem1("log_done")
        block = own.enter_context(nc.Block())

        @block.sync
        def _(sp):
            for to, name in ((w, "rnn_w"), (v, "rnn_v"), (gamma, "rnn_gamma"), (beta, "rnn_beta")):
                sp.dma_start(to[:, :], io[name]).then_inc(loaded, 16)

        @block.gpsimd
        def _(pool):
            nc.gpsimd.memset(pre[:, 0:WARM], 0.0)

        @block.tensor
        def _(pe):
            pe.wait_ge(loaded, 64)

            def project(i, u):
                pe.wait_ge(norm.normed_done, i + 1)
                at_least(pe, pre_out, i - 1)
                nc.tensor.matmul(wx_ps[:, u, 0:CHUNK], w[:, :], norm.normed[:, u, :],
                                 start=True, stop=True).then_inc(wx_done, 1)
            norm.tensor_steps(pe, project)

        @block.scalar
        def _(act):
            nc.scalar.preload_act_table_set("natural_log_exp_and_others")

            def copy_out(i, u):
                act.wait_ge(wx_done, i + 1)
                nc.scalar.activation(pre[:, bass.ds(WARM + i * CHUNK, CHUNK)], wx_ps[:, u, 0:CHUNK], ACT.Copy)\
                    .then_inc(pre_out, 1)
            norm.scalar_steps(act, copy_out)
            act.wait_ge(chain, 1)
            nc.scalar.activation(factor[:, :], moments[:, 1:2], ACT.Ln, bias=eps[:, 0:1]).then_inc(log_done, 1)
            act.wait_ge(log_done, 1)
            nc.scalar.activation(factor[:, :], factor[:, :], ACT.Exp, scale=-0.5).then_inc(log_done, 1)

        @block.vector
        def _(dve):
            def statistics(i, u):
                dve.wait_ge(pre_out, i + 1)
                nc.vector.bn_stats(stats[:, bass.ds(i, 1), :].rearrange("p a s -> p (a s)"),
                                   pre[:, bass.ds(WARM + i * CHUNK, CHUNK)]).then_inc(stats_done, 1)
            norm.vector_steps(dve, ((wx_done, 1),), statistics)
            dve.wait_ge(stats_done, CHUNKS)
            nc.vector.bn_aggr(moments[:, :], stats[:, :, :].rearrange("p a s -> p (a s)")).then_inc(chain, 1)
            dve.wait_ge(log_done, 2)
            dve.wait_ge(loaded, 64)
            nc.vector.tensor_tensor(factor[:, :], factor[:, :], gamma[:, :], ALU.mult).then_inc(chain, 1)
            dve.wait_ge(chain, 2)
            nc.vector.tensor_tensor(offset[:, :], moments[:, 0:1], factor[:, :], ALU.mult).then_inc(chain, 1)
            dve.wait_ge(chain, 3)
            nc.vector.tensor_tensor(offset[:, :], beta[:, :], offset[:, :], ALU.subtract).then_inc(chain, 1)
            dve.wait_ge(chain, 4)
            dve.wait_ge(pre_out, CHUNKS)
            nc.vector.tensor_scalar(pre[:, WARM:WARM + TOKENS], pre[:, WARM:WARM + TOKENS],
                                    factor[:, 0:1], offset[:, 0:1], ALU.mult, ALU.add)

    states = sb("states", [C, TOKENS])
    warm = sb("warm", [C, 2, COLS])
    start = sb("start", [C, COLS])
    ends = sb("ends", [C, COLS])
    apart = sb("apart", [C, COLS])
    apart_max = sb("apart_max", [C, 1])
    differs = sb("differs", [C, 1])
    ones = sb("ones", [C, 1])
    count = sb("count", [1, 1], mybir.dt.int32)
    HALVES = 2
    HALF = COLS // HALVES
    step_ps = ps("step_ps", [C, 2, HALVES, BANK])
    count_ps = ps("count_ps", [C, BANK])

    def inputs_at(t, h):
        return pre[:, bass.DynSlice(t + WARM + h * HALF * SPAN, HALF, step=SPAN)]

    def states_at(t, h):
        return states[:, bass.DynSlice(t + h * HALF * SPAN, HALF, step=SPAN)]

    def product(pe, sems, q, t, u, h, before, first):
        product_done, state_done = sems
        if not first:
            at_least(pe, state_done[h], q - 1)
        nc.tensor.matmul(step_ps[:, u, h, 0:HALF], ident[:, :], inputs_at(t, h), start=True, stop=False)
        at_least(pe, state_done[h], q)
        nc.tensor.matmul(step_ps[:, u, h, 0:HALF], v[:, :], before, start=False, stop=True)\
            .then_inc(product_done[h], 1)

    def sigmoid(act, sems, q, u, h, to):
        product_done, state_done = sems
        act.wait_ge(product_done[h], q + 1)
        nc.scalar.activation(to, step_ps[:, u, h, 0:HALF], ACT.Sigmoid).then_inc(state_done[h], 1)

    def half(x, h):
        return x[:, h * HALF:(h + 1) * HALF]

    def tensor_spans(pe, sems, base):
        def step(s, u, first, last):
            for h in range(HALVES):
                before = half(start, h) if first else states_at(s - 1, h)
                product(pe, sems, base + s, s, u, h, before, first)
        paced(pe, SPAN, step)

    def scalar_spans(act, sems, base):
        def step(s, u, first, last):
            for h in range(HALVES):
                sigmoid(act, sems, base + s, u, h, states_at(s, h))
        paced(act, SPAN, step)

    def without_first(dve, x, sem, count):
        dve.wait_ge(sem, count)
        return nc.vector.memset(x[:, bass.DynSlice(0, B, step=SPANS)], 0.0)

    sides = lambda n: ([sem(f"product_{n}{h}") for h in range(HALVES)], [sem(f"state_{n}{h}") for h in range(HALVES)])
    spans, again = sides("first"), sides("again")
    constants = sem("constants")
    warmed = sem("warmed")
    started = sem("started")
    compared = sem("compared")
    ends_out = sem("ends_out")
    count_done = sem("count_done")
    count_out = sem("count_out")
    restarted = sem("restarted")
    reloaded = sem("reloaded")
    added = sem("added")
    block = ctx.enter_context(nc.Block())

    @block.gpsimd
    def _(pool):
        nc.gpsimd.memset(warm[:, :, :], 0.0).then_inc(constants, 1)
        nc.gpsimd.memset(ones[:, :], 1.0).then_inc(constants, 1)

    @block.tensor
    def _(pe):
        pe.wait_ge(constants, 2)

        def warm_up(q, u, first, last):
            for h in range(HALVES):
                product(pe, spans, q, q - WARM, u, h, half(warm[:, 1 - u, :], h), first)
        paced(pe, WARM, warm_up)
        pe.wait_ge(started, 2)
        tensor_spans(pe, spans, WARM)
        pe.wait_ge(compared, 4)
        nc.tensor.matmul(count_ps[0:1, 0:1], differs[:, :], ones[:, :], start=True, stop=True).then_inc(count_done, 1)
        pe.wait_ge(count_out, 1)
        wrong = pe.value_load(count[0:1, 0:1])
        with pe.If(wrong):
            with pe.Fori(0, SPANS - 1) as r:
                pe.wait_ge(restarted, r + 1)
                tensor_spans(pe, again, r * SPAN)

    @block.scalar
    def _(act):
        act.wait_ge(constants, 2)

        def warm_up(q, u, first, last):
            for h in range(HALVES):
                sigmoid(act, spans, q, u, h, half(warm[:, u, :], h))
        paced(act, WARM, warm_up)
        scalar_spans(act, spans, WARM)
        act.wait_ge(count_out, 1)
        wrong = act.value_load(count[0:1, 0:1])
        with act.If(wrong):
            with act.Fori(0, SPANS - 1) as r:
                scalar_spans(act, again, r * SPAN)

    @block.vector
    def _(dve):
        for h in range(HALVES):
            dve.wait_ge(spans[1][h], WARM)
        nc.vector.tensor_copy(start[:, :], warm[:, (WARM - 1) % 2, :]).then_inc(started, 1)
        without_first(dve, start, started, 1).then_inc(started, 1)
        for h in range(HALVES):
            dve.wait_ge(spans[1][h], WARM + SPAN)
        span_ends = states[:, bass.DynSlice(SPAN - 1, COLS - 1, step=SPAN)]
        nc.vector.tensor_copy(ends[:, 1:COLS], span_ends).then_inc(ends_out, 1)
        without_first(dve, ends, ends_out, 1).then_inc(ends_out, 1)
        dve.wait_ge(ends_out, 2)
        nc.vector.tensor_tensor(apart[:, :], ends[:, :], start[:, :], ALU.subtract).then_inc(compared, 1)
        dve.wait_ge(compared, 1)
        nc.vector.tensor_tensor(apart[:, :], apart[:, :], apart[:, :], ALU.mult).then_inc(compared, 1)
        dve.wait_ge(compared, 2)
        nc.vector.tensor_reduce(apart_max[:, :], apart[:, :], AX, ALU.max).then_inc(compared, 1)
        dve.wait_ge(compared, 3)
        nc.vector.tensor_scalar(differs[:, :], apart_max[:, :], SLACK * SLACK, None, ALU.is_gt).then_inc(compared, 1)
        dve.wait_ge(count_done, 1)
        nc.vector.tensor_copy(count[:, :], count_ps[0:1, 0:1]).then_inc(count_out, 1)
        dve.wait_ge(count_out, 1)
        wrong = dve.value_load(count[0:1, 0:1])
        with dve.If(wrong):
            with dve.Fori(0, SPANS - 1) as r:
                for h in range(HALVES):
                    dve.wait_ge(again[1][h], r * SPAN)
                nc.vector.tensor_copy(start[:, 1:COLS], span_ends).then_inc(reloaded, 1)
                without_first(dve, start, reloaded, r + 1).then_inc(restarted, 1)
            for h in range(HALVES):
                dve.wait_ge(again[1][h], (SPANS - 1) * SPAN)
        nc.vector.tensor_tensor(resid[:, :], resid[:, :], states[:, :], ALU.add).then_inc(added, 1)


def program(nc, io, out):
    with ExitStack() as ctx:
        sb = lambda n, s: ctx.enter_context(nc.sbuf_tensor(n, s, FP32))
        resid = sb("resid", [C, TOKENS])
        ident = sb("ident", [C, C])
        mean_w = sb("mean_w", [C, C])
        eps = sb("eps", [C, 1])
        with ExitStack() as own:
            loaded = own.enter_context(nc.semaphore("loaded"))
            constants = own.enter_context(nc.semaphore("constants"))
            block = own.enter_context(nc.Block())

            @block.sync
            def _(sp):
                sp.dma_start(ident[:, :], io["ident"]).then_inc(loaded, 16)
                for b in range(B):
                    sp.dma_start(resid[:, b * N:(b + 1) * N], io["x"][:, b * N:(b + 1) * N]).then_inc(loaded, 16)
                sp.wait_ge(loaded, 16 * (B + 1))

            @block.gpsimd
            def _(pool):
                nc.gpsimd.memset(mean_w[:, :], 1.0 / C).then_inc(constants, 1)
                nc.gpsimd.memset(eps[:, :], 1e-5).then_inc(constants, 1)

        with ExitStack() as own:
            windowed_attention(nc, own, resid, io, ident, mean_w, eps)
        with ExitStack() as own:
            channel_attention(nc, own, resid, io)
        for stage in (sparse_attention, expert_choice, self_attention, recurrence):
            with ExitStack() as own:
                stage(nc, own, resid, io, ident, mean_w, eps)

        with ExitStack() as own:
            stored = own.enter_context(nc.semaphore("stored"))
            block = own.enter_context(nc.Block())

            @block.sync
            def _(sp):
                for b in range(B):
                    sp.dma_start(out[:, b * N:(b + 1) * N], resid[:, b * N:(b + 1) * N]).then_inc(stored, 16)
                sp.wait_ge(stored, 16 * B)


def kernel(**inputs):
    import numpy as _np
    import concourse.bacc as _bacc
    from concourse.bass_utils import run_bass_kernel_spmd as _run

    a = {k: _np.asarray(v) for k, v in inputs.items()}
    lay = _np.ascontiguousarray
    experts, hidden = a["L2_ffn_weight1"].shape[0], a["L2_ffn_weight1"].shape[2]
    arrays = {
        "x": lay(a["x"].reshape(TOKENS, C).T),
        "qkv_w": lay(a["L0_conv_qkv_w"].T),
        "qkv_b": lay(a["L0_conv_qkv_b"].reshape(3, C).T),
        "qkv_b_row": lay(a["L0_conv_qkv_b"].reshape(1, 3 * C)),
        "rpb": lay(a["L0_conv_rpb"]),
        "proj_w": lay(a["L0_conv_proj_w"].T),
        "proj_b": lay(a["L0_conv_proj_b"].reshape(C, 1)),
        "kernel_f": lay(a["L1_conv_kernel_f"].reshape(C, 16)),
        "kernel_g": lay(a["L1_conv_kernel_g"].reshape(C, 16)),
        "kernel_h": lay(a["L1_conv_kernel_h"].reshape(C, C)),
        "gamma": lay(_np.broadcast_to(a["L1_conv_gamma"].reshape(1, 1), (C, 1))),
        "Wq": lay(a["L2_attn_Wq"]),
        "Wk": lay(a["L2_attn_Wk"]),
        "Wv": lay(a["L2_attn_Wv"]),
        "Wo": lay(a["L2_attn_Wo"]),
        "Ws": lay(a["L2_attn_Ws"]),
        "bq": lay(a["L2_attn_bq"].reshape(C, 1)),
        "bk": lay(a["L2_attn_bk"].reshape(C, 1)),
        "bv": lay(a["L2_attn_bv"].reshape(1, C)),
        "bo": lay(a["L2_attn_bo"].reshape(C, 1)),
        "bs": lay(a["L2_attn_bs"].reshape(1, 1)),
        "gate_w": lay(a["L2_ffn_gate_w"].T),
        "gate_b": lay(a["L2_ffn_gate_b"].reshape(experts, 1)),
        "weight1": lay(a["L2_ffn_weight1"]),
        "weight2": lay(a["L2_ffn_weight2"]),
        "bias1": lay(a["L2_ffn_weight1"][:, C, :].reshape(experts, C, hidden // C).transpose(1, 0, 2)),
        "bias2": lay(a["L2_ffn_weight2"][:, hidden, :].T),
        "rnn_w": lay(a["L3_ffn_W"].T),
        "rnn_v": lay(a["L3_ffn_V"].T),
        "rnn_gamma": lay(a["L3_ffn_gamma"].reshape(C, 1)),
        "rnn_beta": lay(a["L3_ffn_beta"].reshape(C, 1)),
        "ident": _np.eye(C, dtype=_np.float32),
    }
    arrays.update(shape_constants())
    nc = _bacc.Bacc("TRN2", target_bir_lowering=False, num_devices=1)
    io = {k: nc.dram_tensor(f"in_{k}", v.shape, mybir.dt.from_np(v.dtype), kind="ExternalInput").ap()
          for k, v in arrays.items()}
    out = nc.dram_tensor("out", (C, TOKENS), FP32, kind="ExternalOutput").ap()
    program(nc, io, out)
    r = _run(nc, [{f"in_{k}": v for k, v in arrays.items()}], core_ids=[0])
    return lay(_np.asarray(r.results[0]["out"]).T).reshape(B, H, W, C)
```

```python
import concourse.bass as bass
import concourse.mybir as mybir
import numpy as np
from contextlib import ExitStack

FP32 = mybir.dt.float32
FP32R = mybir.dt.float32r
BF16 = mybir.dt.bfloat16
ALU = mybir.AluOpType
ACT = mybir.ActivationFunctionType
AX = mybir.AxisListType.X

B, H, W, C = 4, 56, 56, 128
N = H * W
TOKENS = B * N
TILE = 112
CHUNK = 4 * TILE
TILES = TOKENS // TILE
CHUNKS = TOKENS // CHUNK
CPI = N // CHUNK
TPI = N // TILE
BANK = 512
NEG = -1e30


def at_least(eng, sem, value):
    if not isinstance(value, int) or value > 0:
        eng.wait_ge(sem, value)


def paced(eng, count, step):
    step(0, 0, True, False)
    step(1, 1, False, False)
    with eng.Fori(1, count // 2 - 1) as j:
        step(2 * j, 0, False, False)
        step(2 * j + 1, 1, False, False)
    step(count - 2, 0, False, False)
    step(count - 1, 1, False, True)


def pipelined(eng, count, ops, slots=2):
    deepest = max(lag for lag, _ in ops)
    head = -(-(deepest + 1) // slots) * slots

    def step(s, slot, lo, hi):
        for lag, op in ops:
            if lo is None or lo <= s - lag < hi:
                op(s - lag, (slot - lag) % slots)
    for s in range(head):
        step(s, s % slots, 0, count)
    with eng.Fori(head // slots, count // slots) as j:
        for k in range(slots):
            step(j * slots + k, k, None, None)
    for s in range(count, count + deepest):
        step(s, s % slots, 0, count)


def allocators(nc, ctx, stage):
    def sb(name, shape, dtype=FP32):
        return ctx.enter_context(nc.sbuf_tensor(f"{stage}_{name}", shape, dtype))

    def ps(name, shape, dtype=FP32):
        return ctx.enter_context(nc.psum_tensor(f"{stage}_{name}", shape, dtype))

    taken = []

    def sem(name):
        taken.append(nc.alloc_semaphore(f"{stage}_{name}"))
        return taken[-1]

    def give_back():
        nc.clear_and_free_semaphores(taken)
        nc.all_engine_barrier()
    ctx.callback(give_back)
    return sb, ps, sem


class Norm:
    SLOTS = 4

    def __init__(self, nc, ctx, stage, resid, mean_w, eps):
        sb, ps, sem = allocators(nc, ctx, stage + "_ln")
        self.nc, self.resid, self.mean_w, self.eps = nc, resid, mean_w, eps
        self.centred = sb("centred", [C, self.SLOTS, CHUNK])
        self.squared = sb("squared", [C, 2, CHUNK])
        self.inverse = sb("inverse", [C, 2, CHUNK])
        self.normed = sb("normed", [C, 2, CHUNK])
        self.mean_ps = ps("mean_ps", [C, BANK])
        self.var_ps = ps("var_ps", [C, BANK])
        self.mean_done = sem("mean_done")
        self.centred_done = sem("centred_done")
        self.squared_done = sem("squared_done")
        self.var_done = sem("var_done")
        self.log_done = sem("log_done")
        self.inverse_done = sem("inverse_done")
        self.normed_done = sem("normed_done")

    def pe_mean(self, pe, i, u):
        at_least(pe, self.centred_done, i)
        self.nc.tensor.matmul(self.mean_ps[:, 0:CHUNK], self.mean_w[:, :],
                              self.resid[:, bass.ds(i * CHUNK, CHUNK)],
                              start=True, stop=True).then_inc(self.mean_done, 1)

    def pe_var(self, pe, i, u):
        pe.wait_ge(self.squared_done, i + 1)
        at_least(pe, self.log_done, i)
        self.nc.tensor.matmul(self.var_ps[:, 0:CHUNK], self.mean_w[:, :], self.squared[:, u % 2, :],
                              start=True, stop=True).then_inc(self.var_done, 1)

    def dve_centre(self, dve, i, u):
        dve.wait_ge(self.mean_done, i + 1)
        at_least(dve, self.normed_done, i - self.SLOTS + 1)
        self.nc.vector.tensor_tensor(self.centred[:, u, :], self.resid[:, bass.ds(i * CHUNK, CHUNK)],
                                     self.mean_ps[:, 0:CHUNK], ALU.subtract).then_inc(self.centred_done, 1)

    def act_square(self, act, i, u):
        act.wait_ge(self.centred_done, i + 1)
        at_least(act, self.var_done, i - 1)
        self.nc.scalar.activation(self.squared[:, u % 2, :], self.centred[:, u, :],
                                  ACT.Square).then_inc(self.squared_done, 1)

    def act_inverse(self, act, i, u):
        act.wait_ge(self.var_done, i + 1)
        at_least(act, self.normed_done, i - 1)
        self.nc.scalar.activation(self.inverse[:, u % 2, :], self.var_ps[:, 0:CHUNK], ACT.Ln,
                                  bias=self.eps[:, 0:1]).then_inc(self.log_done, 1)
        act.wait_ge(self.log_done, i + 1)
        self.nc.scalar.activation(self.inverse[:, u % 2, :], self.inverse[:, u % 2, :], ACT.Exp,
                                  scale=-0.5).then_inc(self.inverse_done, 1)

    def dve_normalise(self, dve, i, u, used):
        dve.wait_ge(self.inverse_done, i + 1)
        for sem, per_chunk in used:
            at_least(dve, sem, (i - 1) * per_chunk)
        self.nc.vector.tensor_tensor(self.normed[:, u % 2, :], self.centred[:, u, :], self.inverse[:, u % 2, :],
                                     ALU.mult).then_inc(self.normed_done, 1)

    def tensor_steps(self, pe, project):
        pipelined(pe, CHUNKS, [(0, lambda i, u: self.pe_mean(pe, i, u)), (5, lambda i, u: project(i, u % 2)),
                               (2, lambda i, u: self.pe_var(pe, i, u))], self.SLOTS)

    def vector_steps(self, dve, used, copy_out, lag=6, more=None):
        pipelined(dve, CHUNKS, [(4, lambda i, u: self.dve_normalise(dve, i, u, used)),
                                (0, lambda i, u: self.dve_centre(dve, i, u)),
                                (5, (lambda i, u: more(i, u % 2)) if more else lambda i, u: None),
                                (lag, lambda i, u: copy_out(i, u % 2))], self.SLOTS)

    def scalar_steps(self, act, copy_out):
        pipelined(act, CHUNKS, [(6, lambda i, u: copy_out(i, u % 2)), (1, lambda i, u: self.act_square(act, i, u)),
                                (3, lambda i, u: self.act_inverse(act, i, u))], self.SLOTS)


def shape_constants():
    span = np.arange(TILES)
    query, key = np.arange(TILE)[:, None], np.arange(C + TILE)[None, :]
    return {
        "not_first": (span % TPI != 0).astype(np.float32)[:, None],
        "group_mean": np.kron(np.eye(C // 4), np.full((4, 4), 0.25)).astype(np.float32),
        "head_rows": np.kron(np.eye(4), np.ones((C // 4, 1))).astype(np.float32),
        "image_sum": (span[:, None] % TPI == np.arange(TPI)[None, :]).astype(np.float32),
        "band": np.where((key >= query) & (key <= query + C), 0.0, NEG).astype(np.float32),
    }


def windowed_attention(nc, ctx, resid, io, ident, mean_w, eps):
    HEADS, D, KSIZE = 4, C // 4, 7
    PAD = KSIZE // 2
    SCALE = float(D) ** -0.5
    TW = 14
    TH = TILE // TW
    ACROSS = W // TW
    KW, KH = TW + 2 * PAD, TH + 2 * PAD
    KEYS = KW * KH
    LOTS, LOT_ROWS = 3, 5
    LOT = LOT_ROWS * KW
    PW = W + 2 * PAD
    PIXELS = (H + 2 * PAD) * PW
    RUNON = 2 * PW
    sb, ps, sem = allocators(nc, ctx, "window")
    k_t = sb("k_t", [C, B * PIXELS + RUNON])
    q_dram = nc.dram_tensor("window_q", [TILES, C, TILE], FP32).ap()
    v_dram = nc.dram_tensor("window_v", [B * PIXELS + RUNON, C], FP32).ap()
    BIAS_ROW = TW * KEYS + KW
    BIAS_HEAD = TH * BIAS_ROW
    bias_dram = nc.dram_tensor("window_bias_table", [HEADS * BIAS_HEAD], FP32).ap()
    proj_w = sb("proj_w", [C, C])
    proj_b = sb("proj_b", [C, 1])
    factor = sb("factor", [C, B])
    offset = sb("offset", [C, B])
    proj_in = sem("proj_in")

    def padded_pixel(chunk):
        return chunk // CPI * PIXELS + chunk % CPI * (CHUNK // W * PW) + PAD * PW + PAD

    with ExitStack() as own:
        sb1, ps1, sem1 = allocators(nc, own, "window_norm")
        group_mean = sb1("group_mean", [C, C])
        stats = sb1("stats", [C, CHUNKS, 6])
        moments = sb1("moments", [C, B, 2])
        apart = sb1("apart", [C, B])
        spread = sb1("spread", [C, B])
        negs = sb1("negs", [C, HEADS * BIAS_HEAD // C])
        mean_ps = ps1("mean_ps", [C, BANK])
        var_ps = ps1("var_ps", [C, BANK])
        x_in = [sem1(f"x_in{b}") for b in range(B)]
        weights = sem1("weights")
        negs_done = sem1("negs_done")
        bias_cleared = sem1("bias_cleared")
        bias_stored = sem1("bias_stored")
        borders = sem1("borders")
        zeroed = sem1("zeroed")
        stats_done = sem1("stats_done")
        moments_done = sem1("moments_done")
        means_done = sem1("means_done")
        chain = sem1("chain")
        var_done = sem1("var_done")
        log_done = sem1("log_done")
        zeros = sb1("zeros", [61, 2 * PAD * C])
        block = own.enter_context(nc.Block())

        @block.gpsimd
        def _(pool):
            nc.gpsimd.memset(negs[:, :], NEG).then_inc(negs_done, 1)
            nc.gpsimd.memset(zeros[:, :], 0.0).then_inc(zeroed, 1)
            nc.gpsimd.memset(k_t[:, :], 0.0)

        @block.sync
        def _(sp):
            for b in range(B):
                sp.dma_start(resid[:, b * N:(b + 1) * N], io["x"][:, b * N:(b + 1) * N]).then_inc(x_in[b], 16)
            sp.dma_start(group_mean[:, :], io["group_mean"]).then_inc(weights, 16)
            sp.wait_ge(negs_done, 1)
            sp.dma_start(bias_dram.rearrange("(p n) -> p n", p=C), negs[:, :]).then_inc(bias_cleared, 16)
            sp.wait_ge(zeroed, 1)
            edge = PAD * PW - PAD
            for b in range(B):
                top, side, low = b * PIXELS, b * PIXELS + edge, (b + 1) * PIXELS - edge
                for start in (top, low):
                    sp.dma_start(v_dram[start:start + edge, :].rearrange("(p a) c -> p (a c)", a=PAD),
                                 zeros[0:edge // PAD, 0:PAD * C]).then_inc(borders, 16)
                rows = v_dram[side:side + (H + 1) * PW, :].rearrange("(r w) c -> r w c", w=PW)
                sp.dma_start(rows[:, 0:2 * PAD, :].rearrange("r w c -> r (w c)"), zeros[0:H + 1, :])\
                  .then_inc(borders, 16)
            end = B * PIXELS
            sp.dma_start(v_dram[end:end + RUNON, :].rearrange("(p a) c -> p (a c)", a=4),
                         zeros[0:RUNON // 4, 0:4 * C]).then_inc(borders, 16)
            sp.dma_start(proj_w[:, :], io["proj_w"]).then_inc(proj_in, 16)
            sp.dma_start(proj_b[:, :], io["proj_b"]).then_inc(proj_in, 16)
            sp.wait_ge(bias_cleared, 16)
            for h in range(HEADS):
                own_bias = io["rpb"][h, PAD:PAD + KSIZE, PAD:PAD + KSIZE].unsqueeze(0)
                for r in range(TH):
                    start = h * BIAS_HEAD + r * BIAS_ROW
                    to = bias_dram[start:start + TW * (KEYS + 1)].rearrange("(q s) -> q s", s=KEYS + 1)
                    to = to[:, 0:KSIZE * KW].rearrange("q (a b) -> q a b", b=KW)[:, :, 0:KSIZE]
                    sp.dma_start(to, own_bias.to_broadcast([TW, KSIZE, KSIZE])).then_inc(bias_stored, 16)
            sp.wait_ge(borders, (3 * B + 1) * 16)
            sp.wait_ge(bias_stored, HEADS * TH * 16)

        @block.vector
        def _(dve):
            for b in range(B):
                dve.wait_ge(x_in[b], 16)
                with dve.Fori(b * CPI, (b + 1) * CPI) as i:
                    nc.vector.bn_stats(stats[:, bass.ds(i, 1), :].rearrange("p a s -> p (a s)"),
                                       resid[:, bass.ds(i * CHUNK, CHUNK)]).then_inc(stats_done, 1)
            dve.wait_ge(stats_done, CHUNKS)
            for b in range(B):
                nc.vector.bn_aggr(moments[:, b, :], stats[:, b * CPI:(b + 1) * CPI, :].rearrange("p a s -> p (a s)"))\
                    .then_inc(moments_done, 1)
            dve.wait_ge(moments_done, B)
            dve.wait_ge(means_done, 1)
            nc.vector.tensor_tensor(apart[:, :], moments[:, :, 0], mean_ps[:, 0:B], ALU.subtract).then_inc(chain, 1)
            dve.wait_ge(chain, 1)
            nc.vector.tensor_tensor(spread[:, :], apart[:, :], apart[:, :], ALU.mult).then_inc(chain, 1)
            dve.wait_ge(chain, 2)
            nc.vector.tensor_tensor(spread[:, :], spread[:, :], moments[:, :, 1], ALU.add).then_inc(chain, 1)
            dve.wait_ge(log_done, 2)
            nc.vector.tensor_tensor(offset[:, :], factor[:, :], mean_ps[:, 0:B], ALU.mult).then_inc(chain, 1)
            dve.wait_ge(chain, 4)
            nc.vector.tensor_scalar(offset[:, :], offset[:, :], -1.0, None, ALU.mult)

        @block.tensor
        def _(pe):
            pe.wait_ge(weights, 16)
            pe.wait_ge(moments_done, B)
            nc.tensor.matmul(mean_ps[:, 0:B], group_mean[:, :], moments[:, :, 0], start=True, stop=True)\
                .then_inc(means_done, 1)
            pe.wait_ge(chain, 3)
            nc.tensor.matmul(var_ps[:, 0:B], group_mean[:, :], spread[:, :], start=True, stop=True)\
                .then_inc(var_done, 1)

        @block.scalar
        def _(act):
            nc.scalar.preload_act_table_set("natural_log_exp_and_others")
            act.wait_ge(var_done, 1)
            nc.scalar.activation(factor[:, :], var_ps[:, 0:B], ACT.Ln, bias=eps[:, 0:1]).then_inc(log_done, 1)
            act.wait_ge(log_done, 1)
            nc.scalar.activation(factor[:, :], factor[:, :], ACT.Exp, scale=-0.5).then_inc(log_done, 1)

    with ExitStack() as own:
        sb1, ps1, sem1 = allocators(nc, own, "window_in")
        qkv_w = sb1("qkv_w", [C, 3 * C])
        qkv_b = sb1("qkv_b", [C, 3])
        v_bias = sb1("v_bias", [TILE, C])
        q_bias = sb1("q_bias", [C, 1])
        normed = sb1("normed", [C, 2, CHUNK])
        query = sb1("query", [C, 2, ACROSS, TILE])
        value = sb1("value", [TILE, 2, 4, C])
        qk_ps = ps1("qk_ps", [C, 2, 2, BANK])
        value_ps = ps1("value_ps", [TILE, 2, 4, C])
        weights = sem1("weights")
        q_bias_done = sem1("q_bias_done")
        normed_done = sem1("normed_done")
        q_done, k_done, value_done = sem1("q_done"), sem1("k_done"), sem1("value_done")
        q_out, k_out, value_out = sem1("q_out"), sem1("k_out"), sem1("value_out")
        q_stored = [sem1(f"q_stored{u}") for u in range(2)]
        v_stored = [sem1(f"v_stored{u}") for u in range(2)]
        block = own.enter_context(nc.Block())

        @block.sync
        def _(sp):
            sp.dma_start(qkv_w[:, :], io["qkv_w"]).then_inc(weights, 16)
            sp.dma_start(qkv_b[:, :], io["qkv_b"]).then_inc(weights, 16)
            sp.dma_start(v_bias[:, :], io["qkv_b_row"][:, 2 * C:3 * C].to_broadcast([TILE, C])).then_inc(weights, 16)

            def step(i, u, first, last):
                sp.wait_ge(q_out, i + 1)
                sp.dma_start(q_dram[bass.ds(i * 4, 4), :, :].rearrange("t c q -> c t q"), query[:, u, :, :])\
                  .then_inc(q_stored[u], 16)
                sp.wait_ge(value_out, i + 1)
                for r in range(2):
                    rows = v_dram[bass.ds(padded_pixel(i) + r * PW, 4 * 2 * PW), :]
                    sp.dma_start(rows.rearrange("(t w) c -> w t c", w=2 * PW)[0:W, :, :],
                                 value[r * W:(r + 1) * W, u, :, :]).then_inc(v_stored[u], 16)
            paced(sp, CHUNKS, step)
            for u in range(2):
                sp.wait_ge(q_stored[u], 16 * (CHUNKS // 2))
                sp.wait_ge(v_stored[u], 32 * (CHUNKS // 2))

        @block.tensor
        def _(pe):
            pe.wait_ge(weights, 48)

            def step(i, u, first, last):
                pe.wait_ge(normed_done, i + 1)
                for x, (done, out) in enumerate(((q_done, q_out), (k_done, k_out))):
                    at_least(pe, out, i - 1)
                    nc.tensor.matmul(qk_ps[:, u, x, 0:CHUNK], qkv_w[:, x * C:(x + 1) * C], normed[:, u, :],
                                     start=True, stop=True).then_inc(done, 1)
                at_least(pe, value_out, i - 1)
                for t in range(4):
                    mm = nc.tensor.matmul(value_ps[:, u, t, :], normed[:, u, t * TILE:(t + 1) * TILE],
                                          qkv_w[:, 2 * C:3 * C], start=True, stop=True)
                mm.then_inc(value_done, 1)
            paced(pe, CHUNKS, step)

        @block.scalar
        def _(act):
            act.wait_ge(weights, 48)
            nc.scalar.activation(q_bias[:, :], qkv_b[:, 0:1], ACT.Copy, scale=SCALE).then_inc(q_bias_done, 1)
            act.wait_ge(q_bias_done, 1)

            def step(i, u, first, last):
                act.wait_ge(q_done, i + 1)
                if not (isinstance(i, int) and i < 2):
                    act.wait_ge(q_stored[u], 8 * (i - u))
                by_tile = qk_ps[:, u, 0, 0:CHUNK].rearrange("p (r x c) -> p x r c", x=ACROSS, c=TW)
                nc.scalar.activation(query[:, u, :, :].rearrange("p x (r c) -> p x r c", c=TW), by_tile,
                                     ACT.Identity, bias=q_bias[:, 0:1], scale=SCALE).then_inc(q_out, 1)
                act.wait_ge(k_done, i + 1)
                rows = k_t[:, bass.ds(padded_pixel(i), CHUNK // W * PW)].rearrange("p (r w) -> p r w", w=PW)
                nc.scalar.activation(rows[:, :, 0:W], qk_ps[:, u, 1, 0:CHUNK].rearrange("p (r w) -> p r w", w=W),
                                     ACT.Identity, bias=qkv_b[:, 1:2]).then_inc(k_out, 1)
            paced(act, CHUNKS, step)

        @block.vector
        def _(dve):
            def normalise(i, u):
                at_least(dve, value_done, i - 1)
                nc.vector.tensor_scalar(normed[:, u, :], resid[:, bass.ds(i * CHUNK, CHUNK)],
                                        factor[:, bass.ds(i // CPI, 1)], offset[:, bass.ds(i // CPI, 1)],
                                        ALU.mult, ALU.add).then_inc(normed_done, 1)

            def copy_out(i, u):
                dve.wait_ge(value_done, i + 1)
                if not (isinstance(i, int) and i < 2):
                    dve.wait_ge(v_stored[u], 16 * (i - u))
                nc.vector.tensor_tensor(value[:, u, :, :], value_ps[:, u, :, :],
                                        v_bias[:, :].unsqueeze(1).to_broadcast([TILE, 4, C]), ALU.add)\
                    .then_inc(value_out, 1)

            def step(i, u, first, last):
                if first:
                    normalise(i, u)
                if not last:
                    normalise(i + 1, 1 - u)
                copy_out(i, u)
            dve.wait_ge(weights, 48)
            paced(dve, CHUNKS, step)

    SLOTS = ACROSS
    bias = sb("bias", [TILE, HEADS, KEYS])
    query = sb("query", [C, SLOTS, HEADS, TILE])
    raw_query = sb("raw_query", [C, SLOTS, TILE])
    head_rows = sb("head_rows", [C, HEADS])
    values = sb("values", [LOT, 2, LOTS, C])
    probs = sb("probs", [TILE, SLOTS, HEADS, LOTS * LOT])
    weights_t = sb("weights_t", [LOT, 2, LOTS, TILE])
    row_max = sb("row_max", [TILE, SLOTS, HEADS])
    neg_max = sb("neg_max", [TILE, SLOTS, HEADS])
    row_sum = sb("row_sum", [TILE, SLOTS, HEADS])
    row_inv = sb("row_inv", [TILE, SLOTS, HEADS])
    mixed = sb("mixed", [C, 2, TILE])
    gate = sb("gate", [1, HEADS])
    score_ps = ps("score_ps", [TILE, HEADS, BANK])
    turned_ps = ps("turned_ps", [LOT, 2, BANK])
    mixed_ps = ps("mixed_ps", [C, BANK])
    out_ps = ps("out_ps", [C, BANK])
    constants = sem("constants")
    bias_in = sem("bias_in")
    head_rows_in = sem("head_rows_in")
    query_done = sem("query_done")
    query_in = [sem(f"query_in{u}") for u in range(SLOTS)]
    values_in = [sem(f"values_in{u}") for u in range(2)]
    scores_done = sem("scores_done")
    biased = sem("biased")
    neg_done = sem("neg_done")
    exp_done = sem("exp_done")
    inv_done = sem("inv_done")
    probs_done = sem("probs_done")
    turned = sem("turned")
    even_out = sem("even_out")
    odd_out = sem("odd_out")
    mixed_done = sem("mixed_done")
    mixed_out = sem("mixed_out")
    out_done = sem("out_done")
    added = sem("added")
    block = ctx.enter_context(nc.Block())

    def first_key(n, u):
        return n // TPI * PIXELS + n % TPI // ACROSS * (TH * PW) + u * TW

    @block.sync
    def _(sp):
        sp.dma_start(bias[:, :, :],
                     bias_dram.rearrange("(h n) -> h n", h=HEADS)[:, 0:TILE * KEYS]
                     .rearrange("h (q k) -> q h k", k=KEYS)).then_inc(bias_in, 16)
        sp.dma_start(head_rows[:, :], io["head_rows"]).then_inc(head_rows_in, 16)

        def load_query(n, u):
            at_least(sp, query_done, n - SLOTS + 1)
            sp.dma_start(raw_query[:, u, :], q_dram[bass.ds(n, 1), :, :].rearrange("t c q -> (t c) q"))\
              .then_inc(query_in[u], 16)

        def load_values(n, u):
            at_least(sp, mixed_done, n - 1)
            for x in range(LOTS):
                rows = v_dram[bass.ds(first_key(n, u) + x * LOT_ROWS * PW, LOT_ROWS * PW), :]
                sp.dma_start(values[:, u % 2, x, :], rows.rearrange("(r w) c -> r w c", w=PW)[:, 0:KW, :])\
                  .then_inc(values_in[u % 2], 16)
        pipelined(sp, TILES, [(0, load_query), (4, load_values)], SLOTS)

    @block.gpsimd
    def _(pool):
        nc.gpsimd.memset(probs[:, :, :, :], 0.0).then_inc(constants, 1)

        def normalise(half):
            def op(n, u):
                pool.wait_ge(inv_done, 2 * n + half + 1)
                part = probs[:, u, 2 * half:2 * half + 2, 0:KEYS]
                inverse = row_inv[:, u, 2 * half:2 * half + 2].unsqueeze(2).to_broadcast([TILE, 2, KEYS])
                nc.gpsimd.tensor_tensor(part, part, inverse, ALU.mult).then_inc(probs_done, 1)
            return op
        def spread_query(n, u):
            at_least(pool, scores_done, (n - SLOTS + 1) * HEADS)
            pool.wait_ge(query_in[u], 16 // SLOTS * (n - u) + 16)
            nc.gpsimd.tensor_tensor(query[:, u, :, :], raw_query[:, u, :].unsqueeze(1).to_broadcast([C, HEADS, TILE]),
                                    head_rows[:, :].unsqueeze(2).to_broadcast([C, HEADS, TILE]), ALU.mult)\
                .then_inc(query_done, 1)
        pool.wait_ge(head_rows_in, 16)
        pipelined(pool, TILES, [(3, normalise(0)), (0, spread_query), (3, normalise(1))], SLOTS)

    @block.tensor
    def _(pe):
        def scores(h):
            def op(n, u):
                if h == 0:
                    pe.wait_ge(query_done, n + 1)
                at_least(pe, biased, (n - 1) * HEADS + h + 1)
                keys = k_t[:, bass.ds(first_key(n, u), KH * PW)].rearrange("p (r w) -> p r w", w=PW)[:, :, 0:KW]
                nc.tensor.matmul(score_ps[:, h, 0:KEYS], query[:, u, h, :], keys, start=True, stop=True)\
                    .then_inc(scores_done, 1)
            return op

        def turn(h):
            def op(n, u):
                if h % 2 == 0:
                    pe.wait_ge(probs_done, 2 * n + h // 2 + 1)
                copied = odd_out if h % 2 else even_out
                at_least(pe, copied, n * 2 + h // 2)
                for x in range(LOTS):
                    mm = nc.tensor.transpose(turned_ps[:, h % 2, x * TILE:(x + 1) * TILE],
                                             probs[:, u, h, x * LOT:(x + 1) * LOT], ident[0:TILE, 0:TILE])
                mm.then_inc(turned, 1)
            return op

        def product(h):
            def op(n, u):
                if h == 0:
                    pe.wait_ge(values_in[u % 2], 16 * LOTS // 2 * (n - u % 2) + 16 * LOTS)
                    at_least(pe, mixed_out, n)
                copied = odd_out if h % 2 else even_out
                pe.wait_ge(copied, n * 2 + h // 2 + 1)
                for x in range(LOTS):
                    mm = nc.tensor.matmul(mixed_ps[h * D:(h + 1) * D, 0:TILE], values[:, u % 2, x, h * D:(h + 1) * D],
                                          weights_t[:, h % 2, x, :], start=(x == 0), stop=(x == LOTS - 1))
                if h == HEADS - 1:
                    mm.then_inc(mixed_done, 1)
            return op

        def project(n, u):
            pe.wait_ge(mixed_out, n + 1)
            at_least(pe, added, n)
            nc.tensor.matmul(out_ps[:, 0:TILE], proj_w[:, :], mixed[:, u % 2, :], start=True, stop=True)\
                .then_inc(out_done, 1)

        pe.wait_ge(proj_in, 32)
        pe.wait_ge(constants, 1)
        pipelined(pe, TILES, [
            (0, scores(0)), (3, turn(0)), (4, product(3)),
            (0, scores(1)), (3, turn(1)), (3, product(0)),
            (0, scores(2)), (3, turn(2)), (3, product(1)), (4, project),
            (0, scores(3)), (3, turn(3)), (3, product(2))], SLOTS)

    def turned_copy(eng, copy, h, done):
        def op(n, u):
            eng.wait_ge(turned, n * HEADS + h + 1)
            copy(weights_t[:, h % 2, :, :], turned_ps[:, h % 2, 0:LOTS * TILE].rearrange("p (x q) -> p x q", x=LOTS))\
                .then_inc(done, 1)
        return op

    @block.vector
    def _(dve):
        def add_bias(h):
            def op(n, u):
                dve.wait_ge(scores_done, n * HEADS + h + 1)
                at_least(dve, turned, (n - SLOTS) * HEADS + h + 1)
                nc.vector.memset(gate[:, h:h + 1], 0.0)
                nc.vector.tensor_tensor_reduce(probs[:, u, h, 0:KEYS], score_ps[:, h, 0:KEYS], bias[:, h, :],
                                               1.0, -3e38, ALU.add, ALU.max, row_max[:, u, h:h + 1])\
                    .then_inc(biased, 1)
            return op

        def negative(n, u):
            dve.wait_ge(biased, (n + 1) * HEADS)
            nc.vector.tensor_scalar(neg_max[:, u, :], row_max[:, u, :], -1.0, None, ALU.mult).then_inc(neg_done, 1)

        def inverse(half):
            def op(n, u):
                dve.wait_ge(exp_done, 2 * n + half + 1)
                at_least(dve, probs_done, 2 * (n - SLOTS + 1))
                nc.vector.reciprocal(row_inv[:, u, 2 * half:2 * half + 2], row_sum[:, u, 2 * half:2 * half + 2])\
                    .then_inc(inv_done, 1)
            return op

        def add_up(n, u):
            dve.wait_ge(out_done, n + 1)
            at = resid[:, bass.ds(n // ACROSS * CHUNK, CHUNK)].rearrange("p (r w) -> p r w", w=W)
            at = at[:, :, bass.ds(n % ACROSS * TW, TW)]
            nc.vector.scalar_tensor_tensor(at, out_ps[:, 0:TILE].rearrange("p (r w) -> p r w", w=TW),
                                           proj_b[:, 0:1], at, ALU.add, ALU.add).then_inc(added, 1)

        def turned_copy_of(h):
            return turned_copy(dve, nc.vector.tensor_copy, h, even_out)
        dve.wait_ge(bias_in, 16)
        dve.wait_ge(proj_in, 32)
        dve.wait_ge(constants, 1)
        pipelined(dve, TILES, [
            (0, add_bias(0)), (3, turned_copy_of(0)), (0, add_bias(1)),
            (0, add_bias(2)), (1, inverse(0)), (3, turned_copy_of(2)), (0, add_bias(3)), (4, add_up),
            (0, negative), (1, inverse(1))], SLOTS)

    @block.scalar
    def _(act):
        def exponentials(h):
            def op(n, u):
                if h == 0:
                    act.wait_ge(neg_done, n + 1)
                    at_least(act, inv_done, 2 * (n - SLOTS + 1))
                e = nc.scalar.activation(probs[:, u, h, 0:KEYS], probs[:, u, h, 0:KEYS], ACT.Exp,
                                         bias=neg_max[:, u, h:h + 1], accum_out=row_sum[:, u, h:h + 1])
                if h % 2 == 1:
                    e.then_inc(exp_done, 1)
            return op

        def turned_copy_of(h):
            return turned_copy(act, lambda to, at: nc.scalar.activation(to, at, ACT.Copy), h, odd_out)

        def mixed_copy(n, u):
            act.wait_ge(mixed_done, n + 1)
            at_least(act, out_done, n - 1)
            nc.scalar.activation(mixed[:, u % 2, :], mixed_ps[:, 0:TILE], ACT.Copy).then_inc(mixed_out, 1)

        pipelined(act, TILES, [
            (1, exponentials(0)), (4, mixed_copy), (1, exponentials(1)),
            (3, turned_copy_of(1)), (1, exponentials(2)), (1, exponentials(3)), (3, turned_copy_of(3))], SLOTS)


def channel_attention(nc, ctx, resid, io):
    D = 16
    STACK = 96
    GROUP = 4
    GROUPS = TILES // GROUP
    GPI = TPI // GROUP
    CHAIN = GROUP * CPI
    LAG = 6
    SCALE_AT = 3
    SBANKS = 4
    sb, ps, sem = allocators(nc, ctx, "chan")
    g_dram = nc.dram_tensor("g_scratch", [STACK, TOKENS], FP32).ap()
    f_dram = nc.dram_tensor("f_scratch", [STACK, TOKENS], FP32).ap()
    hh_dram = nc.dram_tensor("hh_scratch", [TILE, TILES, C], FP32).ap()

    with ExitStack() as own:
        sb1, ps1, sem1 = allocators(nc, own, "chan_in")
        gf_w = sb1("gf_w", [C, 2, STACK])
        hh_w = sb1("hh_w", [C, C])
        chunk = sb1("chunk", [C, 2, CHUNK])
        gf = sb1("gf", [STACK, 2, 2, CHUNK], FP32R)
        hh = sb1("hh", [TILE, 2, 4, C])
        gf_ps = ps1("gf_ps", [STACK, 2, 2, BANK])
        hh_ps = ps1("hh_ps", [TILE, 2, 4, C])
        weights = sem1("weights")
        zeroed = sem1("zeroed")
        staged = sem1("staged")
        gf_done = sem1("gf_done")
        hh_done = sem1("hh_done")
        hi_out = sem1("hi_out")
        gf_out = sem1("gf_out")
        hh_out = sem1("hh_out")
        stored = [sem1(f"stored{u}") for u in range(2)]
        block = own.enter_context(nc.Block())

        def stores_before(i, u):
            return 24 * (i - u)

        @block.gpsimd
        def _(pool):
            nc.gpsimd.memset(gf_w[:, :, :], 0.0).then_inc(zeroed, 1)

            def step(i, u, first, last):
                at_least(pool, hh_done, i - 1)
                nc.gpsimd.tensor_copy(chunk[:, u, :], resid[:, bass.ds(i * CHUNK, CHUNK)]).then_inc(staged, 1)
            paced(pool, CHUNKS, step)

        @block.sync
        def _(sp):
            sp.wait_ge(zeroed, 1)
            for p in range(0, STACK, 32):
                sp.dma_start(gf_w[:, 0, p:p + D], io["kernel_g"]).then_inc(weights, 16)
                sp.dma_start(gf_w[:, 1, p:p + D], io["kernel_f"]).then_inc(weights, 16)
            sp.dma_start(hh_w[:, :], io["kernel_h"]).then_inc(weights, 16)

            def step(i, u, first, last):
                sp.wait_ge(gf_out, i + 1)
                sp.wait_ge(hh_out, i + 1)
                sp.dma_start(g_dram[:, bass.ds(i * CHUNK, CHUNK)], gf[:, u, 0, :].bitcast(FP32)).then_inc(stored[u], 16)
                sp.dma_start(f_dram[:, bass.ds(i * CHUNK, CHUNK)], gf[:, u, 1, :].bitcast(FP32)).then_inc(stored[u], 16)
                sp.dma_start(hh_dram[:, bass.ds(i * 4, 4), :], hh[:, u, :, :]).then_inc(stored[u], 16)
            paced(sp, CHUNKS, step)
            for u in range(2):
                sp.wait_ge(stored[u], 48 * (CHUNKS // 2))

        @block.tensor
        def _(pe):
            pe.wait_ge(weights, 7 * 16)

            def step(i, u, first, last):
                pe.wait_ge(staged, i + 1)
                at_least(pe, gf_out, i - 1)
                for x in range(2):
                    mm = nc.tensor.matmul(gf_ps[:, u, x, 0:CHUNK], gf_w[:, x, :], chunk[:, u, :],
                                          start=True, stop=True)
                mm.then_inc(gf_done, 1)
                at_least(pe, hh_out, i - 1)
                for t in range(4):
                    mm = nc.tensor.matmul(hh_ps[:, u, t, :], chunk[:, u, t * TILE:(t + 1) * TILE], hh_w[:, :],
                                          start=True, stop=True)
                mm.then_inc(hh_done, 1)
            paced(pe, CHUNKS, step)

        @block.scalar
        def _(act):
            def step(i, u, first, last):
                act.wait_ge(gf_done, i + 1)
                if not first and not (isinstance(i, int) and i < 2):
                    act.wait_ge(stored[u], stores_before(i, u))
                nc.scalar.activation(gf[:, u, :, :], gf_ps[:, u, :, 0:CHUNK], ACT.Copy).then_inc(hi_out, 1)
            paced(act, CHUNKS, step)

        @block.vector
        def _(dve):
            def step(i, u, first, last):
                dve.wait_ge(hh_done, i + 1)
                if not (isinstance(i, int) and i < 2):
                    dve.wait_ge(stored[u], stores_before(i, u))
                nc.vector.tensor_copy(hh[:, u, :, :], hh_ps[:, u, :, :]).then_inc(hh_out, 1)
                dve.wait_ge(hi_out, i + 1)
                for x, p in ((0, 32), (1, 64)):
                    part = gf[p:p + 32, u, x, :]
                    lo = nc.vector.tensor_tensor(part, gf_ps[p:p + 32, u, x, 0:CHUNK], part.bitcast(FP32),
                                                 ALU.subtract)
                lo.then_inc(gf_out, 1)
            paced(dve, CHUNKS, step)

    g_row = sb("g_row", [STACK, 2, N], FP32R)
    f_cols = sb("f_cols", [STACK, 2, GROUP * TILE], FP32R)
    values = sb("values", [TILE, 2, GROUP, C])
    scaled = sb("scaled", [TILE, 2, GROUP, C])
    probs = sb("probs", [TILE, 2, GROUP, N])
    chunk_max = sb("chunk_max", [TILE, 2, GROUP, CPI])
    row_max = sb("row_max", [TILE, 2, GROUP])
    neg_max = sb("neg_max", [TILE, 2, GROUP])
    row_sum = sb("row_sum", [TILE, 2, GROUP])
    row_inv = sb("row_inv", [TILE, 2, GROUP])
    gamma = sb("gamma", [C, 1])
    score_ps = ps("score_ps", [TILE, SBANKS, BANK])
    out_ps = ps("out_ps", [C, 2, BANK])
    gamma_in = sem("gamma_in")
    loaded = [sem(f"loaded{u}") for u in range(2)]
    scores_done = sem("scores_done")
    copied = sem("copied")
    max_done = sem("max_done")
    neg_done = sem("neg_done")
    exp_done = sem("exp_done")
    inv_done = sem("inv_done")
    scaled_done = sem("scaled_done")
    product_done = sem("product_done")
    added = sem("added")
    block = ctx.enter_context(nc.Block())

    def has_two_before(i):
        return not isinstance(i, int) or i >= 2

    @block.sync
    def _(sp):
        sp.dma_start(gamma[:, :], io["gamma"]).then_inc(gamma_in, 16)

        def step(i, u, first, last):
            at_least(sp, scores_done, (i - 1) * GROUP * CPI)
            sp.dma_start(g_row[:, u, :].bitcast(FP32), g_dram[:, bass.ds((i // GPI) * N, N)]).then_inc(loaded[u], 16)
            sp.dma_start(f_cols[:, u, :].bitcast(FP32), f_dram[:, bass.ds(i * CHUNK, CHUNK)]).then_inc(loaded[u], 16)
            at_least(sp, scaled_done, (i - 1) * GROUP)
            sp.dma_start(values[:, u, :, :], hh_dram[:, bass.ds(i * GROUP, GROUP), :]).then_inc(loaded[u], 16)
        paced(sp, GROUPS, step)

    @block.tensor
    def _(pe):
        def scores(i, u, k):
            at_least(pe, copied, i * GROUP * CPI + k - (SBANKS - 1))
            m, c = k // CPI, k % CPI
            nc.tensor.matmul(score_ps[:, k % SBANKS, 0:CHUNK], f_cols[:, u, m * TILE:(m + 1) * TILE],
                             g_row[:, u, c * CHUNK:(c + 1) * CHUNK], start=True, stop=True)\
                .then_inc(scores_done, 1)

        def product(i, u, k):
            c, m = k // GROUP, k % GROUP
            if m == 0:
                if c == 0:
                    pe.wait_ge(scaled_done, (i + 1) * GROUP)
                at_least(pe, added, i * CPI + c - 1)
            mm = nc.tensor.matmul(out_ps[:, (u + c) % 2, 0:CHUNK], scaled[:, u, m, :],
                                  probs[:, u, m, c * CHUNK:(c + 1) * CHUNK],
                                  start=(m == 0), stop=(m == GROUP - 1))
            if m == GROUP - 1:
                mm.then_inc(product_done, 1)

        def step(i, u, first, last):
            pe.wait_ge(loaded[u], 24 * (i - u) + 48)
            for k in range(CHAIN):
                scores(i, u, k)
                if k >= LAG and not first:
                    product(i - 1, 1 - u, k - LAG)
                if k < LAG and has_two_before(i):
                    product(i - 2, u, CHAIN + k - LAG)
            if last:
                for k in range(CHAIN - LAG, CHAIN):
                    product(i - 1, 1 - u, k)
                for k in range(CHAIN):
                    product(i, u, k)
        paced(pe, GROUPS, step)

    @block.vector
    def _(dve):
        def copy_out(i, u, k):
            m, c = k // CPI, k % CPI
            dve.wait_ge(scores_done, i * GROUP * CPI + k + 1)
            if m == 0:
                at_least(dve, product_done, (i - 2) * CPI + c + 1)
            nc.vector.tensor_scalar(probs[:, u, m, c * CHUNK:(c + 1) * CHUNK], score_ps[:, k % SBANKS, 0:CHUNK],
                                    1.0, None, ALU.mult, ALU.max,
                                    accum_out=chunk_max[:, u, m, c:c + 1]).then_inc(copied, 1)

        def negative_max(i, u, m):
            dve.wait_ge(copied, (i * GROUP + m + 1) * CPI)
            nc.vector.tensor_reduce(row_max[:, u, m:m + 1], chunk_max[:, u, m, :], AX, ALU.max).then_inc(max_done, 1)
            dve.wait_ge(max_done, i * GROUP + m + 1)
            nc.vector.tensor_scalar(neg_max[:, u, m:m + 1], row_max[:, u, m:m + 1], -1.0, None, ALU.mult)\
                .then_inc(neg_done, 1)

        def scale_values(i, u, m):
            dve.wait_ge(exp_done, i * GROUP + m + 1)
            nc.vector.reciprocal(row_inv[:, u, m:m + 1], row_sum[:, u, m:m + 1]).then_inc(inv_done, 1)
            dve.wait_ge(inv_done, i * GROUP + m + 1)
            if m == 0:
                dve.wait_ge(loaded[u], 24 * (i - u) + 48)
            nc.vector.tensor_scalar(scaled[:, u, m, :], values[:, u, m, :], row_inv[:, u, m:m + 1], None, ALU.mult)\
                .then_inc(scaled_done, 1)

        def add_up(i, u, c):
            dve.wait_ge(product_done, i * CPI + c + 1)
            at = resid[:, bass.ds((i // GPI) * N + c * CHUNK, CHUNK)]
            nc.vector.scalar_tensor_tensor(at, out_ps[:, (u + c) % 2, 0:CHUNK], gamma[:, 0:1], at,
                                           ALU.mult, ALU.add).then_inc(added, 1)

        def step(i, u, first, last):
            for k in range(CHAIN):
                copy_out(i, u, k)
                if k % CPI == CPI - 1:
                    negative_max(i, u, k // CPI)
                if k % CPI == SCALE_AT:
                    if k >= CPI:
                        scale_values(i, u, k // CPI - 1)
                    elif not first:
                        scale_values(i - 1, 1 - u, GROUP - 1)
                if (k - LAG) % GROUP == 0:
                    c = (k - LAG) // GROUP - 1
                    if c >= 0 and not first:
                        add_up(i - 1, 1 - u, c)
                    if c < 0 and has_two_before(i):
                        add_up(i - 2, u, c + CPI)
            if last:
                for c in range((CHAIN - 1 - LAG) // GROUP, CPI):
                    add_up(i - 1, 1 - u, c)
                scale_values(i, u, GROUP - 1)
                for c in range(CPI):
                    add_up(i, u, c)
        dve.wait_ge(gamma_in, 16)
        paced(dve, GROUPS, step)

    @block.scalar
    def _(act):
        def step(i, u, first, last):
            for m in range(GROUP):
                act.wait_ge(neg_done, i * GROUP + m + 1)
                nc.scalar.activation(probs[:, u, m, :], probs[:, u, m, :], ACT.Exp, bias=neg_max[:, u, m:m + 1],
                                     accum_out=row_sum[:, u, m:m + 1]).then_inc(exp_done, 1)
        paced(act, GROUPS, step)


def sparse_attention(nc, ctx, resid, io, ident, mean_w, eps):
    WINDOW, STRIDE, FIRST = 128, 64, 4
    EVERY = N // STRIDE
    GLOBALS = EVERY + FIRST - 1
    LOCAL = WINDOW + TILE
    SCALE = float(np.float32(1.0 / np.sqrt(C)))
    DECAY = float(np.exp(np.float32(-1.0 / 10.0)))
    PADDED = WINDOW + N
    COLS = LOCAL + GLOBALS
    KEYS = 3 * C
    SPLIT = C - TILE
    sb, ps, sem = allocators(nc, ctx, "sparse")
    k_t = sb("k_t", [C, B * PADDED])
    q_t = sb("q_t", [C, TOKENS])
    k_every = sb("k_every", [C, B, GLOBALS])
    v_dram = nc.dram_tensor("sparse_v", [B * PADDED, C], FP32).ap()
    local_mask = sb("local_mask", [1, PADDED], BF16)
    every_mask = sb("every_mask", [1, GLOBALS], BF16)
    current = sb("current", [TILES, TILE])
    wo = sb("wo", [C, C])
    bo = sb("bo", [C, 1])
    loaded = sem("loaded")

    with ExitStack() as own:
        norm = Norm(nc, own, "sparse", resid, mean_w, eps)
        sb1, ps1, sem1 = allocators(nc, own, "sparse_in")
        ws = sb1("ws", [C, 1])
        bs = sb1("bs", [TILE, 1])
        by_token = sb1("by_token", [TILE, TILES])
        current_ps = ps1("current_ps", [TILE, 2, BANK])
        turn_ps = ps1("turn_ps", [C, BANK])
        weights = sem1("weights")
        kept = sem1("kept")
        current_done = sem1("current_done")
        current_out = sem1("current_out")
        turned = sem1("turned")
        block = own.enter_context(nc.Block())

        @block.sync
        def _(sp):
            sp.dma_start(ws[:, :], io["Ws"]).then_inc(weights, 16)
            sp.dma_start(bs[:, :], io["bs"].to_broadcast([TILE, 1])).then_inc(weights, 16)

        @block.gpsimd
        def _(pool):
            nc.gpsimd.memset(k_t[:, :].rearrange("p (b n) -> p b n", b=B)[:, :, 0:WINDOW], 0.0)

            def keep(i, u, first, last):
                pool.wait_ge(norm.normed_done, i + 1)
                nc.gpsimd.tensor_copy(q_t[:, bass.ds(i * CHUNK, CHUNK)], norm.normed[:, u, :]).then_inc(kept, 1)
            paced(pool, CHUNKS, keep)

        @block.tensor
        def _(pe):
            pe.wait_ge(weights, 32)

            def project(i, u):
                pe.wait_ge(norm.normed_done, i + 1)
                at_least(pe, current_out, i - 1)
                for t in range(4):
                    mm = nc.tensor.matmul(current_ps[:, u, t:t + 1], norm.normed[:, u, t * TILE:(t + 1) * TILE],
                                          ws[:, :], start=True, stop=True)
                mm.then_inc(current_done, 1)
            norm.tensor_steps(pe, project)
            pe.wait_ge(current_out, CHUNKS)
            nc.tensor.transpose(turn_ps[0:TILES, 0:TILE], by_token[:, :], ident[0:TILE, 0:TILE]).then_inc(turned, 1)

        @block.scalar
        def _(act):
            nc.scalar.preload_act_table_set("natural_log_exp_and_others")
            norm.scalar_steps(act, lambda i, u: None)

        @block.vector
        def _(dve):
            dve.wait_ge(weights, 32)

            def take_current(i, u):
                dve.wait_ge(current_done, i + 1)
                nc.vector.tensor_scalar(by_token[:, bass.ds(i * 4, 4)], current_ps[:, u, 0:4], bs[:, 0:1], None,
                                        ALU.add).then_inc(current_out, 1)
            norm.vector_steps(dve, ((current_done, 1), (kept, 1)), take_current)
            dve.wait_ge(turned, 1)
            nc.vector.tensor_copy(current[:, :], turn_ps[0:TILES, 0:TILE])

    with ExitStack() as own:
        sb1, ps1, sem1 = allocators(nc, own, "sparse_fire")
        mask_dram = nc.dram_tensor("sparse_mask", [TPI, TILE], BF16).ap()
        LOT = 16
        STEPS = TILE // LOT * (2 * LOT + 2)
        RUNS = 3
        charge = sb1("charge", [TILES, TILE])
        lot_in = sb1("lot_in", [TILES, LOT])
        lot_charge = sb1("lot_charge", [TILES, LOT])
        start = sb1("start", [TILES, 1])
        state = sb1("state", [TILES, 2])
        end = sb1("end", [TILES, 1])
        fired = sb1("fired", [TILES, TILE])
        apart = sb1("apart", [TILES, 1])
        ones = sb1("ones", [TILES, 1])
        not_first = sb1("not_first", [TILES, 1])
        image_sum = sb1("image_sum", [TILES, TPI])
        mask_rows = sb1("mask_rows", [TPI, TILE], BF16)
        count = sb1("count", [1, 1], mybir.dt.int32)
        sum_ps = ps1("sum_ps", [C, BANK])
        count_ps = ps1("count_ps", [C, BANK])
        wq, wk, wv = sb1("wq", [C, C]), sb1("wk", [C, C]), sb1("wv", [C, C])
        bq = sb1("bq", [C, 1])
        bk = sb1("bk", [C, 1])
        bv = sb1("bv", [TILE, C])
        zeros = sb1("zeros", [C, C])
        normed = sb1("normed", [C, 2, CHUNK])
        value = sb1("value", [TILE, 2, 4, C])
        qk_ps = ps1("qk_ps", [C, 2, 2, BANK])
        value_ps = ps1("value_ps", [TILE, 2, 4, C])
        zeroed = sem1("zeroed")
        weights = sem1("weights")
        staged = sem1("staged")
        q_done, k_done = sem1("q_done"), sem1("k_done")
        value_done = sem1("value_done")
        q_out, k_out = sem1("q_out"), sem1("k_out")
        value_copied = sem1("value_copied")
        value_out = sem1("value_out")
        stored = [sem1(f"stored{u}") for u in range(2)]
        padded = sem1("padded")
        constants = sem1("constants")
        consts_in = sem1("consts_in")
        chain = sem1("chain")
        again_chain = sem1("again_chain")
        moved = sem1("moved")
        moved_again = sem1("moved_again")
        end_out = sem1("end_out")
        end_again = sem1("end_again")
        count_ready = sem1("count_ready")
        count_done = sem1("count_done")
        count_out = sem1("count_out")
        fired_done = sem1("fired_done")
        sum_done = sem1("sum_done")
        rows_out = sem1("rows_out")
        flat = sem1("flat")
        block = own.enter_context(nc.Block())

        def shift_down(sp, to):
            return sp.dma_start(start[1:TILES, :], end[0:TILES - 1, :]).then_inc(to, 16)

        @block.gpsimd
        def _(pool):
            nc.gpsimd.memset(ones[:, :], 1.0).then_inc(constants, 1)
            nc.gpsimd.memset(local_mask[0:1, 0:WINDOW], NEG).then_inc(constants, 1)
            nc.gpsimd.memset(zeros[:, :], 0.0).then_inc(zeroed, 1)
            pool.wait_ge(weights, 6 * 16)

            def add_bias(i, u, first, last):
                pool.wait_ge(value_copied, i + 1)
                nc.gpsimd.tensor_tensor(value[:, u, :, :], value[:, u, :, :],
                                        bv[:, :].unsqueeze(1).to_broadcast([TILE, 4, C]), ALU.add)\
                    .then_inc(value_out, 1)
                pool.wait_ge(value_out, i + 1)
                row = i * CHUNK + (i // CPI + 1) * WINDOW
                pool.dma_start(v_dram[bass.ds(row, CHUNK), :].rearrange("(t p) c -> p t c", p=TILE),
                               value[:, u, :, :]).then_inc(stored[u], 16)
            paced(pool, CHUNKS, add_bias)
            for u in range(2):
                pool.wait_ge(stored[u], 16 * (CHUNKS // 2))

        @block.sync
        def _(sp):
            sp.dma_start(not_first[:, :], io["not_first"]).then_inc(consts_in, 16)
            sp.dma_start(image_sum[:, :], io["image_sum"]).then_inc(consts_in, 16)
            for to, name in ((wq, "Wq"), (wk, "Wk"), (wv, "Wv"), (bq, "bq"), (bk, "bk")):
                sp.dma_start(to[:, :], io[name]).then_inc(weights, 16)
            sp.dma_start(bv[:, :], io["bv"].to_broadcast([TILE, C])).then_inc(weights, 16)
            sp.dma_start(wo[:, :], io["Wo"]).then_inc(loaded, 16)
            sp.dma_start(bo[:, :], io["bo"]).then_inc(loaded, 16)
            sp.wait_ge(zeroed, 1)
            for b in range(B):
                sp.dma_start(v_dram[b * PADDED:b * PADDED + WINDOW, :], zeros[:, :]).then_inc(padded, 16)
            sp.wait_ge(padded, 16 * B)
            for r in range(1, RUNS):
                sp.wait_ge(end_out, r)
                shift_down(sp, moved)
            sp.wait_ge(count_out, 1)
            wrong = sp.value_load(count[0:1, 0:1])
            with sp.If(wrong):
                with sp.Fori(0, TPI) as r:
                    sp.wait_ge(end_again, r)
                    shift_down(sp, moved_again)
            sp.wait_ge(rows_out, 1)
            sp.dma_start(mask_dram[:, :], mask_rows[:, :]).then_inc(flat, 16)
            sp.wait_ge(flat, 16)
            sp.dma_start(local_mask[0:1, WINDOW:PADDED], mask_dram.rearrange("(a s) n -> a (s n)", a=1))\
              .then_inc(flat, 16)

        def run(dve, links, base):
            per_lot = 2 * LOT + 2
            with dve.Fori(0, TILE // LOT) as g:
                at = base + g * per_lot
                dve.wait_ge(links, at)
                nc.vector.tensor_copy(lot_in[:, :], current[:, bass.ds(g * LOT, LOT)]).then_inc(links, 1)
                for k in range(LOT):
                    u = k % 2
                    dve.wait_ge(links, at + 1 + 2 * k)
                    nc.vector.scalar_tensor_tensor(lot_charge[:, k:k + 1], state[:, 1 - u:2 - u], DECAY,
                                                   lot_in[:, k:k + 1], ALU.mult, ALU.add).then_inc(links, 1)
                    dve.wait_ge(links, at + 2 + 2 * k)
                    nc.vector.scalar_tensor_tensor(state[:, u:u + 1], lot_charge[:, k:k + 1], 1.0,
                                                   lot_charge[:, k:k + 1], ALU.is_lt, ALU.mult).then_inc(links, 1)
                nc.vector.tensor_copy(charge[:, bass.ds(g * LOT, LOT)], lot_charge[:, :]).then_inc(links, 1)
            dve.wait_ge(links, base + STEPS)
            return nc.vector.tensor_copy(end[:, :], state[:, 1:2])

        @block.vector
        def _(dve):
            dve.wait_ge(constants, 2)
            dve.wait_ge(consts_in, 32)
            nc.vector.memset(start[:, :], 0.0).then_inc(chain, 1)
            nc.vector.memset(state[:, :], 0.0).then_inc(chain, 1)
            run(dve, chain, 2).then_inc(end_out, 1)
            done = 2 + STEPS
            for r in range(1, RUNS):
                dve.wait_ge(moved, 16 * r)
                nc.vector.tensor_tensor(state[:, 1:2], start[:, :], not_first[:, :], ALU.mult).then_inc(chain, 1)
                done += 1
                if r == RUNS - 1:
                    nc.vector.tensor_copy(apart[:, :], end[:, :]).then_inc(chain, 1)
                    done += 1
                run(dve, chain, done).then_inc(end_out, 1)
                done += STEPS
            dve.wait_ge(end_out, RUNS)
            nc.vector.tensor_tensor(apart[:, :], apart[:, :], end[:, :], ALU.not_equal).then_inc(count_ready, 1)
            dve.wait_ge(count_done, 1)
            nc.vector.tensor_copy(count[:, :], count_ps[0:1, 0:1]).then_inc(count_out, 1)
            dve.wait_ge(count_out, 1)
            wrong = dve.value_load(count[0:1, 0:1])
            with dve.If(wrong):
                with dve.Fori(0, TPI) as r:
                    dve.wait_ge(moved_again, 16 * (r + 1))
                    nc.vector.tensor_tensor(state[:, 1:2], start[:, :], not_first[:, :], ALU.mult)\
                        .then_inc(again_chain, 1)
                    run(dve, again_chain, r * (STEPS + 1) + 1).then_inc(end_again, 1)
                dve.wait_ge(end_again, TPI)
            nc.vector.tensor_scalar(fired[:, :], charge[:, :], 1.0, None, ALU.is_ge).then_inc(fired_done, 1)
            dve.wait_ge(sum_done, 1)
            nc.vector.tensor_scalar(mask_rows[:, :], sum_ps[0:TPI, 0:TILE], 0.5, NEG, ALU.is_lt, ALU.mult)\
                .then_inc(rows_out, 1)
            dve.wait_ge(flat, 32)
            nc.vector.tensor_copy(every_mask[0:1, 0:EVERY], local_mask[0:1, WINDOW:PADDED:STRIDE]).then_inc(rows_out, 1)
            nc.vector.tensor_copy(every_mask[0:1, EVERY:GLOBALS],
                                  local_mask[0:1, WINDOW + 1:WINDOW + FIRST]).then_inc(rows_out, 1)
            dve.wait_ge(rows_out, 3)
            nc.vector.memset(local_mask[0:1, WINDOW:PADDED:STRIDE], NEG).then_inc(rows_out, 1)
            nc.vector.memset(local_mask[0:1, WINDOW + 1:WINDOW + FIRST], NEG)
            dve.wait_ge(k_out, CHUNKS)
            images = k_t[:, :].rearrange("p (b n) -> p b n", b=B)
            nc.vector.tensor_copy(k_every[:, :, 0:EVERY], images[:, :, WINDOW:PADDED:STRIDE])
            nc.vector.tensor_copy(k_every[:, :, EVERY:GLOBALS], images[:, :, WINDOW + 1:WINDOW + FIRST])

        @block.scalar
        def _(act):
            act.wait_ge(weights, 6 * 16)

            def stage(i, u):
                at_least(act, value_done, i - 1)
                nc.scalar.activation(normed[:, u, :], q_t[:, bass.ds(i * CHUNK, CHUNK)], ACT.Copy).then_inc(staged, 1)

            def copy_out(i, u):
                act.wait_ge(q_done, i + 1)
                nc.scalar.activation(q_t[:, bass.ds(i * CHUNK, CHUNK)], qk_ps[:, u, 0, 0:CHUNK], ACT.Identity,
                                     bias=bq[:, 0:1]).then_inc(q_out, 1)
                act.wait_ge(k_done, i + 1)
                nc.scalar.activation(k_t[:, bass.ds(i * CHUNK + (i // CPI + 1) * WINDOW, CHUNK)],
                                     qk_ps[:, u, 1, 0:CHUNK], ACT.Identity, bias=bk[:, 0:1]).then_inc(k_out, 1)
                act.wait_ge(value_done, i + 1)
                if not (isinstance(i, int) and i < 2):
                    act.wait_ge(stored[u], 8 * (i - u))
                nc.scalar.activation(value[:, u, :, :], value_ps[:, u, :, :], ACT.Copy).then_inc(value_copied, 1)
            pipelined(act, CHUNKS, [(2, copy_out), (0, stage)])

        @block.tensor
        def _(pe):
            pe.wait_ge(weights, 6 * 16)

            def project(i, u):
                pe.wait_ge(staged, i + 1)
                at_least(pe, q_out, i - 1)
                nc.tensor.matmul(qk_ps[:, u, 0, 0:CHUNK], wq[:, :], normed[:, u, :], start=True, stop=True)\
                    .then_inc(q_done, 1)
                at_least(pe, k_out, i - 1)
                nc.tensor.matmul(qk_ps[:, u, 1, 0:CHUNK], wk[:, :], normed[:, u, :], start=True, stop=True)\
                    .then_inc(k_done, 1)
                at_least(pe, value_copied, i - 1)
                for t in range(4):
                    mm = nc.tensor.matmul(value_ps[:, u, t, :], normed[:, u, t * TILE:(t + 1) * TILE], wv[:, :],
                                          start=True, stop=True)
                mm.then_inc(value_done, 1)
            pipelined(pe, CHUNKS, [(0, project)])
            pe.wait_ge(constants, 2)
            pe.wait_ge(count_ready, 1)
            nc.tensor.matmul(count_ps[0:1, 0:1], apart[:, :], ones[:, :], start=True, stop=True).then_inc(count_done, 1)
            pe.wait_ge(consts_in, 32)
            pe.wait_ge(fired_done, 1)
            nc.tensor.matmul(sum_ps[0:TPI, 0:TILE], image_sum[:, :], fired[:, :], start=True, stop=True)\
                .then_inc(sum_done, 1)

    band = sb("band", [TILE, LOCAL], BF16)
    band_full = sb("band_full", [TILE, LOCAL])
    ident_half = sb("ident_half", [TILE, TILE], BF16)
    ones_row = sb("ones_row", [1, TILE], BF16)
    query = sb("query", [C, 2, TILE])
    values = sb("values", [C, 2, 3, C])
    probs = sb("probs", [TILE, 2, KEYS])
    weights_t = sb("weights_t", [C, 2, 3, TILE])
    row_max = sb("row_max", [TILE, 2])
    neg_max = sb("neg_max", [TILE, 2])
    row_sum = sb("row_sum", [TILE, 2])
    row_inv = sb("row_inv", [TILE, 2])
    mixed = sb("mixed", [C, 2, TILE])
    score_ps = ps("score_ps", [TILE, 2, BANK])
    turned_ps = ps("turned_ps", [C, 2, BANK])
    mixed_ps = ps("mixed_ps", [C, 2, BANK])
    out_ps = ps("out_ps", [C, 2, BANK])
    constants = sem("constants")
    band_in = sem("band_in")
    band_out = sem("band_out")
    query_in = sem("query_in")
    values_in = [sem(f"values_in{u}") for u in range(2)]
    scores_done = sem("scores_done")
    max_done = sem("max_done")
    neg_done = sem("neg_done")
    exp_done = sem("exp_done")
    sum_safe = sem("sum_safe")
    inv_done = sem("inv_done")
    probs_done = sem("probs_done")
    turned = sem("turned")
    turned_out = sem("turned_out")
    mixed_done = sem("mixed_done")
    mixed_out = sem("mixed_out")
    out_done = sem("out_done")
    added = sem("added")
    block = ctx.enter_context(nc.Block())

    @block.gpsimd
    def _(pool):
        nc.gpsimd.memset(ones_row[:, :], 1.0).then_inc(constants, 1)
        nc.gpsimd.memset(probs[:, :, :], 0.0).then_inc(constants, 1)
        nc.gpsimd.memset(values[:, :, :, :], 0.0).then_inc(constants, 1)

    @block.sync
    def _(sp):
        sp.dma_start(band_full[:, :], io["band"]).then_inc(band_in, 16)
        sp.wait_ge(constants, 3)
        with sp.Fori(0, B) as b:
            def step(t, u, first, last):
                n = b * TPI + t
                if isinstance(t, int) and t < 2:
                    sp.wait_ge(mixed_done, b * TPI)
                else:
                    sp.wait_ge(mixed_done, n - 1)
                row = b * PADDED + t * TILE
                sp.dma_start(values[:, u, 0, :], v_dram[bass.ds(row, WINDOW), :]).then_inc(values_in[u], 16)
                sp.dma_start(values[0:TILE, u, 1, :], v_dram[bass.ds(row + WINDOW, TILE), :])\
                  .then_inc(values_in[u], 16)
                if isinstance(t, int) and t < 2:
                    every = v_dram[bass.ds(b * PADDED + WINDOW, N), :].rearrange("(g s) c -> g s c", s=STRIDE)
                    sp.dma_start(values[TILE:C, u, 1, :], every[0:SPLIT, 0, :]).then_inc(values_in[u], 16)
                    sp.dma_start(values[0:EVERY - SPLIT, u, 2, :], every[SPLIT:EVERY, 0, :])\
                      .then_inc(values_in[u], 16)
                    sp.dma_start(values[EVERY - SPLIT:GLOBALS - SPLIT, u, 2, :],
                                 v_dram[bass.ds(b * PADDED + WINDOW + 1, FIRST - 1), :]).then_inc(values_in[u], 16)
            paced(sp, TPI, step)

    def values_loaded(n, u):
        return (n - u) * 16 + n // TPI * 48 + 80

    @block.tensor
    def _(pe):
        def scores(n, u):
            pe.wait_ge(query_in, n + 1)
            at_least(pe, exp_done, n - 1)
            s = score_ps[:, u, :]
            nc.tensor.matmul(s[:, 0:LOCAL], query[:, u, :], k_t[:, bass.ds(n * TILE + n // TPI * WINDOW, LOCAL)],
                             start=True, stop=False)
            nc.tensor.matmul(s[:, 0:LOCAL], ident_half[:, :], band[:, :], start=False, stop=False)
            nc.tensor.matmul(s[:, 0:LOCAL], ones_row[:, :],
                             local_mask[0:1, bass.ds(n % TPI * TILE, LOCAL)], start=False, stop=True)
            nc.tensor.matmul(s[:, LOCAL:COLS], query[:, u, :], every_t[:, bass.ds(n // TPI * GLOBALS, GLOBALS)],
                             start=True, stop=False)
            nc.tensor.matmul(s[:, LOCAL:COLS], ones_row[:, :], every_mask[:, :], start=False, stop=True)\
                .then_inc(scores_done, 1)

        def turn(n, u):
            pe.wait_ge(probs_done, n + 1)
            at_least(pe, turned_out, n - 1)
            for x in range(3):
                mm = nc.tensor.transpose(turned_ps[:, u, x * TILE:(x + 1) * TILE],
                                         probs[:, u, x * C:(x + 1) * C], ident[0:TILE, 0:TILE])
            mm.then_inc(turned, 1)

        def product(n, u):
            pe.wait_ge(values_in[u], values_loaded(n, u))
            pe.wait_ge(turned_out, n + 1)
            at_least(pe, mixed_out, n - 1)
            for x in range(3):
                mm = nc.tensor.matmul(mixed_ps[:, u, 0:TILE], values[:, u, x, :], weights_t[:, u, x, :],
                                      start=(x == 0), stop=(x == 2))
            mm.then_inc(mixed_done, 1)

        def project(n, u):
            pe.wait_ge(mixed_out, n + 1)
            at_least(pe, added, n - 1)
            nc.tensor.matmul(out_ps[:, u, 0:TILE], wo[:, :], mixed[:, u, :], start=True, stop=True)\
                .then_inc(out_done, 1)

        every_t = k_every[:, :, :].rearrange("p b g -> p (b g)")
        pe.wait_ge(constants, 3)
        pe.wait_ge(band_out, 2)
        pe.wait_ge(loaded, 32)
        pipelined(pe, TILES, [(0, scores), (2, turn), (3, product), (4, project)])

    @block.scalar
    def _(act):
        def take_query(n, u):
            at_least(act, scores_done, n - 1)
            nc.scalar.activation(query[:, u, :], q_t[:, bass.ds(n * TILE, TILE)], ACT.Copy).then_inc(query_in, 1)

        def exponential(n, u):
            act.wait_ge(neg_done, n + 1)
            at_least(act, turned, n - 1)
            at_least(act, inv_done, n - 1)
            nc.scalar.activation(probs[:, u, 0:COLS], score_ps[:, u, 0:COLS], ACT.Exp, bias=neg_max[:, u:u + 1],
                                 scale=SCALE, accum_out=row_sum[:, u:u + 1]).then_inc(exp_done, 1)

        def copy_mixed(n, u):
            act.wait_ge(mixed_done, n + 1)
            at_least(act, out_done, n - 1)
            nc.scalar.activation(mixed[:, u, :], mixed_ps[:, u, 0:TILE], ACT.Copy).then_inc(mixed_out, 1)

        act.wait_ge(constants, 3)
        pipelined(act, TILES, [(0, take_query), (2, exponential), (4, copy_mixed)])

    @block.vector
    def _(dve):
        def largest(n, u):
            dve.wait_ge(scores_done, n + 1)
            nc.vector.tensor_reduce(row_max[:, u:u + 1], score_ps[:, u, 0:COLS], AX, ALU.max).then_inc(max_done, 1)
            dve.wait_ge(max_done, n + 1)
            at_least(dve, exp_done, n - 1)
            nc.vector.tensor_scalar(neg_max[:, u:u + 1], row_max[:, u:u + 1], NEG / 10, -SCALE, ALU.max, ALU.mult)\
                .then_inc(neg_done, 1)

        def normalise(n, u):
            dve.wait_ge(exp_done, n + 1)
            nc.vector.tensor_scalar(row_inv[:, u:u + 1], row_sum[:, u:u + 1], 1e-30, None, ALU.max)\
                .then_inc(sum_safe, 1)
            dve.wait_ge(sum_safe, n + 1)
            nc.vector.reciprocal(row_inv[:, u:u + 1], row_inv[:, u:u + 1]).then_inc(inv_done, 1)
            dve.wait_ge(inv_done, n + 1)
            nc.vector.tensor_scalar(probs[:, u, 0:COLS], probs[:, u, 0:COLS], row_inv[:, u:u + 1], None,
                                    ALU.mult).then_inc(probs_done, 1)

        def copy_turned(n, u):
            dve.wait_ge(turned, n + 1)
            at_least(dve, mixed_done, n - 1)
            nc.vector.tensor_copy(weights_t[:, u, :, :].rearrange("p x n -> p (x n)"),
                                  turned_ps[:, u, 0:3 * TILE]).then_inc(turned_out, 1)

        def add(n, u):
            dve.wait_ge(out_done, n + 1)
            at = resid[:, bass.ds(n * TILE, TILE)]
            nc.vector.scalar_tensor_tensor(at, out_ps[:, u, 0:TILE], bo[:, 0:1], at, ALU.add, ALU.add)\
                .then_inc(added, 1)

        nc.vector.tensor_copy(ident_half[:, :], ident[0:TILE, 0:TILE]).then_inc(band_out, 1)
        dve.wait_ge(band_in, 16)
        nc.vector.tensor_copy(band[:, :], band_full[:, :]).then_inc(band_out, 1)
        dve.wait_ge(loaded, 32)
        pipelined(dve, TILES, [(1, normalise), (0, largest), (2, copy_turned), (4, add)])


def expert_choice(nc, ctx, resid, io, ident, mean_w, eps):
    E = 64
    HID = io["weight1"].shape[2]
    KCH = HID // C
    GROUP = 4
    PAIRS = B // 2
    sb, ps, sem = allocators(nc, ctx, "expert")
    z = sb("z", [TILE, TILES, C])
    weights = sb("weights", [C, PAIRS, N])
    exp_sum = sb("exp_sum", [C, PAIRS])
    bias2 = sb("bias2", [C, E])
    biases = sem("biases")
    pooled_t = sb("pooled_t", [C, B, E])

    with ExitStack() as first_half:
        logits = allocators(nc, first_half, "expert_gate")[0]("logits", [C, B, N])
        with ExitStack() as own:
            norm = Norm(nc, own, "expert", resid, mean_w, eps)
            sb1, ps1, sem1 = allocators(nc, own, "expert_in")
            gate = sb1("gate", [C, 2, E])
            gate_b = sb1("gate_b", [C, 1])
            turned_ps = ps1("turned_ps", [TILE, 2, 4, C])
            logit_ps = ps1("logit_ps", [C, 2, BANK])
            gate_in = sem1("gate_in")
            turned = sem1("turned")
            z_out = sem1("z_out")
            logit_done = sem1("logit_done")
            logit_out = sem1("logit_out")
            block = own.enter_context(nc.Block())

            @block.sync
            def _(sp):
                for h in range(2):
                    sp.dma_start(gate[:, h, :], io["gate_w"]).then_inc(gate_in, 16)
                    sp.dma_start(gate_b[h * E:(h + 1) * E, :], io["gate_b"]).then_inc(gate_in, 16)
                sp.dma_start(bias2[:, :], io["bias2"]).then_inc(biases, 16)

            @block.tensor
            def _(pe):
                pe.wait_ge(gate_in, 64)

                def project(i, u):
                    pe.wait_ge(norm.normed_done, i + 1)
                    at_least(pe, logit_out, i - 1)
                    nc.tensor.matmul(logit_ps[:, u, 0:CHUNK], gate[:, :, :].rearrange("p h e -> p (h e)"),
                                     norm.normed[:, u, :], start=True, stop=True).then_inc(logit_done, 1)
                    at_least(pe, z_out, i - 1)
                    for t in range(4):
                        mm = nc.tensor.transpose(turned_ps[:, u, t, :], norm.normed[:, u, t * TILE:(t + 1) * TILE],
                                                 ident[:, :])
                    mm.then_inc(turned, 1)
                norm.tensor_steps(pe, project)

            @block.vector
            def _(dve):
                def copy_out(i, u):
                    dve.wait_ge(turned, i + 1)
                    nc.vector.tensor_copy(z[:, bass.ds(i * 4, 4), :], turned_ps[:, u, :, :]).then_inc(z_out, 1)
                norm.vector_steps(dve, ((turned, 1),), copy_out)

            @block.scalar
            def _(act):
                nc.scalar.preload_act_table_set("natural_log_exp_and_others")
                act.wait_ge(gate_in, 64)
                flat = logits[:, :, :].rearrange("p b n -> p (b n)")

                def copy_out(i, u):
                    act.wait_ge(logit_done, i + 1)
                    nc.scalar.activation(flat[:, bass.ds(i * CHUNK, CHUNK)], logit_ps[:, u, 0:CHUNK], ACT.Identity,
                                         bias=gate_b[:, 0:1]).then_inc(logit_out, 1)
                norm.scalar_steps(act, copy_out)

        with ExitStack() as own:
            sb1, _, sem1 = allocators(nc, own, "expert_soft")
            largest = sb1("largest", [C, B])
            max_done = sem1("max_done")
            neg_done = sem1("neg_done")
            block = own.enter_context(nc.Block())

            @block.vector
            def _(dve):
                for b in range(B):
                    nc.vector.tensor_reduce(largest[:, b:b + 1], logits[:, b, :], AX, ALU.max).then_inc(max_done, 1)
                    dve.wait_ge(max_done, b + 1)
                    nc.vector.tensor_scalar(largest[:, b:b + 1], largest[:, b:b + 1], -1.0, None, ALU.mult)\
                        .then_inc(neg_done, 1)

            @block.scalar
            def _(act):
                for b in range(B):
                    rows = slice(b % 2 * E, b % 2 * E + E)
                    act.wait_ge(neg_done, b + 1)
                    nc.scalar.activation(weights[rows, b // 2, :], logits[rows, b, :], ACT.Exp,
                                         bias=largest[rows, b:b + 1], accum_out=exp_sum[rows, b // 2:b // 2 + 1])

    with ExitStack() as own:
        sb1, ps1, sem1 = allocators(nc, own, "expert_top")
        rest = sb1("rest", [C, N])
        top = sb1("top", [C, 8])
        exp_inv = sb1("exp_inv", [C, PAIRS])
        chunk = sb1("chunk", [C, 2, CHUNK])
        by_token = sb1("by_token", [TILE, 2, 4, C])
        pooled = sb1("pooled", [C, PAIRS, 2 * C])
        own_half = sb1("own_half", [C, PAIRS, C])
        turned_ps = ps1("turned_ps", [TILE, 2, 4, C])
        pooled_ps = ps1("pooled_ps", [C, 2, BANK])
        pooled_t_ps = ps1("pooled_t_ps", [C, BANK])
        zeroed = sem1("zeroed")
        chain = sem1("chain")
        weights_done = sem1("weights_done")
        staged = sem1("staged")
        turned = sem1("turned")
        by_token_out = sem1("by_token_out")
        pooled_done = sem1("pooled_done")
        pooled_out = sem1("pooled_out")
        half_out = sem1("half_out")
        pooled_turned = sem1("pooled_turned")
        STEPS = PAIRS * CPI
        block = own.enter_context(nc.Block())

        @block.gpsimd
        def _(pool):
            nc.gpsimd.memset(pooled[:, :, :], 0.0).then_inc(zeroed, 1)

        @block.vector
        def _(dve):
            links = 0
            for m in range(PAIRS):
                w = weights[:, m, :]
                for op in (
                    lambda: nc.vector.max(top[:, :], w),
                    lambda: nc.vector.match_replace(rest[:, :], top[:, :], w, 0.0),
                    lambda: nc.vector.scalar_tensor_tensor(w, rest[:, :], -1.0, w, ALU.mult, ALU.add),
                    lambda: nc.vector.reciprocal(exp_inv[:, m:m + 1], exp_sum[:, m:m + 1]),
                ):
                    op().then_inc(chain, 1)
                    links += 1
                    dve.wait_ge(chain, links)
                nc.vector.tensor_scalar(w, w, exp_inv[:, m:m + 1], None, ALU.mult).then_inc(weights_done, 1)

            def copy_turned(i, u):
                dve.wait_ge(turned, i + 1)
                at_least(dve, pooled_done, i - 1)
                nc.vector.tensor_copy(by_token[:, u, :, :], turned_ps[:, u, :, :]).then_inc(by_token_out, 1)

            def add(i, u):
                dve.wait_ge(pooled_done, i + 1)
                at_least(dve, pooled_out, i)
                at = pooled[:, bass.ds(i // CPI, 1), :].rearrange("p a c -> p (a c)")
                nc.vector.tensor_tensor(at, at, pooled_ps[:, u, 0:2 * C], ALU.add).then_inc(pooled_out, 1)
            dve.wait_ge(zeroed, 1)
            pipelined(dve, STEPS, [(1, copy_turned), (2, add)])
            dve.wait_ge(pooled_out, STEPS)
            for h in range(2):
                rows = slice(h * E, h * E + E)
                nc.vector.tensor_copy(own_half[rows, :, :], pooled[rows, :, h * C:(h + 1) * C]).then_inc(half_out, 1)
            dve.wait_ge(pooled_turned, 1)
            nc.vector.tensor_copy(pooled_t[:, :, :].rearrange("p b e -> p (b e)"), pooled_t_ps[:, 0:B * E])

        @block.scalar
        def _(act):
            flat = weights[:, :, :].rearrange("p m n -> p (m n)")
            act.wait_ge(weights_done, PAIRS)

            def stage(i, u):
                at_least(act, turned, i - 1)
                nc.scalar.activation(chunk[:, u, :], flat[:, bass.ds(i * CHUNK, CHUNK)], ACT.Copy).then_inc(staged, 1)
            pipelined(act, STEPS, [(0, stage)])

        @block.tensor
        def _(pe):
            def turn(i, u):
                pe.wait_ge(staged, i + 1)
                at_least(pe, by_token_out, i - 1)
                for t in range(4):
                    mm = nc.tensor.transpose(turned_ps[:, u, t, :], chunk[:, u, t * TILE:(t + 1) * TILE], ident[:, :])
                mm.then_inc(turned, 1)

            def pool_tokens(i, u):
                pe.wait_ge(by_token_out, i + 1)
                at_least(pe, pooled_out, i - 1)
                for t in range(4):
                    tokens = z[:, bass.DynSlice(i * 4 + i // CPI * TPI + t, 2, step=TPI), :]
                    mm = nc.tensor.matmul(pooled_ps[:, u, 0:2 * C].rearrange("p (h c) -> p h c", h=2),
                                          by_token[:, u, t, :], tokens, start=(t == 0), stop=(t == 3))
                mm.then_inc(pooled_done, 1)
            pipelined(pe, STEPS, [(1, turn), (2, pool_tokens)])
            pe.wait_ge(half_out, 2)
            for m in range(PAIRS):
                mm = nc.tensor.transpose(pooled_t_ps[:, m * C:(m + 1) * C], own_half[:, m, :], ident[:, :])
            mm.then_inc(pooled_turned, 1)

    outputs_t = sb("outputs_t", [C, B, E])
    with ExitStack() as own:
        sb1, ps1, sem1 = allocators(nc, own, "expert_mlp")
        ROWS = C // GROUP
        w1 = sb1("w1", [C, 2, GROUP, HID])
        w2 = sb1("w2", [C, 2, GROUP, KCH, C])
        bias1 = sb1("bias1", [C, 2, HID])
        tokens = sb1("tokens", [C, 2, GROUP, ROWS])
        biased = sb1("biased", [C, 2, HID])
        hidden = sb1("hidden", [C, 2, HID])
        hidden_t = sb1("hidden_t", [C, 2, KCH, C])
        output = sb1("output", [C, 2, C])
        hidden_ps = ps1("hidden_ps", [C, 2, BANK])
        hidden_t_ps = ps1("hidden_t_ps", [C, 2, KCH, C])
        out_ps = ps1("out_ps", [C, 2, BANK])
        out_t_ps = ps1("out_t_ps", [C, 2, BANK])
        zeroed = sem1("zeroed")
        w1_in = [sem1(f"w1_in{u}") for u in range(2)]
        bias1_in = [sem1(f"bias1_in{u}") for u in range(2)]
        w2_in = [sem1(f"w2_in{u}") for u in range(2)]
        tokens_in = sem1("tokens_in")
        hidden_done = sem1("hidden_done")
        biased_done = sem1("biased_done")
        gelu_done = sem1("gelu_done")
        hidden_turned = sem1("hidden_turned")
        hidden_t_out = sem1("hidden_t_out")
        out_done = sem1("out_done")
        out_out = sem1("out_out")
        out_turned = sem1("out_turned")
        taken = sem1("taken")
        STEPS = E // GROUP
        block = own.enter_context(nc.Block())

        @block.gpsimd
        def _(pool):
            nc.gpsimd.memset(tokens[:, :, :, :], 0.0).then_inc(zeroed, 1)
            nc.gpsimd.memset(bias1[:, :, :], 0.0).then_inc(zeroed, 1)

        @block.sync
        def _(sp):
            def load_up(i, u):
                at_least(sp, hidden_done, i - 1)
                sp.dma_start(w1[:, u, :, :], io["weight1"][bass.ds(i * GROUP, GROUP), 0:C, :]
                             .rearrange("e d h -> d e h")).then_inc(w1_in[u], 16)
                at_least(sp, biased_done, i - 1)
                for e in range(GROUP):
                    sp.dma_start(bias1[e * ROWS:e * ROWS + B, u, :],
                                 io["weight1"][bass.ds(i * GROUP + e, 1), C, :].to_broadcast([B, HID]))\
                      .then_inc(bias1_in[u], 16)

            def load_down(i, u):
                at_least(sp, out_done, i - 1)
                sp.dma_start(w2[:, u, :, :, :].rearrange("p e k o -> p e (k o)"),
                             io["weight2"][bass.ds(i * GROUP, GROUP), 0:HID, :]
                             .rearrange("e (p k) o -> p e (k o)", k=KCH)).then_inc(w2_in[u], 16)
            sp.wait_ge(zeroed, 2)
            pipelined(sp, STEPS, [(0, load_up), (2, load_down)])

        @block.tensor
        def _(pe):
            def up(i, u):
                pe.wait_ge(w1_in[u], 8 * (i - u) + 16)
                pe.wait_ge(tokens_in, i + 1)
                at_least(pe, biased_done, i - 1)
                for e in range(GROUP):
                    mm = nc.tensor.matmul(hidden_ps[e * ROWS:(e + 1) * ROWS, u, :], tokens[:, u, e, :],
                                          w1[:, u, e, :], start=True, stop=True)
                mm.then_inc(hidden_done, 1)

            def turn_hidden(i, u):
                pe.wait_ge(gelu_done, i + 1)
                at_least(pe, hidden_t_out, i - 1)
                for k in range(KCH):
                    mm = nc.tensor.transpose(hidden_t_ps[:, u, k, :], hidden[:, u, k:HID:KCH], ident[:, :])
                mm.then_inc(hidden_turned, 1)

            def down(i, u):
                pe.wait_ge(w2_in[u], 8 * (i - u) + 16)
                pe.wait_ge(hidden_t_out, i + 1)
                at_least(pe, out_out, i - 1)
                for e in range(GROUP):
                    rows = slice(e * ROWS, (e + 1) * ROWS)
                    for k in range(KCH):
                        mm = nc.tensor.matmul(out_ps[rows, u, 0:C], hidden_t[:, u, k, rows], w2[:, u, e, k, :],
                                              start=(k == 0), stop=(k == KCH - 1))
                mm.then_inc(out_done, 1)

            def turn_output(i, u):
                pe.wait_ge(out_out, i + 1)
                at_least(pe, taken, i - 1)
                nc.tensor.transpose(out_t_ps[:, u, 0:C], output[:, u, :], ident[:, :]).then_inc(out_turned, 1)
            pipelined(pe, STEPS, [(1, up), (2, turn_hidden), (3, down), (4, turn_output)])

        @block.scalar
        def _(act):
            by_expert = pooled_t[:, :, :].rearrange("p b e -> p e b")
            act.wait_ge(zeroed, 2)

            def take_tokens(i, u):
                at_least(act, hidden_done, i - 1)
                nc.scalar.activation(tokens[:, u, :, 0:B], by_expert[:, bass.ds(i * GROUP, GROUP), :], ACT.Copy)\
                    .then_inc(tokens_in, 1)

            def gelu(i, u):
                act.wait_ge(biased_done, i + 1)
                at_least(act, hidden_turned, i - 1)
                nc.scalar.activation(hidden[:, u, :], biased[:, u, :], ACT.Gelu).then_inc(gelu_done, 1)

            def copy_output(i, u):
                act.wait_ge(out_done, i + 1)
                at_least(act, out_turned, i - 1)
                nc.scalar.activation(output[:, u, :], out_ps[:, u, 0:C], ACT.Copy).then_inc(out_out, 1)
            pipelined(act, STEPS, [(0, take_tokens), (1, gelu), (3, copy_output)])

        @block.vector
        def _(dve):
            dve.wait_ge(biases, 16)

            def add_bias(i, u):
                dve.wait_ge(bias1_in[u], 32 * (i - u) + 64)
                dve.wait_ge(hidden_done, i + 1)
                at_least(dve, gelu_done, i - 1)
                nc.vector.tensor_tensor(biased[:, u, :], hidden_ps[:, u, :], bias1[:, u, :], ALU.add)\
                    .then_inc(biased_done, 1)

            def copy_hidden(i, u):
                dve.wait_ge(hidden_turned, i + 1)
                at_least(dve, out_done, i - 1)
                nc.vector.tensor_copy(hidden_t[:, u, :, :], hidden_t_ps[:, u, :, :]).then_inc(hidden_t_out, 1)

            def take_output(i, u):
                dve.wait_ge(out_turned, i + 1)
                nc.vector.tensor_tensor(outputs_t[:, :, bass.ds(i * GROUP, GROUP)].rearrange("p b e -> p e b"),
                                        out_t_ps[:, u, 0:C].rearrange("p (e r) -> p e r", e=GROUP)[:, :, 0:B],
                                        bias2[:, bass.ds(i * GROUP, GROUP)].unsqueeze(2)
                                        .to_broadcast([C, GROUP, B]), ALU.add).then_inc(taken, 1)
            pipelined(dve, STEPS, [(1, add_bias), (2, copy_hidden), (4, take_output)])

    with ExitStack() as own:
        sb1, ps1, sem1 = allocators(nc, own, "expert_out")
        outputs = sb1("outputs", [C, PAIRS, 2, C])
        turned_ps = ps1("turned_ps", [C, BANK])
        back_ps = ps1("back_ps", [C, 2, BANK])
        zeroed = sem1("zeroed")
        turned = sem1("turned")
        outputs_out = sem1("outputs_out")
        back_done = sem1("back_done")
        added = sem1("added")
        block = own.enter_context(nc.Block())

        @block.gpsimd
        def _(pool):
            nc.gpsimd.memset(outputs[:, :, :, :], 0.0).then_inc(zeroed, 1)

        @block.tensor
        def _(pe):
            for m in range(PAIRS):
                mm = nc.tensor.transpose(turned_ps[:, m * C:(m + 1) * C],
                                         outputs_t[:, 2 * m:2 * m + 2, :].rearrange("p h e -> p (h e)"), ident[:, :])
            mm.then_inc(turned, 1)
            pe.wait_ge(outputs_out, 2)
            for m in range(PAIRS):
                def step(c, first):
                    for h in range(2):
                        n = (m * CPI + c) * 2 + h
                        if not first:
                            pe.wait_ge(added, n - 1)
                        nc.tensor.matmul(back_ps[:, h, 0:CHUNK], outputs[:, m, h, :],
                                         weights[:, m, bass.ds(c * CHUNK, CHUNK)], start=True, stop=True)\
                            .then_inc(back_done, 1)
                step(0, m == 0)
                with pe.Fori(1, CPI) as c:
                    step(c, False)

        @block.vector
        def _(dve):
            dve.wait_ge(zeroed, 1)
            dve.wait_ge(turned, 1)
            for h in range(2):
                rows = slice(h * E, h * E + E)
                nc.vector.tensor_copy(outputs[rows, :, h, :],
                                      turned_ps[rows, 0:PAIRS * C].rearrange("p (m c) -> p m c", m=PAIRS))\
                    .then_inc(outputs_out, 1)
            for m in range(PAIRS):
                with dve.Fori(0, CPI) as c:
                    for h in range(2):
                        dve.wait_ge(back_done, (m * CPI + c) * 2 + h + 1)
                        at = resid[:, bass.ds((2 * m + h) * N + c * CHUNK, CHUNK)]
                        nc.vector.tensor_tensor(at, at, back_ps[:, h, 0:CHUNK], ALU.add).then_inc(added, 1)


def self_attention(nc, ctx, resid, io, ident, mean_w, eps):
    SHIFT = -52.0
    sb, ps, sem = allocators(nc, ctx, "self")
    PARTS = 2
    zt_dram = nc.dram_tensor("self_zt", [PARTS, C, TOKENS], FP32).ap()
    z_dram = nc.dram_tensor("self_z", [TILES, TILE, PARTS, C], FP32).ap()

    with ExitStack() as own:
        norm = Norm(nc, own, "self", resid, mean_w, eps)
        sb1, ps1, sem1 = allocators(nc, own, "self_in")
        zt = sb1("zt", [C, 2, PARTS, CHUNK], FP32R)
        z = sb1("z", [TILE, 2, 4, PARTS, C], FP32R)
        turned_ps = ps1("turned_ps", [TILE, 2, 4, C])
        one = sb1("one", [C, 1])
        one_done = sem1("one_done")
        turned = sem1("turned")
        zt_hi_out = sem1("zt_hi_out")
        zt_out = sem1("zt_out")
        z_hi_out = sem1("z_hi_out")
        z_out = sem1("z_out")
        zt_stored = [sem1(f"zt_stored{u}") for u in range(2)]
        z_stored = [sem1(f"z_stored{u}") for u in range(2)]
        block = own.enter_context(nc.Block())

        @block.tensor
        def _(pe):
            def turn(i, u):
                pe.wait_ge(norm.normed_done, i + 1)
                at_least(pe, z_out, i - 1)
                for t in range(4):
                    mm = nc.tensor.transpose(turned_ps[:, u, t, :], norm.normed[:, u, t * TILE:(t + 1) * TILE],
                                             ident[:, :])
                mm.then_inc(turned, 1)
            norm.tensor_steps(pe, turn)

        @block.gpsimd
        def _(pool):
            def step(i, u, first, last):
                pool.wait_ge(norm.normed_done, i + 1)
                if not (isinstance(i, int) and i < 2):
                    pool.wait_ge(zt_stored[u], 8 * (i - u))
                nc.gpsimd.tensor_tensor(zt[:, u, 0, :], norm.normed[:, u, :], one[:, 0:1].to_broadcast([C, CHUNK]),
                                        ALU.mult).then_inc(zt_hi_out, 1)
            nc.gpsimd.memset(one[:, :], 1.0).then_inc(one_done, 1)
            pool.wait_ge(one_done, 1)
            paced(pool, CHUNKS, step)

        @block.scalar
        def _(act):
            nc.scalar.preload_act_table_set("natural_log_exp_and_others")

            def high(i, u):
                act.wait_ge(turned, i + 1)
                if not (isinstance(i, int) and i < 2):
                    act.wait_ge(z_stored[u], 8 * (i - u))
                nc.scalar.activation(z[:, u, :, 0, :], turned_ps[:, u, :, :], ACT.Copy).then_inc(z_hi_out, 1)
            norm.scalar_steps(act, high)

        @block.vector
        def _(dve):
            def zt_low(i, u):
                dve.wait_ge(zt_hi_out, i + 1)
                nc.vector.tensor_tensor(zt[:, u, 1, :], norm.normed[:, u, :], zt[:, u, 0, :].bitcast(FP32),
                                        ALU.subtract).then_inc(zt_out, 1)

            def z_low(i, u):
                dve.wait_ge(z_hi_out, i + 1)
                nc.vector.tensor_tensor(z[:, u, :, 1, :], turned_ps[:, u, :, :], z[:, u, :, 0, :].bitcast(FP32),
                                        ALU.subtract).then_inc(z_out, 1)
            norm.vector_steps(dve, ((turned, 1), (zt_out, 1)), z_low, more=zt_low)

        @block.sync
        def _(sp):
            def store_zt(i, u):
                sp.wait_ge(zt_out, i + 1)
                sp.dma_start(zt_dram[:, :, bass.ds(i * CHUNK, CHUNK)].rearrange("x c n -> c x n"),
                             zt[:, u, :, :].bitcast(FP32)).then_inc(zt_stored[u], 16)

            def store_z(i, u):
                sp.wait_ge(z_out, i + 1)
                sp.dma_start(z_dram[bass.ds(i * 4, 4), :, :, :].rearrange("t q x c -> q t (x c)"),
                             z[:, u, :, :, :].rearrange("q t x c -> q t (x c)").bitcast(FP32))\
                  .then_inc(z_stored[u], 16)
            pipelined(sp, CHUNKS, [(0, store_zt), (1, store_z)])
            for u in range(2):
                sp.wait_ge(zt_stored[u], 16 * (CHUNKS // 2))
                sp.wait_ge(z_stored[u], 16 * (CHUNKS // 2))

    LOTS = ((0, 4), (4, 3))
    PRODUCTS = ((0, 0), (0, 1), (1, 0))
    SPARE = 3
    query_t = sb("query_t", [C, PARTS, 2 * N], FP32R)
    key_t = sb("key_t", [C, 2, PARTS, TILE], FP32R)
    key = sb("key", [TILE, 2, PARTS, C], FP32R)
    whole = sb("whole", [TILE, 4, CHUNK])
    probs = sb("probs", [TILE, 2, PARTS, 4, CHUNK], FP32R)
    sums = sb("sums", [TILE, 2, 4])
    lot_sum = sb("lot_sum", [TILE, 2, TPI])
    total = sb("total", [TILE, TPI])
    inverse = sb("inverse", [TILE, TPI])
    diag = sb("diag", [TILE, 4, TILE])
    raw = sb("raw", [C, 2 * N])
    part = sb("part", [C, CHUNK])
    shift = sb("shift", [C, 1])
    ones = sb("ones", [TILE, C])
    zeros = sb("zeros", [TILE, CHUNK], BF16)
    score_ps = ps("score_ps", [C, 4, BANK])
    out_ps = ps("out_ps", [C, 4, BANK])
    constants = sem("constants")
    query_in = sem("query_in")
    key_t_in = [sem(f"key_t_in{u}") for u in range(2)]
    key_in = [sem(f"key_in{u}") for u in range(2)]
    scores_done = sem("scores_done")
    exp_done = sem("exp_done")
    hi_done = sem("hi_done")
    split_done = sem("split_done")
    product_done = sem("product_done")
    lot_done = sem("lot_done")
    summed = sem("summed")
    raw_out = sem("raw_out")
    total_done = sem("total_done")
    inverse_done = sem("inverse_done")
    diag_done = sem("diag_done")
    spread_done = sem("spread_done")
    scaled = sem("scaled")
    added = sem("added")
    block = ctx.enter_context(nc.Block())

    def images(eng, image, finish):
        image(0, False)
        with eng.Fori(1, B) as b:
            image(b, True)
        for c in range(CPI):
            finish(B - 1, c)

    def steps(eng, step, rest):
        head = CPI + 1 if rest else 2
        for j in range(head):
            step(j, j % 2, j == 0, False)
            if rest and j < CPI:
                rest(j)
        with eng.Fori(head // 2, TPI // 2 - 1) as k:
            step(2 * k, 0, False, False)
            step(2 * k + 1, 1, False, False)
        step(TPI - 2, 0, False, False)
        step(TPI - 1, 1, False, True)

    def before(b, lot):
        return b * (TPI * CPI) + lot * TPI * LOTS[0][1]

    def before_last(b, lot, c=-1):
        width = LOTS[1 - lot][1]
        return before(b, lot) - width + min(c + 1, width)

    def tiles_in(b, lot, j, u):
        return (b * 2 + lot) * (TPI * 8) + (j - u) * 8 + 16

    @block.gpsimd
    def _(pool):
        nc.gpsimd.memset(shift[:, :], SHIFT).then_inc(constants, 1)
        nc.gpsimd.memset(ones[:, :], 1.0).then_inc(constants, 1)
        nc.gpsimd.memset(zeros[:, :], 0.0).then_inc(constants, 1)

    @block.sync
    def _(sp):
        def load_queries(b, c):
            sp.dma_start(query_t[:, :, bass.ds(b % 2 * N + c * CHUNK, CHUNK)].bitcast(FP32),
                         zt_dram[:, :, bass.ds(b * N + c * CHUNK, CHUNK)].rearrange("x c n -> c x n"))\
              .then_inc(query_in, 16)

        def image(b, more):
            for lot, (c0, n) in enumerate(LOTS):
                def step(j, u, first, last):
                    if isinstance(j, int) and j < 2:
                        used = before_last(b, lot) if j == 0 else before(b, lot)
                    else:
                        used = before(b, lot) + (j - 1) * n
                    at_least(sp, scores_done, used)
                    sp.dma_start(key_t[:, u, :, :].bitcast(FP32),
                                 zt_dram[:, :, bass.ds(b * N + j * TILE, TILE)].rearrange("x c n -> c x n"))\
                      .then_inc(key_t_in[u], 16)
                    at_least(sp, product_done, used)
                    sp.dma_start(key[:, u, :, :].rearrange("q x c -> q (x c)").bitcast(FP32),
                                 z_dram[bass.ds(b * TPI + j, 1), :, :, :].rearrange("t q x c -> (t q) (x c)"))\
                      .then_inc(key_in[u], 16)

                def load_next(c):
                    at_least(sp, scores_done, before(b, 0))
                    load_queries(b + 1, c)
                steps(sp, step, load_next if more and lot == 0 else None)
        for c in range(CPI):
            load_queries(0, c)
        image(0, True)
        with sp.Fori(1, B - 1) as b:
            image(b, True)
        image(B - 1, False)

    def spread(pe, b, c):
        pe.wait_ge(diag_done, b * CPI + c + 1)
        at_least(pe, scaled, b * CPI + c)
        nc.tensor.matmul(score_ps[:, SPARE, 0:CHUNK], ones[:, :], diag[:, :, :].rearrange("p t n -> p (t n)"),
                         start=True, stop=True).then_inc(spread_done, 1)

    @block.tensor
    def _(pe):
        pe.wait_ge(constants, 3)

        def image(b, rest):
            pe.wait_ge(query_in, b * (16 * CPI) + 16 * CPI)
            for lot, (c0, n) in enumerate(LOTS):
                def scores(j, u, c):
                    pe.wait_ge(key_t_in[u], tiles_in(b, lot, j, u))
                    if isinstance(j, int) and j == 0:
                        at_least(pe, exp_done, before_last(b, lot, c))
                        if lot == 0 and c == SPARE:
                            at_least(pe, scaled, (b - 1) * CPI)
                    else:
                        pe.wait_ge(exp_done, before(b, lot) + (j - 1) * n + c + 1)
                    for x, (k, q) in enumerate(PRODUCTS):
                        mm = nc.tensor.matmul(score_ps[0:TILE, c, 0:CHUNK], key_t[:, u, k, :],
                                              query_t[:, q, bass.ds(b % 2 * N + (c0 + c) * CHUNK, CHUNK)],
                                              start=(x == 0), stop=(x == len(PRODUCTS) - 1))
                    mm.then_inc(scores_done, 1)

                def product(j, u, c):
                    pe.wait_ge(key_in[u], tiles_in(b, lot, j, u))
                    pe.wait_ge(split_done, before(b, lot) + j * n + c + 1)
                    for k, q in PRODUCTS:
                        mm = nc.tensor.matmul(out_ps[:, c, 0:CHUNK], key[:, u, k, :], probs[:, u, q, c, :],
                                              start=False, stop=False)
                    mm.then_inc(product_done, 1)

                def step(j, u, first, last):
                    if first:
                        for c in range(n):
                            scores(j, u, c)
                        at_least(pe, raw_out, b * CPI + c0)
                        for c in range(n):
                            nc.tensor.matmul(out_ps[:, c, 0:CHUNK], zeros[:, 0:C], zeros[:, :], start=True, stop=False)
                    for c in range(n):
                        if not last:
                            scores(j + 1, 1 - u, c)
                        product(j, u, c)
                    if last:
                        for c in range(n):
                            mm = nc.tensor.matmul(out_ps[:, c, 0:CHUNK], zeros[:, 0:C], zeros[:, :],
                                                  start=False, stop=True)
                        mm.then_inc(lot_done, 1)
                steps(pe, step, (lambda c: spread(pe, b - 1, c)) if rest and lot == 1 else None)
        images(pe, image, lambda b, c: spread(pe, b, c))

    @block.scalar
    def _(act):
        act.wait_ge(constants, 3)

        def image(b, rest):
            for lot, (c0, n) in enumerate(LOTS):
                def step(j, u, first, last):
                    for c in range(n):
                        act.wait_ge(scores_done, before(b, lot) + j * n + c + 1)
                        if isinstance(j, int) and j == 0:
                            at_least(act, split_done, before_last(b, lot, c))
                        else:
                            act.wait_ge(split_done, before(b, lot) + (j - 1) * n + c + 1)
                        if c == 0:
                            at_least(act, summed, (b * 2 + lot) * TPI + j - 1)
                        nc.scalar.activation(whole[:, c, :], score_ps[0:TILE, c, 0:CHUNK], ACT.Exp,
                                             bias=shift[0:TILE, 0:1],
                                             accum_out=sums[:, u, c:c + 1]).then_inc(exp_done, 1)
                paced(act, TPI, step)
                act.wait_ge(lot_done, b * 2 + lot + 1)
                for c in range(2, n):
                    nc.scalar.activation(raw[:, bass.ds(b % 2 * N + (c0 + c) * CHUNK, CHUNK)],
                                         out_ps[:, c, 0:CHUNK], ACT.Copy).then_inc(raw_out, 1)
        image(0, False)
        with act.Fori(1, B) as b:
            image(b, True)

    @block.vector
    def _(dve):
        def finish(b, c):
            at_least(dve, spread_done, b * CPI + c)
            nc.vector.tensor_tensor(diag[:, :, :], ident[0:TILE, 0:TILE].unsqueeze(1).to_broadcast([TILE, 4, TILE]),
                                    inverse[:, 4 * c:4 * c + 4].unsqueeze(2).to_broadcast([TILE, 4, TILE]),
                                    ALU.mult).then_inc(diag_done, 1)
            dve.wait_ge(spread_done, b * CPI + c + 1)
            at_least(dve, added, b * CPI + c)
            nc.vector.tensor_tensor(part[:, :], raw[:, bass.ds(b % 2 * N + c * CHUNK, CHUNK)],
                                    score_ps[:, SPARE, 0:CHUNK], ALU.mult).then_inc(scaled, 1)
            dve.wait_ge(scaled, b * CPI + c + 1)
            at = resid[:, bass.ds(b * N + c * CHUNK, CHUNK)]
            nc.vector.tensor_tensor(at, at, part[:, :], ALU.add).then_inc(added, 1)

        def image(b, rest):
            for lot, (c0, n) in enumerate(LOTS):
                def step(j, u, first, last):
                    for c in range(n):
                        done = before(b, lot) + j * n + c
                        dve.wait_ge(exp_done, done + 1)
                        if isinstance(j, int) and j < 2:
                            at_least(dve, product_done, before_last(b, lot, -1 if j == 0 else c))
                        else:
                            dve.wait_ge(product_done, before(b, lot) + (j - 2) * n + c + 1)
                        nc.vector.tensor_copy(probs[:, u, 0, c, :], whole[:, c, :]).then_inc(hi_done, 1)
                        dve.wait_ge(hi_done, done + 1)
                        nc.vector.tensor_tensor(probs[:, u, 1, c, :], whole[:, c, :],
                                                probs[:, u, 0, c, :].bitcast(FP32), ALU.subtract)\
                            .then_inc(split_done, 1)
                    if first:
                        at_least(dve, total_done, b)
                    nc.vector.tensor_reduce(lot_sum[:, lot, bass.ds(j, 1)], sums[:, u, 0:n], AX, ALU.add)\
                        .then_inc(summed, 1)
                steps(dve, step, (lambda c: finish(b - 1, c)) if rest and lot == 1 else None)
                dve.wait_ge(lot_done, b * 2 + lot + 1)
                for c in range(2):
                    nc.vector.tensor_copy(raw[:, bass.ds(b % 2 * N + (c0 + c) * CHUNK, CHUNK)],
                                          out_ps[:, c, 0:CHUNK]).then_inc(raw_out, 1)
            dve.wait_ge(summed, b * (2 * TPI) + 2 * TPI)
            nc.vector.tensor_tensor(total[:, :], lot_sum[:, 0, :], lot_sum[:, 1, :], ALU.add).then_inc(total_done, 1)
            dve.wait_ge(total_done, b + 1)
            nc.vector.reciprocal(inverse[:, :], total[:, :]).then_inc(inverse_done, 1)
            dve.wait_ge(inverse_done, b + 1)
            dve.wait_ge(raw_out, b * CPI + CPI)
        images(dve, image, finish)


def recurrence(nc, ctx, resid, io, ident, mean_w, eps):
    SPAN = 64
    SPANS = N // SPAN
    COLS = TOKENS // SPAN
    WARM = 16
    SLACK = 2.0 ** -22
    sb, ps, sem = allocators(nc, ctx, "rnn")
    pre = sb("pre", [C, WARM + TOKENS])
    w = sb("w", [C, C])
    v = sb("v", [C, C])
    gamma = sb("gamma", [C, 1])
    beta = sb("beta", [C, 1])
    stats = sb("stats", [C, CHUNKS, 6])
    moments = sb("moments", [C, 2])
    factor = sb("factor", [C, 1])
    offset = sb("offset", [C, 1])
    loaded = sem("loaded")

    with ExitStack() as own:
        norm = Norm(nc, own, "rnn", resid, mean_w, eps)
        _, ps1, sem1 = allocators(nc, own, "rnn_in")
        wx_ps = ps1("wx_ps", [C, 2, BANK])
        wx_done = sem1("wx_done")
        pre_out = sem1("pre_out")
        stats_done = sem1("stats_done")
        chain = sem1("chain")
        log_done = sem1("log_done")
        block = own.enter_context(nc.Block())

        @block.sync
        def _(sp):
            for to, name in ((w, "rnn_w"), (v, "rnn_v"), (gamma, "rnn_gamma"), (beta, "rnn_beta")):
                sp.dma_start(to[:, :], io[name]).then_inc(loaded, 16)

        @block.gpsimd
        def _(pool):
            nc.gpsimd.memset(pre[:, 0:WARM], 0.0)

        @block.tensor
        def _(pe):
            pe.wait_ge(loaded, 64)

            def project(i, u):
                pe.wait_ge(norm.normed_done, i + 1)
                at_least(pe, pre_out, i - 1)
                nc.tensor.matmul(wx_ps[:, u, 0:CHUNK], w[:, :], norm.normed[:, u, :],
                                 start=True, stop=True).then_inc(wx_done, 1)
            norm.tensor_steps(pe, project)

        @block.scalar
        def _(act):
            nc.scalar.preload_act_table_set("natural_log_exp_and_others")

            def copy_out(i, u):
                act.wait_ge(wx_done, i + 1)
                nc.scalar.activation(pre[:, bass.ds(WARM + i * CHUNK, CHUNK)], wx_ps[:, u, 0:CHUNK], ACT.Copy)\
                    .then_inc(pre_out, 1)
            norm.scalar_steps(act, copy_out)
            act.wait_ge(chain, 1)
            nc.scalar.activation(factor[:, :], moments[:, 1:2], ACT.Ln, bias=eps[:, 0:1]).then_inc(log_done, 1)
            act.wait_ge(log_done, 1)
            nc.scalar.activation(factor[:, :], factor[:, :], ACT.Exp, scale=-0.5).then_inc(log_done, 1)

        @block.vector
        def _(dve):
            def statistics(i, u):
                dve.wait_ge(pre_out, i + 1)
                nc.vector.bn_stats(stats[:, bass.ds(i, 1), :].rearrange("p a s -> p (a s)"),
                                   pre[:, bass.ds(WARM + i * CHUNK, CHUNK)]).then_inc(stats_done, 1)
            norm.vector_steps(dve, ((wx_done, 1),), statistics, lag=7)
            dve.wait_ge(stats_done, CHUNKS)
            nc.vector.bn_aggr(moments[:, :], stats[:, :, :].rearrange("p a s -> p (a s)")).then_inc(chain, 1)
            dve.wait_ge(log_done, 2)
            dve.wait_ge(loaded, 64)
            nc.vector.tensor_tensor(factor[:, :], factor[:, :], gamma[:, :], ALU.mult).then_inc(chain, 1)
            dve.wait_ge(chain, 2)
            nc.vector.tensor_tensor(offset[:, :], moments[:, 0:1], factor[:, :], ALU.mult).then_inc(chain, 1)
            dve.wait_ge(chain, 3)
            nc.vector.tensor_tensor(offset[:, :], beta[:, :], offset[:, :], ALU.subtract).then_inc(chain, 1)
            dve.wait_ge(chain, 4)
            dve.wait_ge(pre_out, CHUNKS)
            nc.vector.tensor_scalar(pre[:, WARM:WARM + TOKENS], pre[:, WARM:WARM + TOKENS],
                                    factor[:, 0:1], offset[:, 0:1], ALU.mult, ALU.add)

    states = sb("states", [C, TOKENS])
    warm = sb("warm", [C, 2, COLS])
    start = sb("start", [C, COLS])
    ends = sb("ends", [C, COLS])
    apart = sb("apart", [C, COLS])
    apart_max = sb("apart_max", [C, 1])
    differs = sb("differs", [C, 1])
    ones = sb("ones", [C, 1])
    count = sb("count", [1, 1], mybir.dt.int32)
    HALVES = 2
    HALF = COLS // HALVES
    step_ps = ps("step_ps", [C, 2, HALVES, BANK])
    count_ps = ps("count_ps", [C, BANK])

    def inputs_at(t, h):
        return pre[:, bass.DynSlice(t + WARM + h * HALF * SPAN, HALF, step=SPAN)]

    def states_at(t, h):
        return states[:, bass.DynSlice(t + h * HALF * SPAN, HALF, step=SPAN)]

    def product(pe, sems, q, t, u, h, before, first):
        product_done, state_done = sems
        if not first:
            at_least(pe, state_done[h], q - 1)
        nc.tensor.matmul(step_ps[:, u, h, 0:HALF], ident[:, :], inputs_at(t, h), start=True, stop=False)
        at_least(pe, state_done[h], q)
        nc.tensor.matmul(step_ps[:, u, h, 0:HALF], v[:, :], before, start=False, stop=True)\
            .then_inc(product_done[h], 1)

    def sigmoid(act, sems, q, u, h, to):
        product_done, state_done = sems
        act.wait_ge(product_done[h], q + 1)
        nc.scalar.activation(to, step_ps[:, u, h, 0:HALF], ACT.Sigmoid).then_inc(state_done[h], 1)

    def half(x, h):
        return x[:, h * HALF:(h + 1) * HALF]

    def tensor_spans(pe, sems, base):
        def step(s, u, first, last):
            for h in range(HALVES):
                before = half(start, h) if first else states_at(s - 1, h)
                product(pe, sems, base + s, s, u, h, before, first)
        paced(pe, SPAN, step)

    def scalar_spans(act, sems, base):
        def step(s, u, first, last):
            for h in range(HALVES):
                sigmoid(act, sems, base + s, u, h, states_at(s, h))
        paced(act, SPAN, step)

    def without_first(dve, x, sem, count):
        dve.wait_ge(sem, count)
        return nc.vector.memset(x[:, bass.DynSlice(0, B, step=SPANS)], 0.0)

    sides = lambda n: ([sem(f"product_{n}{h}") for h in range(HALVES)], [sem(f"state_{n}{h}") for h in range(HALVES)])
    spans, again = sides("first"), sides("again")
    constants = sem("constants")
    warmed = sem("warmed")
    started = sem("started")
    compared = sem("compared")
    ends_out = sem("ends_out")
    count_done = sem("count_done")
    count_out = sem("count_out")
    restarted = sem("restarted")
    reloaded = sem("reloaded")
    added = sem("added")
    stored = sem("stored")
    PIECES = 2 * B
    PIECE = TOKENS // PIECES
    block = ctx.enter_context(nc.Block())

    @block.sync
    def _(sp):
        for k in range(PIECES):
            piece = slice(k * PIECE, (k + 1) * PIECE)
            sp.wait_ge(added, k + 1)
            sp.dma_start(io["out"][:, piece], resid[:, piece]).then_inc(stored, 16)
        sp.wait_ge(stored, 16 * PIECES)

    @block.gpsimd
    def _(pool):
        nc.gpsimd.memset(warm[:, :, :], 0.0).then_inc(constants, 1)
        nc.gpsimd.memset(ones[:, :], 1.0).then_inc(constants, 1)

    @block.tensor
    def _(pe):
        pe.wait_ge(constants, 2)

        def warm_up(q, u, first, last):
            for h in range(HALVES):
                product(pe, spans, q, q - WARM, u, h, half(warm[:, 1 - u, :], h), first)
        paced(pe, WARM, warm_up)
        pe.wait_ge(started, 2)
        tensor_spans(pe, spans, WARM)
        pe.wait_ge(compared, 4)
        nc.tensor.matmul(count_ps[0:1, 0:1], differs[:, :], ones[:, :], start=True, stop=True).then_inc(count_done, 1)
        pe.wait_ge(count_out, 1)
        wrong = pe.value_load(count[0:1, 0:1])
        with pe.If(wrong):
            with pe.Fori(0, SPANS - 1) as r:
                pe.wait_ge(restarted, r + 1)
                tensor_spans(pe, again, r * SPAN)

    @block.scalar
    def _(act):
        act.wait_ge(constants, 2)

        def warm_up(q, u, first, last):
            for h in range(HALVES):
                sigmoid(act, spans, q, u, h, half(warm[:, u, :], h))
        paced(act, WARM, warm_up)
        scalar_spans(act, spans, WARM)
        act.wait_ge(count_out, 1)
        wrong = act.value_load(count[0:1, 0:1])
        with act.If(wrong):
            with act.Fori(0, SPANS - 1) as r:
                scalar_spans(act, again, r * SPAN)

    @block.vector
    def _(dve):
        for h in range(HALVES):
            dve.wait_ge(spans[1][h], WARM)
        nc.vector.tensor_copy(start[:, :], warm[:, (WARM - 1) % 2, :]).then_inc(started, 1)
        without_first(dve, start, started, 1).then_inc(started, 1)
        for h in range(HALVES):
            dve.wait_ge(spans[1][h], WARM + SPAN)
        span_ends = states[:, bass.DynSlice(SPAN - 1, COLS - 1, step=SPAN)]
        nc.vector.tensor_copy(ends[:, 1:COLS], span_ends).then_inc(ends_out, 1)
        without_first(dve, ends, ends_out, 1).then_inc(ends_out, 1)
        dve.wait_ge(ends_out, 2)
        nc.vector.tensor_tensor(apart[:, :], ends[:, :], start[:, :], ALU.subtract).then_inc(compared, 1)
        dve.wait_ge(compared, 1)
        nc.vector.tensor_tensor(apart[:, :], apart[:, :], apart[:, :], ALU.mult).then_inc(compared, 1)
        dve.wait_ge(compared, 2)
        nc.vector.tensor_reduce(apart_max[:, :], apart[:, :], AX, ALU.max).then_inc(compared, 1)
        dve.wait_ge(compared, 3)
        nc.vector.tensor_scalar(differs[:, :], apart_max[:, :], SLACK * SLACK, None, ALU.is_gt).then_inc(compared, 1)
        dve.wait_ge(count_done, 1)
        nc.vector.tensor_copy(count[:, :], count_ps[0:1, 0:1]).then_inc(count_out, 1)
        dve.wait_ge(count_out, 1)
        wrong = dve.value_load(count[0:1, 0:1])
        with dve.If(wrong):
            with dve.Fori(0, SPANS - 1) as r:
                for h in range(HALVES):
                    dve.wait_ge(again[1][h], r * SPAN)
                nc.vector.tensor_copy(start[:, 1:COLS], span_ends).then_inc(reloaded, 1)
                without_first(dve, start, reloaded, r + 1).then_inc(restarted, 1)
            for h in range(HALVES):
                dve.wait_ge(again[1][h], (SPANS - 1) * SPAN)
        for k in range(PIECES):
            piece = slice(k * PIECE, (k + 1) * PIECE)
            nc.vector.tensor_tensor(resid[:, piece], resid[:, piece], states[:, piece], ALU.add).then_inc(added, 1)


def program(nc, io):
    with ExitStack() as ctx:
        sb = lambda n, s: ctx.enter_context(nc.sbuf_tensor(n, s, FP32))
        resid = sb("resid", [C, TOKENS])
        ident = sb("ident", [C, C])
        mean_w = sb("mean_w", [C, C])
        eps = sb("eps", [C, 1])
        with ExitStack() as own:
            loaded = own.enter_context(nc.semaphore("loaded"))
            constants = own.enter_context(nc.semaphore("constants"))
            block = own.enter_context(nc.Block())

            @block.sync
            def _(sp):
                sp.dma_start(ident[:, :], io["ident"]).then_inc(loaded, 16)
                sp.wait_ge(loaded, 16)

            @block.gpsimd
            def _(pool):
                nc.gpsimd.memset(mean_w[:, :], 1.0 / C).then_inc(constants, 1)
                nc.gpsimd.memset(eps[:, :], 1e-5).then_inc(constants, 1)

        with ExitStack() as own:
            windowed_attention(nc, own, resid, io, ident, mean_w, eps)
        with ExitStack() as own:
            channel_attention(nc, own, resid, io)
        for stage in (sparse_attention, expert_choice, self_attention, recurrence):
            with ExitStack() as own:
                stage(nc, own, resid, io, ident, mean_w, eps)


def kernel(**inputs):
    import numpy as _np
    import concourse.bacc as _bacc
    from concourse.bass_utils import run_bass_kernel_spmd as _run

    a = {k: _np.asarray(v) for k, v in inputs.items()}
    lay = _np.ascontiguousarray
    experts, hidden = a["L2_ffn_weight1"].shape[0], a["L2_ffn_weight1"].shape[2]
    arrays = {
        "x": lay(a["x"].reshape(TOKENS, C).T),
        "qkv_w": lay(a["L0_conv_qkv_w"].T),
        "qkv_b": lay(a["L0_conv_qkv_b"].reshape(3, C).T),
        "qkv_b_row": lay(a["L0_conv_qkv_b"].reshape(1, 3 * C)),
        "rpb": lay(a["L0_conv_rpb"]),
        "proj_w": lay(a["L0_conv_proj_w"].T),
        "proj_b": lay(a["L0_conv_proj_b"].reshape(C, 1)),
        "kernel_f": lay(a["L1_conv_kernel_f"].reshape(C, 16)),
        "kernel_g": lay(a["L1_conv_kernel_g"].reshape(C, 16)),
        "kernel_h": lay(a["L1_conv_kernel_h"].reshape(C, C)),
        "gamma": lay(_np.broadcast_to(a["L1_conv_gamma"].reshape(1, 1), (C, 1))),
        "Wq": lay(a["L2_attn_Wq"]),
        "Wk": lay(a["L2_attn_Wk"]),
        "Wv": lay(a["L2_attn_Wv"]),
        "Wo": lay(a["L2_attn_Wo"]),
        "Ws": lay(a["L2_attn_Ws"]),
        "bq": lay(a["L2_attn_bq"].reshape(C, 1)),
        "bk": lay(a["L2_attn_bk"].reshape(C, 1)),
        "bv": lay(a["L2_attn_bv"].reshape(1, C)),
        "bo": lay(a["L2_attn_bo"].reshape(C, 1)),
        "bs": lay(a["L2_attn_bs"].reshape(1, 1)),
        "gate_w": lay(a["L2_ffn_gate_w"].T),
        "gate_b": lay(a["L2_ffn_gate_b"].reshape(experts, 1)),
        "weight1": lay(a["L2_ffn_weight1"]),
        "weight2": lay(a["L2_ffn_weight2"]),
        "bias2": lay(a["L2_ffn_weight2"][:, hidden, :].T),
        "rnn_w": lay(a["L3_ffn_W"].T),
        "rnn_v": lay(a["L3_ffn_V"].T),
        "rnn_gamma": lay(a["L3_ffn_gamma"].reshape(C, 1)),
        "rnn_beta": lay(a["L3_ffn_beta"].reshape(C, 1)),
        "ident": _np.eye(C, dtype=_np.float32),
    }
    arrays.update(shape_constants())
    nc = _bacc.Bacc("TRN2", target_bir_lowering=False, num_devices=1)
    io = {k: nc.dram_tensor(f"in_{k}", v.shape, mybir.dt.from_np(v.dtype), kind="ExternalInput").ap()
          for k, v in arrays.items()}
    out = nc.dram_tensor("out", (C, TOKENS), FP32, kind="ExternalOutput").ap()
    io["out"] = out
    program(nc, io)
    r = _run(nc, [{f"in_{k}": v for k, v in arrays.items()}], core_ids=[0])
    return lay(_np.asarray(r.results[0]["out"]).T).reshape(B, H, W, C)
```
